# Optimizing a Trainium2 kernel written in Bass

```python
import numpy as np
import jax
import jax.numpy as jnp

def _softmax(x, axis=-1):
    return jax.nn.softmax(x, axis=axis)

def _gelu(x):
    return jax.nn.gelu(x, approximate=True)

def _silu(x):
    return jax.nn.silu(x)

def _sigmoid(x):
    return jax.nn.sigmoid(x)

def _layernorm(x, axis=-1, eps=1e-05):
    m = jnp.mean(x, axis=axis, keepdims=True)
    v = jnp.var(x, axis=axis, keepdims=True)
    return (x - m) / jnp.sqrt(v + eps)

def _scatter_add(tgt, idx, src, axis=0):
    return tgt.at[idx].add(src)

def _segment_sum(src, seg, n):
    return jax.ops.segment_sum(src, seg, n)
kernel_name = 'mk_adaln_d1_jaxref_r8_7783b9'

def setup_inputs(seed: int=0):
    np.random.seed(seed)
    _w = jnp.asarray

    def _L0_attn_setup():
        import jax, jax.numpy as jnp
        import numpy as np
        B, N, C = (2, 256, 128)
        H = 16
        HD = C // H
        KA_IN = 2 * HD
        KA_OUT = HD
        T = 4
        KA_HID = KA_IN // 2
        KA_O = KA_OUT // T
        TEMPERATURE = 0.72
        SCALE = HD ** (-0.5)
        LN_EPS = 1e-05
        key = jax.random.key(seed)
        ks = jax.random.split(key, 20)

        def w(k, shape, fan_in):
            return jax.random.normal(k, shape, jnp.float32) / np.sqrt(fan_in)
        return {'x': jax.random.normal(ks[0], (B, N, C), jnp.float32), 'Wqkv': w(ks[1], (C, 3 * C), C), 'Wproj': w(ks[2], (C, C), C), 'bproj': jnp.zeros((C,), jnp.float32), 'alpha': jnp.ones((H,), jnp.float32), 'beta': jnp.ones((H,), jnp.float32), 'gamma': jnp.ones((H,), jnp.float32), 'A': w(ks[3], (T, KA_IN, KA_IN), KA_IN), 'Wphi1': w(ks[4], (T, KA_IN, KA_HID), KA_IN), 'bphi1': jnp.zeros((T, KA_HID), jnp.float32), 'Wphi2': w(ks[5], (T, KA_HID, KA_O), KA_HID), 'bphi2': jnp.zeros((T, KA_O), jnp.float32), 'Wpsi1': w(ks[6], (T, KA_IN, KA_IN), KA_IN), 'bpsi1': jnp.zeros((T, KA_IN), jnp.float32), 'ln_g': jnp.ones((T, KA_IN), jnp.float32), 'ln_b': jnp.zeros((T, KA_IN), jnp.float32), 'Wpsi2': w(ks[7], (T, KA_IN, KA_O), KA_IN), 'bpsi2': jnp.zeros((T, KA_O), jnp.float32), 'mixing': jnp.full((T,), 1.0 / T, jnp.float32), 'temp_scale': jnp.asarray(TEMPERATURE, jnp.float32)}
    _L0_attn_in = _L0_attn_setup()

    def _L0_ffn_setup():
        import jax, jax.numpy as jnp
        import numpy as np
        D_IN, D_H, D_OUT = (128, 128, 128)
        D_MOE = 512
        N_EXPERTS = 8
        TOP_K = 2
        key = jax.random.key(seed)
        ks = jax.random.split(key, 10)
        s = lambda d: 1.0 / np.sqrt(d)
        x = jax.random.normal(ks[0], (2, 256, D_IN), dtype=jnp.float32)
        W_in = jax.random.normal(ks[1], (D_IN, D_H), dtype=jnp.float32) * s(D_IN)
        b_in = jnp.zeros((D_H,), jnp.float32)
        W_gate = jax.random.normal(ks[2], (D_H, N_EXPERTS), dtype=jnp.float32) * s(D_H)
        b_gate = jnp.zeros((N_EXPERTS,), jnp.float32)
        W1 = jax.random.normal(ks[3], (N_EXPERTS, D_H, D_MOE), dtype=jnp.float32) * s(D_H)
        b1 = jnp.zeros((N_EXPERTS, D_MOE), jnp.float32)
        W2 = jax.random.normal(ks[4], (N_EXPERTS, D_MOE, D_H), dtype=jnp.float32) * s(D_MOE)
        b2 = jnp.zeros((N_EXPERTS, D_H), jnp.float32)
        W_out = jax.random.normal(ks[5], (D_H, D_OUT), dtype=jnp.float32) * s(D_H)
        b_out = jnp.zeros((D_OUT,), jnp.float32)
        return {'x': x, 'W_in': W_in, 'b_in': b_in, 'W_gate': W_gate, 'b_gate': b_gate, 'W1': W1, 'b1': b1, 'W2': W2, 'b2': b2, 'W_out': W_out, 'b_out': b_out}
    _L0_ffn_in = _L0_ffn_setup()
    _L0_c = _w((lambda *s: np.random.randn(*s).astype(np.float32) * 0.05)(4, 128))
    _L0_wmod = _w((lambda *s: np.random.randn(*s).astype(np.float32) * 0.05)(128, 6 * 128) * 128 ** (-0.5))
    _d = {'L0_attn_x': _L0_attn_in['x'], 'L0_attn_Wqkv': _L0_attn_in['Wqkv'], 'L0_attn_Wproj': _L0_attn_in['Wproj'], 'L0_attn_bproj': _L0_attn_in['bproj'], 'L0_attn_alpha': _L0_attn_in['alpha'], 'L0_attn_beta': _L0_attn_in['beta'], 'L0_attn_gamma': _L0_attn_in['gamma'], 'L0_attn_A': _L0_attn_in['A'], 'L0_attn_Wphi1': _L0_attn_in['Wphi1'], 'L0_attn_bphi1': _L0_attn_in['bphi1'], 'L0_attn_Wphi2': _L0_attn_in['Wphi2'], 'L0_attn_bphi2': _L0_attn_in['bphi2'], 'L0_attn_Wpsi1': _L0_attn_in['Wpsi1'], 'L0_attn_bpsi1': _L0_attn_in['bpsi1'], 'L0_attn_ln_g': _L0_attn_in['ln_g'], 'L0_attn_ln_b': _L0_attn_in['ln_b'], 'L0_attn_Wpsi2': _L0_attn_in['Wpsi2'], 'L0_attn_bpsi2': _L0_attn_in['bpsi2'], 'L0_attn_mixing': _L0_attn_in['mixing'], 'L0_attn_temp_scale': _L0_attn_in['temp_scale'], 'L0_ffn_W_in': _L0_ffn_in['W_in'], 'L0_ffn_b_in': _L0_ffn_in['b_in'], 'L0_ffn_W_gate': _L0_ffn_in['W_gate'], 'L0_ffn_b_gate': _L0_ffn_in['b_gate'], 'L0_ffn_W1': _L0_ffn_in['W1'], 'L0_ffn_b1': _L0_ffn_in['b1'], 'L0_ffn_W2': _L0_ffn_in['W2'], 'L0_ffn_b2': _L0_ffn_in['b2'], 'L0_ffn_W_out': _L0_ffn_in['W_out'], 'L0_ffn_b_out': _L0_ffn_in['b_out'], 'L0_c': _L0_c, 'L0_wmod': _L0_wmod}
    _x0 = _d['L0_attn_x']
    _d['L0_attn_x'] = jax.random.normal(jax.random.fold_in(jax.random.key(seed), 1), (4, 1024, 128), dtype=_x0.dtype)
    del _x0
    return _d

def reference(L0_attn_x, L0_attn_Wqkv, L0_attn_Wproj, L0_attn_bproj, L0_attn_alpha, L0_attn_beta, L0_attn_gamma, L0_attn_A, L0_attn_Wphi1, L0_attn_bphi1, L0_attn_Wphi2, L0_attn_bphi2, L0_attn_Wpsi1, L0_attn_bpsi1, L0_attn_ln_g, L0_attn_ln_b, L0_attn_Wpsi2, L0_attn_bpsi2, L0_attn_mixing, L0_attn_temp_scale, L0_ffn_W_in, L0_ffn_b_in, L0_ffn_W_gate, L0_ffn_b_gate, L0_ffn_W1, L0_ffn_b1, L0_ffn_W2, L0_ffn_b2, L0_ffn_W_out, L0_ffn_b_out, L0_c, L0_wmod):

    def _L0_attn_ref(x, Wqkv, Wproj, bproj, alpha, beta, gamma, A, Wphi1, bphi1, Wphi2, bphi2, Wpsi1, bpsi1, ln_g, ln_b, Wpsi2, bpsi2, mixing, temp_scale):
        import jax, jax.numpy as jnp
        import numpy as np
        B, N, C = (2, 256, 128)
        H = 16
        HD = C // H
        KA_IN = 2 * HD
        KA_OUT = HD
        T = 4
        KA_HID = KA_IN // 2
        KA_O = KA_OUT // T
        TEMPERATURE = 0.72
        SCALE = HD ** (-0.5)
        LN_EPS = 1e-05
        Bx, Nx, Cx = x.shape
        qkv = (x @ Wqkv).reshape(Bx, Nx, 3, H, HD).transpose(2, 0, 3, 1, 4)
        q, k, v = (qkv[0], qkv[1], qkv[2])
        attn = jnp.einsum('bhnd,bhmd->bhnm', q, k) * (SCALE / TEMPERATURE)
        attn = attn * alpha[None, :, None, None] + beta[None, :, None, None]
        attn = jax.nn.softmax(attn, axis=-1) * gamma[None, :, None, None]
        qk = jnp.concatenate([q.mean(-2), k.mean(-2)], -1).reshape(Bx * H, KA_IN)
        Ax = jnp.einsum('md,tde->tme', qk, A)
        phi = jax.nn.silu(jnp.einsum('md,tdh->tmh', qk, Wphi1) + bphi1[:, None, :])
        phi = jnp.einsum('tmh,tho->tmo', phi, Wphi2) + bphi2[:, None, :]
        psi = jnp.einsum('tme,teg->tmg', Ax, Wpsi1) + bpsi1[:, None, :]
        mu = psi.mean(-1, keepdims=True)
        var = ((psi - mu) ** 2).mean(-1, keepdims=True)
        psi = (psi - mu) / jnp.sqrt(var + LN_EPS) * ln_g[:, None, :] + ln_b[:, None, :]
        psi = jax.nn.gelu(psi, approximate=False)
        psi = jnp.einsum('tmg,tgo->tmo', psi, Wpsi2) + bpsi2[:, None, :]
        terms = phi * psi * temp_scale * mixing[:, None, None]
        ka = jnp.transpose(terms, (1, 0, 2)).reshape(Bx, H, 1, HD)
        enhanced_v = v * (1.0 + ka)
        out = jnp.einsum('bhnm,bhmd->bhnd', attn, enhanced_v)
        out = out.transpose(0, 2, 1, 3).reshape(Bx, Nx, Cx)
        return out @ Wproj + bproj

    def _L0_ffn_ref(x, W_in, b_in, W_gate, b_gate, W1, b1, W2, b2, W_out, b_out):
        import jax, jax.numpy as jnp
        import numpy as np
        D_IN, D_H, D_OUT = (128, 128, 128)
        D_MOE = 512
        N_EXPERTS = 8
        TOP_K = 2
        B, S, _ = x.shape
        h = x @ W_in + b_in
        t = h.reshape(B * S, -1)
        logits = t @ W_gate + b_gate
        probs = jax.nn.softmax(logits, axis=-1)
        topv, topi = jax.lax.top_k(probs, TOP_K)
        topv = topv / jnp.sum(topv, axis=-1, keepdims=True)
        route = jnp.zeros_like(probs).at[jnp.arange(t.shape[0])[:, None], topi].set(topv)
        mid = jax.nn.relu(jnp.einsum('nd,edh->neh', t, W1) + b1)
        eout = jnp.einsum('neh,ehd->ned', mid, W2) + b2
        moe_out = jnp.einsum('ne,ned->nd', route, eout)
        out = moe_out.reshape(B, S, -1) @ W_out + b_out
        return out
    x = L0_attn_x
    mod = (_silu(L0_c) @ L0_wmod).reshape(L0_c.shape[0], 6, 1, -1)
    sa, ca, ga, sb, cb, gb = (mod[:, 0], mod[:, 1], mod[:, 2], mod[:, 3], mod[:, 4], mod[:, 5])
    ga = (2 * (ga >= 0) - 1) * jnp.maximum(jnp.abs(ga), 0.25)
    gb = (2 * (gb >= 0) - 1) * jnp.maximum(jnp.abs(gb), 0.25)
    h = _layernorm(x, axis=-1) * (1 + ca) + sa
    x = x + ga * _L0_attn_ref(h, L0_attn_Wqkv, L0_attn_Wproj, L0_attn_bproj, L0_attn_alpha, L0_attn_beta, L0_attn_gamma, L0_attn_A, L0_attn_Wphi1, L0_attn_bphi1, L0_attn_Wphi2, L0_attn_bphi2, L0_attn_Wpsi1, L0_attn_bpsi1, L0_attn_ln_g, L0_attn_ln_b, L0_attn_Wpsi2, L0_attn_bpsi2, L0_attn_mixing, L0_attn_temp_scale)
    h = _layernorm(x, axis=-1) * (1 + cb) + sb
    x = x + gb * _L0_ffn_ref(h, L0_ffn_W_in, L0_ffn_b_in, L0_ffn_W_gate, L0_ffn_b_gate, L0_ffn_W1, L0_ffn_b1, L0_ffn_W2, L0_ffn_b2, L0_ffn_W_out, L0_ffn_b_out)
    return x

_drawn_inputs = setup_inputs


def setup_inputs(seed=0):
    import zlib

    import numpy as np

    out = dict(_drawn_inputs(seed))
    spreads = {'L0_attn_bproj': (0.0, 0.492),
     'L0_attn_alpha': (1.0, 0.6),
     'L0_attn_beta': (1.0, 0.6),
     'L0_attn_gamma': (1.0, 0.6),
     'L0_attn_bphi1': (0.0, 0.8),
     'L0_attn_bphi2': (0.0, 0.8),
     'L0_attn_bpsi1': (0.0, 0.8),
     'L0_attn_ln_g': (1.0, 0.6),
     'L0_attn_ln_b': (0.0, 0.8),
     'L0_attn_bpsi2': (0.0, 0.8),
     'L0_attn_mixing': (0.25, 0.6),
     'L0_ffn_b_in': (0.0, 0.41),
     'L0_ffn_b_gate': (0.0, 0.309),
     'L0_ffn_b1': (0.0, 0.611),
     'L0_ffn_b2': (0.0, 0.441),
     'L0_ffn_b_out': (0.0, 0.312)}
    factors = {'L0_attn_A': 8.0,
     'L0_attn_Wphi1': 8.0,
     'L0_attn_Wphi2': 8.0,
     'L0_attn_Wpsi1': 8.0,
     'L0_attn_Wpsi2': 8.0}
    for name, (base, spread) in spreads.items():
        noise = np.random.default_rng([zlib.crc32(name.encode()), seed]).standard_normal(out[name].shape)
        drawn = base * np.exp(spread * noise) if base else spread * noise
        out[name] = jnp.asarray(drawn.astype(out[name].dtype))
    for name, factor in factors.items():
        out[name] = (out[name] * factor).astype(out[name].dtype)
    return out
```

```python
from contextlib import ExitStack

import concourse.bass as bass
from concourse import mybir

F32 = mybir.dt.float32
F32R = mybir.dt.float32r
ACT = mybir.ActivationFunctionType
ALU = mybir.AluOpType
X = mybir.AxisListType.X

P = 128
B, N, C = 4, 1024, 128
H, HD = 16, 8
T = 4
KI, KH, KO = 16, 8, 2
E, DM = 8, 512
NT = N // P
GH = 4
NG = H // GH
NI = B * NG
PARTS = 3 * HD
ROWS = PARTS + 2
HALF = 512
CH = DM // P
STEPS = 64
LAG = 16
AHEAD = STEPS - LAG
UNITS = 16
EPS = 1e-5
ATTN_SCALE = HD ** -0.5 / 0.72

CREDIT = {"exps": 2, "w2_done": 2, "pv_done": 2, "o_moved": 1, "relus": 1, "moe_added": 1, "x_turned": 1, "lo_ready": 1, "v_kept": 1, "qk_stored": 1, "wout_done": 1, "stored": 1, "o_stored0": 1, "o_stored1": 1}


class Chain:

    def __init__(self, eng, sem):
        self.eng, self.sem, self.n, self.base = eng, sem, 0, None

    def did(self, ins):
        ins.then_inc(self.sem, 1)
        self.n += 1

    def value(self):
        return self.n if self.base is None else self.base + self.n

    def wait(self):
        self.eng.wait_ge(self.sem, self.value())

    def link(self, ins):
        self.did(ins)
        self.wait()

    def enter(self, index, per):
        self.outer = (self.base, self.n)
        start = self.n if self.base is None else self.base + self.n
        self.base, self.n, self.per = index * per + start, 0, per

    def leave(self, times):
        assert self.n == self.per, (self.n, self.per)
        base, n = self.outer
        self.base, self.n = base, n + times * self.per


def build(nc, a, out):
    with ExitStack() as ctx:
        def sb(name, shape, dt=F32):
            return ctx.enter_context(nc.sbuf_tensor(name, shape, dt))

        sems = {}

        def sig(name):
            if name not in sems:
                sems[name] = ctx.enter_context(nc.semaphore(name))
            return sems[name]

        ps = ctx.enter_context(nc.psum_tensor("ps", [P, 8, HALF], F32))

        q_dram = nc.dram_tensor("q_dram", [B * H, ROWS, N], F32)
        k_dram = nc.dram_tensor("k_dram", [B * H, ROWS, N], F32)
        o_dram = nc.dram_tensor("o_dram", [B * H, 2 * HD, N], F32)
        mean_dram = nc.dram_tensor("mean_dram", [2, B, C], F32)
        fac_dram = nc.dram_tensor("fac_dram", [B * H, HD], F32)

        wqkv = sb("wqkv", [P, 3 * C]); wproj = sb("wproj", [P, C])
        win = sb("win", [P, C]); wout = sb("wout", [P, C]); wgate = sb("wgate", [P, E])
        wmod = sb("wmod", [P, 6 * C]); cmod = sb("cmod", [B, C])
        b1rows = sb("b1rows", [E * CH, P]); b2 = sb("b2", [E, C])
        bproj_bc = sb("bproj_bc", [P, C]); bout_bc = sb("bout_bc", [P, C])
        bin_col = sb("bin_col", [P, 1]); bgate_bc = sb("bgate_bc", [P, E])
        beta_bc = sb("beta_bc", [P, B * H]); alpha_col = sb("alpha_col", [P, 1])
        ka_a = sb("ka_a", [KI, T, KI]); ka_phi1 = sb("ka_phi1", [KI, T, KH])
        ka_bphi1 = sb("ka_bphi1", [T * KH, 1]); ka_phi2 = sb("ka_phi2", [T * KH, HD])
        ka_psi1 = sb("ka_psi1", [T * KI, T * KI]); ka_psi2 = sb("ka_psi2", [T * KI, HD])
        MB = B * H
        bphi2_bc = sb("bphi2_bc", [MB, HD]); bpsi1_bc = sb("bpsi1_bc", [MB, T * KI])
        lng_bc = sb("lng_bc", [MB, T * KI]); lnb_bc = sb("lnb_bc", [MB, T * KI])
        bpsi2_bc = sb("bpsi2_bc", [MB, HD]); mix_bc = sb("mix_bc", [MB, T])
        temp_bc = sb("temp_bc", [MB, 1]); gamma_col = sb("gamma_col", [MB, 1])

        ident = sb("ident", [P, P]); rev = sb("rev", [P, E])
        siluT = sb("siluT", [P, B]); silu_bc = sb("silu_bc", [P, B, P])
        mod_col = sb("mod_col", [P, 4, B])
        gate_bc = sb("gate_bc", [P, 2, B * C])
        wproj_g = sb("wproj_g", [P, B, C]); wout_g = sb("wout_g", [P, B, C])
        bproj_g = sb("bproj_g", [P, B, C]); bout_g = sb("bout_g", [P, B, C])
        b1T = sb("b1T", [P, E * CH])

        eps_col = sb("eps_col", [P, 1]); qk_scale = sb("qk_scale", [P, 2]); credit = sb("credit", [P, 16])

        x_all = sb("x_all", [P, B * NT, C]); v_all = sb("v_all", [P, NI, NT, GH * HD])
        stats = sb("stats", [P, B * NT, 6]); mv = sb("mv", [P, B * NT, 2])
        std = sb("std", [P, B * NT]); rstd = sb("rstd", [P, B * NT])
        xn = sb("xn", [P, NT, C]); hT = sb("hT", [P, N])
        hsum = sb("hsum", [P, 2 * B]); hmean = sb("hmean", [P, B])
        qk_hi = sb("qk_hi", [P, 2, N], F32R); qk_lo = sb("qk_lo", [P, 2, N], F32R)

        qkm = sb("qkm", [B, 2, C]); qk = sb("qk", [MB, KI]); qkT = sb("qkT", [KI, MB])
        axT = sb("axT", [T * KI, MB]); phiT = sb("phiT", [T * KH, MB]); phi = sb("phi", [MB, HD])
        psi = sb("psi", [MB, T, KI]); psq = sb("psq", [MB, T, KI]); psm = sb("psm", [MB, T])
        psv = sb("psv", [MB, T]); pst = sb("pst", [MB, T]); psiT = sb("psiT", [T * KI, MB])
        psi_o = sb("psi_o", [MB, HD]); fac = sb("fac", [MB, HD]); vfac = sb("vfac", [P, B])

        Q = [sb(f"Q{i}", [P, N], F32R) for i in range(2)]
        K = [sb(f"K{i}", [P, GH, N], F32R) for i in range(2)]
        V = [sb(f"V{i}", [P, NT, GH, 32]) for i in range(2)]
        beta_g = [sb(f"beta_g{i}", [P, GH]) for i in range(2)]
        probs = sb("probs", [P, 8, HALF])
        gt0, gt1 = probs[:, 0:2, :], probs[:, 2:4, :]
        mxp = sb("mxp", [P, NT, 2, GH]); mx = sb("mx", [P, 16]); mxb = sb("mxb", [P, 16])
        mrow = sb("mrow", [P, 16]); mparts = sb("mparts", [P, 2, 16], F32R)
        mrows = sb("mrows", [32, P])
        oT = sb("oT", [P, 2, HALF])
        w1 = [sb(f"w1_{i}", [P, DM]) for i in range(2)]
        w2 = [sb(f"w2_{i}", [P, CH, C]) for i in range(2)]
        b1s = [sb(f"b1s{i}", [P, 2, CH]) for i in range(2)]
        rts = [sb(f"rts{i}", [P, 2, NT]) for i in range(2)]
        mid = sb("mid", [P, 2, HALF])

        oc = sb("oc", [P, N]); den = sb("den", [P, N])
        xg = sb("xg", [P, NT, C]); x1 = sb("x1", [P, NT, C])
        st2 = sb("st2", [P, NT, 6]); mv2 = sb("mv2", [P, NT, 2]); sd2 = sb("sd2", [P, NT])
        tT = sb("tT", [P, N])
        lg = sb("lg", [P, NT, E]); pr = sb("pr", [P, NT, E]); g0 = sb("g0", [P, NT, E])
        g1 = sb("g1", [P, NT, E]); g2 = sb("g2", [P, NT, E]); gm = sb("gm", [P, NT])
        route = sb("route", [P, NT, E]); routeT = sb("routeT", [E, N])
        acc = sb("acc", [P, NT, C]); accT = sb("accT", [P, N]); y = sb("y", [P, NT, C])

        def bank(i):
            return ps[:, i, :]

        def tiles(i):
            return ps[:, i, :].rearrange("p (t c) -> p t c", c=P)

        def over_experts(t):
            return t[:, :].unsqueeze(2).broadcast_to([P, NT, E])

        def over_tiles(t):
            return t[:, :].unsqueeze(1).broadcast_to([P, NT, E])

        row = lambda v, n: v.partition_broadcast(n)
        loads = [(cmod[:, :], a["L0_c"]), (wmod[:, :], a["L0_wmod"])]
        loads += [(wqkv[:, :], a["L0_attn_Wqkv"]), (wproj[:, :], a["L0_attn_Wproj"]),
                  (win[:, :], a["L0_ffn_W_in"]), (wout[:, :], a["L0_ffn_W_out"]),
                  (wgate[:, :], a["L0_ffn_W_gate"]),
                  (b1rows[:, :], a["L0_ffn_b1"].rearrange("e (c p) -> (e c) p", p=P)),
                  (b2[:, :], a["L0_ffn_b2"]),
                  (bproj_bc[:, :], row(a["L0_attn_bproj"], P)),
                  (bout_bc[:, :], row(a["L0_ffn_b_out"], P)),
                  (bin_col[:, :], a["L0_ffn_b_in"].rearrange("(p o) -> p o", o=1)),
                  (bgate_bc[:, :], row(a["L0_ffn_b_gate"], P)),
                  (ka_a[:, :, :], a["L0_attn_A"].rearrange("t d e -> d t e")),
                  (ka_phi1[:, :, :], a["L0_attn_Wphi1"].rearrange("t d e -> d t e")),
                  (ka_bphi1[:, :], a["L0_attn_bphi1"].rearrange("t (h o) -> (t h) o", o=1)),
                  (bphi2_bc[:, :], row(a["L0_attn_bphi2"].rearrange("t o -> (t o)"), MB)),
                  (bpsi1_bc[:, :], row(a["L0_attn_bpsi1"].rearrange("t o -> (t o)"), MB)),
                  (lng_bc[:, :], row(a["L0_attn_ln_g"].rearrange("t o -> (t o)"), MB)),
                  (lnb_bc[:, :], row(a["L0_attn_ln_b"].rearrange("t o -> (t o)"), MB)),
                  (bpsi2_bc[:, :], row(a["L0_attn_bpsi2"].rearrange("t o -> (t o)"), MB)),
                  (mix_bc[:, :], row(a["L0_attn_mixing"], MB)),
                  (temp_bc[:, :], row(a["L0_attn_temp_scale"].rearrange("(o) -> o", o=1), MB))]
        loads += [(alpha_col[h * HD:(h + 1) * HD, :], row(a["L0_attn_alpha"][h:h + 1], HD)) for h in range(H)]
        loads += [(beta_bc[:, b * H:(b + 1) * H], row(a["L0_attn_beta"], P)) for b in range(B)]
        loads += [(gamma_col[b * H:(b + 1) * H, :], a["L0_attn_gamma"].rearrange("(h o) -> h o", o=1))
                  for b in range(B)]
        blocks = []
        for t in range(T):
            blocks += [(ka_phi2[t * KH:(t + 1) * KH, t * KO:(t + 1) * KO], a["L0_attn_Wphi2"][t]),
                       (ka_psi1[t * KI:(t + 1) * KI, t * KI:(t + 1) * KI], a["L0_attn_Wpsi1"][t]),
                       (ka_psi2[t * KI:(t + 1) * KI, t * KO:(t + 1) * KO], a["L0_attn_Wpsi2"][t])]

        block = ctx.enter_context(nc.Block())

        @block.sync
        def _(sp):
            def load_group(it, p):
                for j in range(GH):
                    head = it * GH + j
                    sp.dma_start(Q[p][32 * j:32 * j + ROWS, :].bitcast(F32), q_dram[head]).then_inc(sig("qk_loaded"), 16)
                    sp.dma_start(K[p][32 * j:32 * j + ROWS, j, :].bitcast(F32), k_dram[head]).then_inc(sig("qk_loaded"), 16)

            def load_expert(e, u):
                sp.dma_start(w1[u][:, :], a["L0_ffn_W1"][e]).then_inc(sig(f"w_loaded{u}"), 16)
                sp.dma_start(w2[u][:, :, :], a["L0_ffn_W2"][e].rearrange("(c p) d -> p c d", p=P)).then_inc(sig(f"w_loaded{u}"), 16)

            def max_rows(count, p, half):
                sp.wait_ge(sig("max_moved"), count + 1)
                for part in range(2):
                    sp.dma_start(Q[p][PARTS + part:P:32, HALF * half:HALF * (half + 1)].rearrange(
                        "j (t n) -> j t n", n=P).bitcast(F32), mrows[16 * part:16 * part + 16, :]).then_inc(sig("max_rows"), 16)

            def store_heads(it, half):
                sp.wait_ge(sig("o_moved"), it * 2 + half + 2)
                for j in range(GH):
                    sp.dma_start(o_dram[it * GH + j, :, HALF * half:HALF * (half + 1)],
                                 oT[32 * j:32 * j + 2 * HD, half, :]).then_inc(sig(f"o_stored{half}"), 16)

            def main(it, p, ffn, g, fi):
                sp.wait_ge(sig("exps"), it * STEPS + 2)
                load_group((it + 1) % NI, 1 - p)
                if ffn:
                    sp.wait_ge(sig("w2_done"), fi * UNITS + 2)
                    load_expert(g * 2 + 1, 1)
                max_rows(it * 2 + 1, p, 1)
                store_heads(it, 0)
                max_rows(it * 2 + 2, 1 - p, 0)
                if ffn:
                    sp.wait_ge(sig("w2_done"), fi * UNITS + UNITS // 2 + 2)
                    load_expert((g * 2 + 2) % E, 0)
                store_heads(it, 1)

            def post(b):
                sp.wait_ge(sig("proj_done"), b * 2)
                sp.wait_ge(sig("o_stored0"), (b + 1) * NG * GH * 16 + 1)
                sp.wait_ge(sig("o_stored1"), (b + 1) * NG * GH * 16 + 1)
                o_b = o_dram[:, :, :].rearrange("(b h) r n -> b h r n", h=H)[b]
                sp.dma_start(oc[:, :], o_b[:, 0:HD, :]).then_inc(sig("o_loaded"), 16)
                sp.dma_start(den[:, :], o_b[:, HD:2 * HD, :]).then_inc(sig("o_loaded"), 16)

            def finish(b, n):
                sp.wait_ge(sig("y_ready"), 2 * n + 2)
                sp.dma_start(out[b].rearrange("(t p) c -> p t c", p=P), y[:, :, :]).then_inc(sig("stored"), 16)

            for dst, src in loads[:2]:
                sp.dma_start(dst, src).then_inc(sig("mod_loaded"), 16)
            for b in range(B):
                sp.dma_start(x_all[:, b * NT:(b + 1) * NT, :], a["L0_attn_x"][b].rearrange("(t p) c -> p t c", p=P)).then_inc(sig(f"x_loaded{b}"), 16)
            for dst, src in loads[2:]:
                sp.dma_start(dst, src).then_inc(sig("loaded"), 16)
            sp.wait_ge(sig("row_values"), 2)
            for dram, src in ((q_dram, acc), (k_dram, y)):
                for part in range(2):
                    sp.dma_start(dram[:, PARTS + part, :], src[0:B * H, :, :].rearrange("p t c -> p (t c)")).then_inc(sig("rows_stored"), 16)
            sp.wait_ge(sig("blocks_zero"), 3)
            for dst, src in blocks:
                sp.dma_start(dst, src).then_inc(sig("blocks_loaded"), 16)
            load_expert(0, 0)

            with sp.Fori(0, B) as b:
                for r in range(2):
                    dram = (q_dram, k_dram)[r][:, :, :].rearrange("(b h) r n -> b h r n", h=H)[b]
                    sp.wait_ge(sig("lo_ready"), b * 4 + 3 + r + 1)
                    for part, src in enumerate(((qk_hi, qk_hi, qk_lo), (qk_hi, qk_lo, qk_hi))[r]):
                        sp.dma_start(dram[:, HD * part:HD * (part + 1), :], src[:, r, :].bitcast(F32)).then_inc(sig("qk_stored"), 16)

            sp.wait_ge(sig("means_ready"), 2)
            sp.dma_start(mean_dram[:, :, :].rearrange("r b c -> b r c"), qkm[:, :, :]).then_inc(sig("means_stored"), 16)
            sp.wait_ge(sig("means_stored"), 16)
            for r in range(2):
                sp.dma_start(qk[:, r * HD:(r + 1) * HD], mean_dram[r].rearrange("b (h d) -> (b h) d", d=HD)).then_inc(sig("qk_means"), 16)
            sp.wait_ge(sig("qk_stored"), B * 6 * 16 + 1)
            sp.wait_ge(sig("qk_zero"), 4)
            sp.wait_ge(sig("rows_stored"), 64)
            load_group(0, 0)
            sp.wait_ge(sig("fac_ready"), 1)
            sp.dma_start(fac_dram[:, :], fac[:, :]).then_inc(sig("fac_stored"), 16)
            sp.wait_ge(sig("fac_stored"), 16)
            for b in range(B):
                sp.dma_start(vfac[:, b:b + 1], fac_dram[b * H:(b + 1) * H, :].rearrange("h (d o) -> (h d) o", o=1)).then_inc(sig("fac_loaded"), 16)
            max_rows(0, 0, 0)

            with sp.Fori(0, NG // 2) as gp:
                for p in range(2):
                    main(gp * 2 + p, p, False, None, None)
            post(0)
            with sp.Fori(1, B) as b:
                with sp.Fori(0, NG // 2) as gp:
                    for p in range(2):
                        g = gp * 2 + p
                        main(b * NG + g, p, True, g, b * NG + g - NG)
                finish(b - 1, b - 1)
                post(b)
            with sp.Fori(0, NG) as g:
                sp.wait_ge(sig("w2_done"), g * UNITS + (NI - NG) * UNITS + 2)
                load_expert(g * 2 + 1, 1)
                sp.wait_ge(sig("w2_done"), g * UNITS + (NI - NG) * UNITS + UNITS // 2 + 2)
                load_expert((g * 2 + 2) % E, 0)
            finish(B - 1, B - 1)
            sp.wait_ge(sig("stored"), B * 16 + 1)
            sp.wait_ge(sig("w_loaded0"), 32 * (NI + 1))
            sp.wait_ge(sig("qk_loaded"), 128 * (NI + 1))
            sp.wait_ge(sig("max_rows"), 32 * (2 * NI + 1))

        @block.tensor
        def _(pe):
            mm = nc.tensor.matmul

            def score_max(a_i, base, p):
                nt, mh, j = a_i // 8, a_i // 4 % 2, a_i % 4
                mm(bank(a_i % 2), Q[p][:, P * nt:P * (nt + 1)], K[p][:, j, HALF * mh:HALF * (mh + 1)],
                   start=True, stop=True).then_inc(sig("max_scores"), 1)

            def move_max(count, n):
                pe.wait_ge(sig("max_parts"), count + 1)
                nc.tensor.transpose(ps[0:32, 7, 0:P], mparts[:, :, :].rearrange("p a b -> p (a b)").bitcast(F32), ident[:, :]).then_inc(sig("max_turned"), 1)

            def expert_up(q, base, fi):
                u, th, c = q // 8, q // 4 % 2, q % 4
                if q % 8 == 0:
                    pe.wait_ge(sig(f"w_loaded{u}"), fi * 32 + 32)
                pe.wait_ge(sig("relus"), fi * UNITS + q + 1)
                mm(bank(5), w1[u][:, P * c:P * (c + 1)], tT[:, HALF * th:HALF * (th + 1)], start=True, stop=True).then_inc(sig("w1_done"), 1)

            def expert_down(q, fi):
                u, th, c = q // 8, q // 4 % 2, q % 4
                pe.wait_ge(sig("relus"), fi * UNITS + q + 2)
                if c == 0:
                    pe.wait_ge(sig("moe_added"), fi * 4 + q // 4 + 1)
                for tt in range(4):
                    m = mm(ps[:, 6, P * tt:P * (tt + 1)], mid[:, q % 2, P * tt:P * (tt + 1)], w2[u][:, c, :],
                           start=(c == 0 and tt == 0), stop=(c == CH - 1), skip_group_check=True)
                m.then_inc(sig("w2_done"), 1)

            def main(it, p, ffn, fi):
                def pv(v):
                    half, mt = v // NT, v % NT
                    pe.wait_ge(sig("exps"), it * STEPS + 4 * (v + 1) + 2)
                    if v == 0:
                        pe.wait_ge(sig("v_staged"), it + 1)
                    if mt == 0:
                        pe.wait_ge(sig("o_moved"), it * 2 + half + 1)
                    for j in range(GH):
                        m = mm(ps[32 * j:32 * j + 32, 4, :], V[p][:, mt, j, :], probs[:, 4 * (mt % 2) + j, :],
                               start=(mt == 0), stop=(mt == NT - 1), tile_position=(0, 32 * j))
                    m.then_inc(sig("pv_done"), 1)

                for s in range(STEPS):
                    if s == LAG:
                        pe.wait_ge(sig("qk_loaded"), it * 128 + 256)
                    pe.wait_ge(sig("maxed"), it * STEPS + AHEAD + s - 1)
                    score_max((s - LAG) % STEPS, None, p if s < LAG else 1 - p)
                    half, mt, j = s // 32, s % 32 // 4, s % 4
                    if s % 32 == 0:
                        pe.wait_ge(sig("max_rows"), it * 64 + 32 * half + 32)
                    pe.wait_ge(sig("exps"), it * STEPS + s + 1)
                    mm(bank(2 + s % 2), K[p][:, j, P * mt:P * (mt + 1)], Q[p][:, HALF * half:HALF * (half + 1)],
                       start=True, stop=True).then_inc(sig("scores"), 1)
                    if ffn and s % 4 == 1:
                        expert_up(s // 4, None, fi)
                    if s % 4 == 3 and s > 3:
                        pv(s // 4 - 1)
                    if ffn and s % 4 == 2 and s > 4:
                        expert_down(s // 4 - 1, fi)
                    if s == 20:
                        move_max(it * 2 + 1, None)
                    if s == 52:
                        move_max(it * 2 + 2, None)
                if ffn:
                    expert_down(UNITS - 1, fi)
                pv(2 * NT - 1)

            def post(b):
                pe.wait_ge(sig("o_normed"), b + 1)
                for t in range(NT):
                    m = mm(ps[:, 4 + t // 4, P * (t % 4):P * (t % 4 + 1)], oc[:, P * t:P * (t + 1)], wproj_g[:, b, :], start=True, stop=True)
                    if t % 4 == 3:
                        m.then_inc(sig("proj_done"), 1)
                for t in range(NT):
                    pe.wait_ge(sig("h2_normed"), b * NT + t + 1)
                    m = nc.tensor.transpose(ps[:, 6 + t // 4, P * (t % 4):P * (t % 4 + 1)], xn[:, t, :], ident[:, :])
                    if t % 4 == 3:
                        m.then_inc(sig("h2_turned"), 1)
                for f in range(2):
                    pe.wait_ge(sig("h2_modded"), b * 2 + f + 1)
                    mm(bank(f), win[:, :], hT[:, HALF * f:HALF * (f + 1)], start=True, stop=True).then_inc(sig("win_done"), 1)
                pe.wait_ge(sig("t_ready"), b * 2 + 2)
                for t in range(NT):
                    m = mm(ps[:, 2, E * t:E * (t + 1)], tT[:, P * t:P * (t + 1)], wgate[:, :], start=True, stop=True)
                m.then_inc(sig("logits"), 1)
                pe.wait_ge(sig("routed"), b + 1)
                for t in range(NT):
                    m = nc.tensor.transpose(ps[0:E, 4 + t // 4, P * (t % 4):P * (t % 4 + 1)], route[:, t, :], ident[:, :])
                m.then_inc(sig("route_turned"), 1)
                pe.wait_ge(sig("route_rows"), b * 2 + 2)
                for t in range(NT):
                    m = mm(ps[:, 6 + t // 4, P * (t % 4):P * (t % 4 + 1)], routeT[:, P * t:P * (t + 1)], b2[:, :], start=True, stop=True)
                m.then_inc(sig("b2_mixed"), 1)
                pe.wait_ge(sig("moe_started"), b * 2 + 2)

            def finish(b):
                pe.wait_ge(sig("moe_added"), b * 16 + 17)
                for t in range(NT):
                    m = nc.tensor.transpose(ps[:, 2 + t // 4, P * (t % 4):P * (t % 4 + 1)], acc[:, t, :], ident[:, :])
                    if t % 4 == 3:
                        m.then_inc(sig("moe_turned"), 1)
                for t in range(NT):
                    if t % 4 == 0:
                        pe.wait_ge(sig("moe_cols"), b * 2 + t // 4 + 1)
                    m = mm(ps[:, 5 + t // 4, P * (t % 4):P * (t % 4 + 1)], accT[:, P * t:P * (t + 1)], wout_g[:, b, :], start=True, stop=True)
                    if t % 4 == 3:
                        m.then_inc(sig("wout_done"), 1)
                pe.wait_ge(sig("y_ready"), b * 2 + 2)

            pe.wait_ge(sig("ident"), 2)
            pe.wait_ge(sig("mod_loaded"), 32)
            nc.tensor.transpose(ps[:, 0, 0:B], cmod[:, :], ident[0:B, 0:B]).then_inc(sig("c_turned"), 1)
            pe.wait_ge(sig("silu_ready"), 2)
            for i, chunk in enumerate((0, 1, 3, 4)):
                m = mm(ps[:, 1, B * i:B * (i + 1)], wmod[:, chunk * C:(chunk + 1) * C], siluT[:, :], start=True, stop=True)
            for i, chunk in enumerate((2, 5)):
                for b in range(B):
                    m = mm(ps[:, 2 + i, C * b:C * (b + 1)], silu_bc[:, b, :], wmod[:, chunk * C:(chunk + 1) * C], start=True, stop=True)
            m.then_inc(sig("mod_done"), 1)
            pe.wait_ge(sig("loaded"), 16 * len(loads[2:]))
            nc.tensor.transpose(ps[:, 4, 0:E * CH], b1rows[:, :], ident[0:E * CH, 0:E * CH]).then_inc(sig("b1_turned"), 1)
            pe.wait_ge(sig("b1_ready"), 1)

            with pe.Fori(0, B) as b:
                for t in range(NT):
                    pe.wait_ge(sig("x_normed"), b * NT + t + 1)
                    m = nc.tensor.transpose(ps[:, t // 4, P * (t % 4):P * (t % 4 + 1)], xn[:, t, :], ident[:, :])
                    if t % 4 == 3:
                        m.then_inc(sig("x_turned"), 1)
                pe.wait_ge(sig("lo_ready"), b * 4 + 1)
                pe.wait_ge(sig("v_kept"), b * 2 + 1)
                for f in range(2):
                    pe.wait_ge(sig("h_ready"), b * 2 + f + 1)
                    for r in range(2):
                        mm(bank(2 + 2 * r + f), wqkv[:, C * r:C * (r + 1)], hT[:, HALF * f:HALF * (f + 1)], start=True, stop=True).then_inc(sig("qk_done"), 1)
                for t in range(NT):
                    m = mm(ps[:, 6 + t // 4, P * (t % 4):P * (t % 4 + 1)], hT[:, P * t:P * (t + 1)], wqkv[:, 2 * C:3 * C], start=True, stop=True)
                    if t % 4 == 3:
                        m.then_inc(sig("v_done"), 1)

            pe.wait_ge(sig("hmean_ready"), 1)
            pe.wait_ge(sig("h_ready"), 2 * B)
            for r in range(2):
                m = mm(ps[0:B, 0, C * r:C * (r + 1)], hmean[:, :], wqkv[:, C * r:C * (r + 1)], start=True, stop=True)
            m.then_inc(sig("means_done"), 1)
            pe.wait_ge(sig("qk_means"), 32)
            pe.wait_ge(sig("means_ready"), 2)
            nc.tensor.transpose(ps[0:KI, 1, 0:MB], qk[:, :], ident[0:MB, 0:MB]).then_inc(sig("ka_pe"), 1)
            pe.wait_ge(sig("ka_sb"), 1)
            mm(ps[0:T * KI, 0, 0:MB], ka_a[:, :, :].rearrange("d t e -> d (t e)"), qkT[:, :], start=True, stop=True).then_inc(sig("ka_pe"), 1)
            pe.wait_ge(sig("lo_ready"), 4 * B + 1)
            mm(ps[0:T * KH, 2, 0:MB], ka_phi1[:, :, :].rearrange("d t e -> d (t e)"), qkT[:, :], start=True, stop=True).then_inc(sig("ka_pe"), 1)
            pe.wait_ge(sig("blocks_loaded"), 16 * len(blocks))
            pe.wait_ge(sig("ka_sb"), 2)
            mm(ps[0:MB, 3, 0:T * KI], axT[:, :], ka_psi1[:, :], start=True, stop=True).then_inc(sig("ka_pe"), 1)
            pe.wait_ge(sig("ka_phi"), 1)
            mm(ps[0:MB, 4, 0:HD], phiT[:, :], ka_phi2[:, :], start=True, stop=True).then_inc(sig("ka_pe"), 1)
            pe.wait_ge(sig("ka_gelu"), 1)
            nc.tensor.transpose(ps[0:T * KI, 5, 0:MB], psi[:, :, :].rearrange("m t g -> m (t g)"), ident[0:MB, 0:MB]).then_inc(sig("ka_pe"), 1)
            pe.wait_ge(sig("v_kept"), 2 * B + 1)
            pe.wait_ge(sig("ka_sb"), 3)
            mm(ps[0:MB, 6, 0:HD], psiT[:, :], ka_psi2[:, :], start=True, stop=True).then_inc(sig("ka_pe"), 1)
            pe.wait_ge(sig("fac_ready"), 1)

            pe.wait_ge(sig("qk_loaded"), 128)
            for a_i in range(AHEAD):
                if a_i >= 2:
                    pe.wait_ge(sig("maxed"), a_i - 1)
                score_max(a_i, None, 0)
            move_max(0, None)

            with pe.Fori(0, NG // 2) as gp:
                for p in range(2):
                    main(gp * 2 + p, p, False, None)
            post(0)
            with pe.Fori(1, B) as b:
                with pe.Fori(0, NG // 2) as gp:
                    for p in range(2):
                        main(b * NG + gp * 2 + p, p, True, b * NG + gp * 2 + p - NG)
                finish(b - 1)
                post(b)
            with pe.Fori(0, NG) as g:
                fi = g + (NI - NG)
                for q in range(UNITS):
                    expert_up(q, None, fi)
                    if q:
                        expert_down(q - 1, fi)
                expert_down(UNITS - 1, fi)
            finish(B - 1)

        @block.scalar
        def _(act):
            act_fn = nc.scalar.activation

            def relu(q, pf, fi):
                u, c = q // 8, q % 4
                if q == 0:
                    act.wait_ge(sig("ffn_staged"), fi + 1)
                act.wait_ge(sig("w1_done"), fi * UNITS + q + 1)
                act.wait_ge(sig("w2_done"), fi * UNITS + q + 1)
                act_fn(mid[:, q % 2, :], bank(5), ACT.Relu, bias=b1s[pf][:, u, c:c + 1]).then_inc(sig("relus"), 1)

            def main(it, p, ffn, fi):
                for s in range(STEPS):
                    if s % 4 == 0:
                        act.wait_ge(sig("pv_done"), it * 16 + s // 4 + 1)
                    act.wait_ge(sig("scores"), it * STEPS + s + 1)
                    act_fn(probs[:, s % 8, :], bank(2 + s % 2), ACT.Exp).then_inc(sig("exps"), 1)
                    if ffn and s % 4 == 1:
                        relu(s // 4, p, fi)

            def post(b):
                act.wait_ge(sig("var2"), b * NT + NT)
                act_fn(sd2[:, :], mv2[:, :, 1], ACT.Sqrt, bias=eps_col[:, 0:1]).then_inc(sig("std2"), 1)
                act.wait_ge(sig("h2_turned"), b * 2 + 2)
                for f in range(2):
                    act_fn(hT[:, HALF * f:HALF * (f + 1)], bank(6 + f), ACT.Identity, scale=mod_col[:, 3, bass.ds(b, 1)], bias=mod_col[:, 2, bass.ds(b, 1)]).then_inc(sig("h2_modded"), 1)
                for f in range(2):
                    act.wait_ge(sig("win_done"), b * 2 + f + 1)
                    act_fn(tT[:, HALF * f:HALF * (f + 1)], bank(f), ACT.Identity, bias=bin_col[:, 0:1]).then_inc(sig("t_ready"), 1)
                act.wait_ge(sig("logits_shifted"), b + 1)
                act_fn(pr[:, :, :], lg[:, :, :], ACT.Exp).then_inc(sig("logit_exps"), 1)
                act.wait_ge(sig("route_turned"), b + 1)
                for f in range(2):
                    act_fn(routeT[:, HALF * f:HALF * (f + 1)], ps[0:E, 4 + f, :], ACT.Copy).then_inc(sig("route_rows"), 1)
                act.wait_ge(sig("b2_mixed"), b + 1)
                for f in range(2):
                    act_fn(acc[:, 4 * f:4 * f + 4, :], tiles(6 + f), ACT.Copy).then_inc(sig("moe_started"), 1)

            def finish(b):
                act.wait_ge(sig("wout_done"), b * 2 + 1)
                for f in range(2):
                    act.wait_ge(sig("moe_turned"), b * 2 + f + 1)
                    act_fn(accT[:, HALF * f:HALF * (f + 1)], bank(2 + f), ACT.Copy).then_inc(sig("moe_cols"), 1)

            act.wait_ge(sig("c_turned"), 1)
            act_fn(siluT[:, :], ps[:, 0, 0:B], ACT.Silu).then_inc(sig("silu_ready"), 1)
            act.wait_ge(sig("eps_set"), 1)
            act.wait_ge(sig("var1"), B * NT)
            act_fn(std[:, :], mv[:, :, 1], ACT.Sqrt, bias=eps_col[:, 0:1]).then_inc(sig("std1"), 1)
            act.wait_ge(sig("b1_ready"), 1)

            with act.Fori(0, B) as b:
                for f in range(2):
                    act.wait_ge(sig("x_turned"), b * 2 + f + 2)
                    act_fn(hT[:, HALF * f:HALF * (f + 1)], bank(f), ACT.Identity, scale=mod_col[:, 1, bass.ds(b, 1)], bias=mod_col[:, 0, bass.ds(b, 1)],
                           accum_out=hsum[:, bass.ds(b * 2 + f, 1)]).then_inc(sig("h_ready"), 1)
                act.wait_ge(sig("qk_stored"), b * 96 + 1)
                for f in range(2):
                    for r in range(2):
                        act.wait_ge(sig("qk_done"), b * 4 + 2 * f + r + 1)
                        act_fn(qk_hi[:, r, HALF * f:HALF * (f + 1)], bank(2 + 2 * r + f), ACT.Identity, scale=qk_scale[:, r:r + 1]).then_inc(sig("hi_ready"), 1)
                for f in range(2):
                    act.wait_ge(sig("v_done"), b * 2 + f + 1)
                    act_fn(v_all[:, bass.ds(b * NG, NG), 4 * f:4 * f + 4, :].rearrange("p g t c -> p t g c"), bank(6 + f).rearrange("p (t g c) -> p t g c", t=4, g=NG), ACT.Copy).then_inc(sig("v_kept"), 1)

            act.wait_ge(sig("means_done"), 1)
            for r in range(2):
                act_fn(qkm[:, r, :], ps[0:B, 0, C * r:C * (r + 1)], ACT.Copy).then_inc(sig("means_ready"), 1)
            act.wait_ge(sig("ka_pe"), 3)
            act_fn(phiT[:, :], ps[0:T * KH, 2, 0:MB], ACT.Silu, bias=ka_bphi1[:, 0:1]).then_inc(sig("ka_phi"), 1)
            act.wait_ge(sig("ka_var"), 1)
            act_fn(pst[:, :], psv[:, :], ACT.Sqrt, bias=eps_col[0:MB, 0:1], scale=1.0 / KI).then_inc(sig("ka_std"), 1)
            act.wait_ge(sig("ka_psi"), 1)
            act_fn(psi[:, :, :], psq[:, :, :], ACT.Gelu).then_inc(sig("ka_gelu"), 1)

            with act.Fori(0, NG // 2) as gp:
                for p in range(2):
                    main(gp * 2 + p, p, False, None)
            post(0)
            with act.Fori(1, B) as b:
                with act.Fori(0, NG // 2) as gp:
                    for p in range(2):
                        main(b * NG + gp * 2 + p, p, True, b * NG + gp * 2 + p - NG)
                finish(b - 1)
                post(b)
            with act.Fori(0, NG // 2) as gp:
                for p in range(2):
                    for q in range(UNITS):
                        relu(q, p, gp * 2 + p + (NI - NG))
            finish(B - 1)

        @block.vector
        def _(dve):
            ch = Chain(dve, sig("dve_steps"))
            tt, tsc, stt = nc.vector.tensor_tensor, nc.vector.tensor_scalar, nc.vector.scalar_tensor_tensor
            red = nc.vector.tensor_reduce

            def take_max(a_i, count):
                nt, mh, j = a_i // 8, a_i // 4 % 2, a_i % 4
                dve.wait_ge(sig("max_scores"), count + 1)
                red(mxp[:, nt, mh, j:j + 1], bank(a_i % 2), X, ALU.max).then_inc(sig("maxed"), 1)

            def split_max(half, done, p, k, staged):
                dve.wait_ge(sig("maxed"), done)
                if k is not None:
                    dve.wait_ge(sig("max_turned"), k)
                dve.wait_ge(sig("beta_staged"), staged)
                m4 = mx[:, :].rearrange("p (j t) -> p j t", j=GH)
                ch.link(tt(m4, mxp[:, 4 * half:4 * half + 4, 0, :].rearrange("p t j -> p j t"),
                           mxp[:, 4 * half:4 * half + 4, 1, :].rearrange("p t j -> p j t"), ALU.max))
                bg = beta_g[p][:, :].unsqueeze(2).broadcast_to([P, GH, 4])
                ch.link(tt(mxb[:, :].rearrange("p (j t) -> p j t", j=GH), m4, bg, ALU.add))
                ch.link(tt(mrow[:, :].rearrange("p (j t) -> p j t", j=GH), bg, mxb[:, :].rearrange("p (j t) -> p j t", j=GH), ALU.subtract))
                ch.link(nc.vector.tensor_copy(mparts[:, 0, :], mrow[:, :]))
                tt(mparts[:, 1, :], mrow[:, :], mparts[:, 0, :].bitcast(F32), ALU.subtract).then_inc(sig("max_parts"), 1)

            def move_max(count, stored):
                dve.wait_ge(sig("max_turned"), count + 1)
                if stored is not None:
                    dve.wait_ge(sig("max_rows"), stored)
                nc.vector.tensor_copy(mrows[:, :], ps[0:32, 7, 0:P]).then_inc(sig("max_moved"), 1)

            def moe_add(k, pf, fi, batches):
                u, th = k // 2, k % 2
                if k == 0:
                    dve.wait_ge(sig("moe_started"), batches * 2)
                dve.wait_ge(sig("w2_done"), fi * UNITS + 4 * k + 6)
                dve.wait_ge(sig("ffn_staged"), fi + 1)
                dve.wait_ge(sig("moe_added"), fi * 4 + k + 1)
                for i in range(4):
                    t = 4 * th + i
                    m = stt(acc[:, t, :], ps[:, 6, P * i:P * (i + 1)], rts[pf][:, u, t:t + 1], acc[:, t, :], ALU.mult, ALU.add)
                m.then_inc(sig("moe_added"), 1)

            def main(it, p, ffn, fi, b):
                def o_move(half):
                    dve.wait_ge(sig("pv_done"), it * 16 + 8 * half + 10)
                    dve.wait_ge(sig(f"o_stored{half}"), it * 64 + 1)
                    nc.vector.tensor_copy(oT[:, half, :], bank(4)).then_inc(sig("o_moved"), 1)

                for s in range(STEPS):
                    take_max((s - LAG) % STEPS, it * STEPS + AHEAD + s)
                    if s == LAG - 1:
                        split_max(1, it * STEPS + AHEAD + s + 1, p, it * 2 + 1, it + 1)
                    if s == LAG + 31:
                        split_max(0, it * STEPS + AHEAD + s + 1, 1 - p, it * 2 + 2, it + 2)
                    if s == 22:
                        move_max(it * 2 + 1, it * 64 + 32)
                    if s == 54:
                        move_max(it * 2 + 2, it * 64 + 64)
                    if s == 37:
                        o_move(0)
                    if ffn and s % 16 == 5 and s > 16:
                        moe_add(s // 16 - 1, p, fi, b)
                if ffn:
                    moe_add(3, p, fi, b)
                o_move(1)

            def post(b):
                dve.wait_ge(sig("o_loaded"), b * 32 + 32)
                ch.link(nc.vector.reciprocal(den[:, :], den[:, :]))
                dve.wait_ge(sig("fac_loaded"), 16 * B)
                stt(oc[:, :], oc[:, :], vfac[:, bass.ds(b, 1)], den[:, :], ALU.mult, ALU.mult).then_inc(sig("o_normed"), 1)
                dve.wait_ge(sig("xg_ready"), b + 1)
                dve.wait_ge(sig("y_ready"), b * 2)
                for f in range(2):
                    dve.wait_ge(sig("proj_done"), b * 2 + f + 1)
                    ch.did(tt(x1[:, 4 * f:4 * f + 4, :], tiles(4 + f), xg[:, 4 * f:4 * f + 4, :], ALU.add))
                ch.wait()
                for t in range(NT):
                    ch.did(nc.vector.bn_stats(st2[:, t, :], x1[:, t, :]))
                ch.wait()
                nc.vector.memset(credit[:, 15:16], 0.0)
                for t in range(NT):
                    nc.vector.bn_aggr(mv2[:, t, :], st2[:, t, :]).then_inc(sig("var2"), 1)
                dve.wait_ge(sig("var2"), b * NT + NT)
                dve.wait_ge(sig("std2"), b + 1)
                ch.link(nc.vector.reciprocal(sd2[:, :], sd2[:, :]))
                dve.wait_ge(sig("h2_turned"), b * 2)
                for t in range(NT):
                    tsc(xn[:, t, :], x1[:, t, :], mv2[:, t, 0:1], sd2[:, t:t + 1], ALU.subtract, ALU.mult).then_inc(sig("h2_normed"), 1)
                dve.wait_ge(sig("logits"), b + 1)
                ch.link(tt(lg[:, :, :], ps[:, 2, 0:NT * E].rearrange("p (t e) -> p t e", e=E), over_tiles(bgate_bc), ALU.add))
                ch.link(red(gm[:, :], lg[:, :, :], X, ALU.max))
                tt(lg[:, :, :], lg[:, :, :], over_experts(gm), ALU.subtract).then_inc(sig("logits_shifted"), 1)
                dve.wait_ge(sig("logit_exps"), b + 1)
                ch.link(red(gm[:, :], pr[:, :, :], X, ALU.add))
                ch.link(nc.vector.reciprocal(gm[:, :], gm[:, :]))
                ch.link(tt(pr[:, :, :], pr[:, :, :], over_experts(gm), ALU.mult))
                for src, pick in ((pr, g1), (g0, g2)):
                    ch.link(red(gm[:, :], src[:, :, :], X, ALU.max))
                    ch.link(tt(pick[:, :, :], src[:, :, :], over_experts(gm), ALU.is_ge))
                    ch.link(tt(pick[:, :, :], pick[:, :, :], over_tiles(rev), ALU.mult))
                    ch.link(red(gm[:, :], pick[:, :, :], X, ALU.max))
                    ch.link(tt(pick[:, :, :], pick[:, :, :], over_experts(gm), ALU.is_equal))
                    if pick is g1:
                        ch.link(stt(g0[:, :, :], g1[:, :, :], -2.0, pr[:, :, :], ALU.mult, ALU.add))
                ch.link(tt(g1[:, :, :], g1[:, :, :], g2[:, :, :], ALU.add))
                ch.link(tt(pr[:, :, :], pr[:, :, :], g1[:, :, :], ALU.mult))
                ch.link(red(gm[:, :], pr[:, :, :], X, ALU.add))
                ch.link(nc.vector.reciprocal(gm[:, :], gm[:, :]))
                dve.wait_ge(sig("ffn_staged"), b * NG)
                tt(route[:, :, :], pr[:, :, :], over_experts(gm), ALU.mult).then_inc(sig("routed"), 1)

            POST = 1 + 2 + NT + 1 + 2 + 3 + 11 + 4

            def finish(b):
                dve.wait_ge(sig("stored"), b * 16 + 1)
                dve.wait_ge(sig("x1b_ready"), b + 1)
                for f in range(2):
                    dve.wait_ge(sig("wout_done"), b * 2 + f + 2)
                    tt(y[:, 4 * f:4 * f + 4, :], tiles(5 + f), x1[:, 4 * f:4 * f + 4, :], ALU.add).then_inc(sig("y_ready"), 1)

            nc.vector.memset(eps_col[:, :], EPS).then_inc(sig("eps_set"), 1)
            for i in range(E):
                nc.vector.memset(rev[:, i:i + 1], float(E - i)).then_inc(sig("rev_set"), 1)
            dve.wait_ge(sig("rev_set"), E)
            ch.did(nc.vector.memset(qk_scale[:, 1:2], 1.0))
            nc.vector.memset(acc[:, :, :], 0.0).then_inc(sig("row_values"), 1)
            nc.vector.memset(y[:, :, :], 1.0).then_inc(sig("row_values"), 1)
            for i, (name, n) in enumerate(CREDIT.items()):
                nc.vector.memset(credit[:, i:i + 1], 0.0).then_inc(sig(name), n)
            for i in range(2):
                nc.vector.memset(K[i][:, :, :].bitcast(F32), 0.0).then_inc(sig("qk_zero"), 1)
                nc.vector.memset(Q[i][:, :].bitcast(F32), 0.0).then_inc(sig("qk_zero"), 1)
                nc.vector.memset(V[i][:, :, :, :], 1.0).then_inc(sig("v_ones"), 1)
            dve.wait_ge(sig("silu_ready"), 1)
            for b in range(B):
                m = nc.vector.tensor_copy(silu_bc[:, b, :], siluT[:, b:b + 1].broadcast_to([P, P]))
            m.then_inc(sig("silu_ready"), 1)
            for t in range(B * NT):
                if t % NT == 0:
                    dve.wait_ge(sig(f"x_loaded{t // NT}"), 16)
                ch.did(nc.vector.bn_stats(stats[:, t, :], x_all[:, t, :]))
            ch.wait()
            for t in range(B * NT):
                nc.vector.bn_aggr(mv[:, t, :], stats[:, t, :]).then_inc(sig("var1"), 1)
            dve.wait_ge(sig("mod_done"), 1)
            ch.did(nc.vector.tensor_copy(mod_col[:, 0, :], ps[:, 1, 0:B]))
            ch.did(tsc(mod_col[:, 1, :], ps[:, 1, B:2 * B], 1.0, None, ALU.add))
            ch.did(nc.vector.tensor_copy(mod_col[:, 2, :], ps[:, 1, 2 * B:3 * B]))
            ch.did(tsc(mod_col[:, 3, :], ps[:, 1, 3 * B:4 * B], 1.0, None, ALU.add))
            ch.link(nc.vector.tensor_copy(gate_bc[:, :, :], ps[:, 2:4, :]))
            ch.link(tsc(gt0[:, :, :], gate_bc[:, :, :], 0.0, 2.0, ALU.is_ge, ALU.mult))
            ch.link(stt(gt1[:, :, :], gate_bc[:, :, :], -1.0, gate_bc[:, :, :], ALU.mult, ALU.max))
            ch.link(tsc(gt1[:, :, :], gt1[:, :, :], 0.25, None, ALU.max))
            ch.link(stt(gate_bc[:, :, :], gt0[:, :, :], -1.0, gt1[:, :, :], ALU.add, ALU.mult))
            dve.wait_ge(sig("loaded"), 16 * len(loads[2:]))
            for b in range(B):
                g_a, g_b = gate_bc[:, 0, C * b:C * (b + 1)], gate_bc[:, 1, C * b:C * (b + 1)]
                ch.did(tt(wproj_g[:, b, :], wproj[:, :], g_a, ALU.mult))
                ch.did(tt(wout_g[:, b, :], wout[:, :], g_b, ALU.mult))
                ch.did(tt(bproj_g[:, b, :], bproj_bc[:, :], g_a, ALU.mult))
                ch.did(tt(bout_g[:, b, :], bout_bc[:, :], g_b, ALU.mult))
            ch.did(tsc(qk_scale[:, 0:1], alpha_col[:, :], ATTN_SCALE, None, ALU.mult))
            ch.wait()
            dve.wait_ge(sig("std1"), 1)
            dve.wait_ge(sig("var1"), B * NT)
            ch.link(nc.vector.reciprocal(rstd[:, :], std[:, :]))
            dve.wait_ge(sig("b1_turned"), 1)
            nc.vector.tensor_copy(b1T[:, :], ps[:, 4, 0:E * CH]).then_inc(sig("b1_ready"), 1)

            with dve.Fori(0, B) as b:
                dve.wait_ge(sig("x_turned"), b * 2 + 1)
                for t in range(NT):
                    i = b * NT + t
                    tsc(xn[:, t, :], x_all[:, i, :], mv[:, bass.ds(i, 1), 0], rstd[:, bass.ds(i, 1)], ALU.subtract, ALU.mult).then_inc(sig("x_normed"), 1)
                dve.wait_ge(sig("qk_stored"), b * 96 + 1)
                for f in range(2):
                    for r in range(2):
                        dve.wait_ge(sig("hi_ready"), b * 4 + 2 * f + r + 1)
                        stt(qk_lo[:, r, HALF * f:HALF * (f + 1)], bank(2 + 2 * r + f), qk_scale[:, r:r + 1],
                            qk_hi[:, r, HALF * f:HALF * (f + 1)].bitcast(F32), ALU.mult, ALU.subtract).then_inc(sig("lo_ready"), 1)

            dve.wait_ge(sig("h_ready"), 2 * B)
            hs = hsum[:, :].rearrange("p (b f) -> p b f", f=2)
            ch.link(red(hmean[:, :], hs, X, ALU.add))
            tsc(hmean[:, :], hmean[:, :], 1.0 / N, None, ALU.mult).then_inc(sig("hmean_ready"), 1)
            dve.wait_ge(sig("ka_pe"), 1)
            nc.vector.tensor_copy(qkT[:, :], ps[0:KI, 1, 0:MB]).then_inc(sig("ka_sb"), 1)
            dve.wait_ge(sig("ka_pe"), 2)
            nc.vector.tensor_copy(axT[:, :], ps[0:T * KI, 0, 0:MB]).then_inc(sig("ka_sb"), 1)
            dve.wait_ge(sig("ka_pe"), 4)
            grp = lambda t: t[:, :].rearrange("m (t g) -> m t g", g=KI)
            wide = lambda t: t[:, :].unsqueeze(2).broadcast_to([MB, T, KI])
            ch.link(tt(psi[:, :, :], ps[0:MB, 3, 0:T * KI].rearrange("m (t g) -> m t g", g=KI), grp(bpsi1_bc), ALU.add))
            ch.link(red(psm[:, :], psi[:, :, :], X, ALU.add))
            ch.link(tsc(psm[:, :], psm[:, :], 1.0 / KI, None, ALU.mult))
            ch.link(tt(psi[:, :, :], psi[:, :, :], wide(psm), ALU.subtract))
            ch.link(tt(psq[:, :, :], psi[:, :, :], psi[:, :, :], ALU.mult))
            red(psv[:, :], psq[:, :, :], X, ALU.add).then_inc(sig("ka_var"), 1)
            dve.wait_ge(sig("ka_std"), 1)
            ch.link(nc.vector.reciprocal(pst[:, :], pst[:, :]))
            ch.link(tt(psq[:, :, :], psi[:, :, :], wide(pst), ALU.mult))
            ch.link(tt(psq[:, :, :], psq[:, :, :], grp(lng_bc), ALU.mult))
            tt(psq[:, :, :], psq[:, :, :], grp(lnb_bc), ALU.add).then_inc(sig("ka_psi"), 1)
            dve.wait_ge(sig("ka_pe"), 5)
            ch.link(tt(phi[:, :], ps[0:MB, 4, 0:HD], bphi2_bc[:, :], ALU.add))
            dve.wait_ge(sig("ka_pe"), 6)
            nc.vector.tensor_copy(psiT[:, :], ps[0:T * KI, 5, 0:MB]).then_inc(sig("ka_sb"), 1)
            dve.wait_ge(sig("ka_pe"), 7)
            ch.link(tt(psi_o[:, :], ps[0:MB, 6, 0:HD], bpsi2_bc[:, :], ALU.add))
            ch.link(tt(phi[:, :], phi[:, :], psi_o[:, :], ALU.mult))
            ch.link(tsc(phi[:, :], phi[:, :], temp_bc[:, 0:1], None, ALU.mult))
            ch.link(tt(fac[:, :].rearrange("m (t o) -> m t o", o=KO), phi[:, :].rearrange("m (t o) -> m t o", o=KO), mix_bc[:, :].unsqueeze(2).broadcast_to([MB, T, KO]), ALU.mult))
            tsc(fac[:, :], fac[:, :], 1.0, gamma_col[:, 0:1], ALU.add, ALU.mult).then_inc(sig("fac_ready"), 1)

            for a_i in range(AHEAD):
                take_max(a_i, a_i)
                if a_i == 31:
                    split_max(0, a_i + 1, 0, None, 1)
            move_max(0, None)

            PER = 2 * 4
            with dve.Fori(0, NG // 2) as gp:
                ch.enter(gp, 2 * PER)
                for p in range(2):
                    main(gp * 2 + p, p, False, None, 0)
                ch.leave(NG // 2)
            post(0)
            with dve.Fori(1, B) as b:
                ch.enter(b - 1, NG * PER + POST)
                with dve.Fori(0, NG // 2) as gp:
                    inner = Chain(dve, ch.sem)
                    inner.base, inner.n = ch.base + gp * (2 * PER), 0
                    keep, ch = ch, inner
                    for p in range(2):
                        main(b * NG + gp * 2 + p, p, True, b * NG + gp * 2 + p - NG, b)
                    assert inner.n == 2 * PER
                    ch = keep
                ch.n += NG * PER
                finish(b - 1)
                post(b)
                ch.leave(B - 1)
            with dve.Fori(0, NG // 2) as gp:
                for p in range(2):
                    for k in range(4):
                        moe_add(k, p, gp * 2 + p + (NI - NG), B)
            finish(B - 1)

        @block.gpsimd
        def _(pool):
            def stage(group, p):
                for j in range(GH):
                    m = nc.gpsimd.tensor_copy(V[p][:, :, j, 0:HD], v_all[:, group, :, HD * j:HD * (j + 1)])
                m.then_inc(sig("v_staged"), 1)
                nc.gpsimd.tensor_copy(beta_g[p][:, :], beta_bc[:, bass.ds(group * GH, GH)]).then_inc(sig("beta_staged"), 1)

            def stage_ffn(p, g):
                nc.gpsimd.tensor_copy(b1s[p][:, :, :].rearrange("p u c -> p (u c)"), b1T[:, bass.ds(g * 2 * CH, 2 * CH)])
                for u in range(2):
                    m = nc.gpsimd.tensor_copy(rts[p][:, u, :], route[:, :, g * 2 + u])
                m.then_inc(sig("ffn_staged"), 1)

            def main(it, p, ffn, b, g):
                if ffn:
                    pool.wait_ge(sig("exps"), it * STEPS - STEPS + 2)
                    pool.wait_ge(sig("o_moved"), it * 2 - 1)
                    pool.wait_ge(sig("routed"), b)
                    stage_ffn(p, g)
                pool.wait_ge(sig("pv_done"), it * 16 + 2)
                pool.wait_ge(sig("maxed"), it * STEPS + AHEAD)
                stage((it + 1) % NI, 1 - p)

            def residual(b):
                pool.wait_ge(sig("h2_normed"), b * NT)
                for t in range(NT):
                    m = nc.gpsimd.tensor_tensor(xg[:, t, :], x_all[:, b * NT + t, :], bproj_g[:, b, :], ALU.add)
                m.then_inc(sig("xg_ready"), 1)

            def residual2(b):
                pool.wait_ge(sig("h2_normed"), b * NT + NT)
                for t in range(NT):
                    m = nc.gpsimd.tensor_tensor(x1[:, t, :], x1[:, t, :], bout_g[:, b, :], ALU.add)
                m.then_inc(sig("x1b_ready"), 1)

            nc.gpsimd.memset(ident[:, :], 0.0).then_inc(sig("ident"), 1)
            for w in (ka_phi2, ka_psi1, ka_psi2):
                nc.gpsimd.memset(w[:, :], 0.0).then_inc(sig("blocks_zero"), 1)
            pool.wait_ge(sig("ident"), 1)
            nc.gpsimd.affine_select(out=ident[:, :], in_=ident[:, :], compare_op=ALU.not_equal, fill=1.0,
                                    base=0, pattern=[[-1, P]], channel_multiplier=1).then_inc(sig("ident"), 1)
            pool.wait_ge(sig("v_ones"), 2)
            pool.wait_ge(sig("loaded"), 16 * len(loads[2:]))
            pool.wait_ge(sig("b1_ready"), 1)
            pool.wait_ge(sig("v_kept"), 2 + 1)
            stage(0, 0)
            pool.wait_ge(sig("v_kept"), 2 * B + 1)

            residual(0)
            with pool.Fori(0, NG // 2) as gp:
                for p in range(2):
                    main(gp * 2 + p, p, False, 0, gp * 2 + p)
            residual2(0)
            with pool.Fori(1, B) as b:
                residual(b)
                with pool.Fori(0, NG // 2) as gp:
                    for p in range(2):
                        main(b * NG + gp * 2 + p, p, True, b, gp * 2 + p)
                residual2(b)
            pool.wait_ge(sig("routed"), B)
            with pool.Fori(0, NG // 2) as gp:
                for p in range(2):
                    fi = gp * 2 + p + (NI - NG)
                    pool.wait_ge(sig("relus"), fi * UNITS - UNITS + 1)
                    pool.wait_ge(sig("moe_added"), fi * 4 - 3)
                    stage_ffn(p, gp * 2 + p)


def kernel(**inputs):
    import numpy as _np
    import concourse.bacc as _bacc
    from concourse import mybir as _mybir
    from concourse.bass_utils import run_bass_kernel_spmd as _run

    nc = _bacc.Bacc("TRN2", target_bir_lowering=False, num_devices=1)
    arrays, args = {}, {}
    for name, value in inputs.items():
        v = _np.ascontiguousarray(value).reshape(_np.shape(value) or (1,))
        arrays[f"in_{name}"] = v
        args[name] = nc.dram_tensor(f"in_{name}", v.shape, _mybir.dt.from_np(v.dtype), kind="ExternalInput").ap()
    out = nc.dram_tensor("out_0", (B, N, C), F32, kind="ExternalOutput").ap()
    build(nc, args, out)
    r = _run(nc, [arrays], core_ids=[0])
    return r.results[0]["out_0"]
```

```python
from contextlib import ExitStack

import concourse.bass as bass
from concourse import mybir

F32 = mybir.dt.float32
F32R = mybir.dt.float32r
ACT = mybir.ActivationFunctionType
ALU = mybir.AluOpType
X = mybir.AxisListType.X

P = 128
B, N, C = 4, 1024, 128
H, HD = 16, 8
T = 4
KI, KH, KO = 16, 8, 2
E, DM = 8, 512
NT = N // P
GH = 4
NG = H // GH
NI = B * NG
PARTS = 3 * HD
ROWS = PARTS + 2
HALF = 512
CH = DM // P
STEPS = 64
LAG = 16
AHEAD = STEPS - LAG
UNITS = 16
EPS = 1e-5
ATTN_SCALE = HD ** -0.5 / 0.72


def rotation(reserved):
    order, used = [], [0, 1, 2]
    for s in range(STEPS):
        pick = next(i for i in used if not (i == 2 and s in reserved))
        used = [i for i in used if i != pick] + [pick]
        order.append(pick)
    back = [next(d for d in range(1, STEPS) if order[(s - d) % STEPS] == order[s]) for s in range(STEPS)]
    return order, back


TURN = (20, 52)
B_BANK, B_BACK = rotation([s + i for s in TURN for i in range(4)])
A_BANK, A_BACK = rotation(())

CREDIT = {"exps": 8, "w2_done": 2, "pv_done": 2, "o_moved": 1, "relus": 1, "w_split1": 1, "moe_taken": 1, "moe_added": 2, "x_turned": 1, "lo_ready": 1, "v_kept": 1, "qk_stored": 1, "wout_done": 1, "stored": 1, "o_stored0": 1, "o_stored1": 1}


class Chain:

    def __init__(self, eng, sem):
        self.eng, self.sem, self.n, self.base = eng, sem, 0, None

    def did(self, ins):
        ins.then_inc(self.sem, 1)
        self.n += 1

    def value(self):
        return self.n if self.base is None else self.base + self.n

    def wait(self):
        self.eng.wait_ge(self.sem, self.value())

    def link(self, ins):
        self.did(ins)
        self.wait()

    def enter(self, index, per):
        self.outer = (self.base, self.n)
        start = self.n if self.base is None else self.base + self.n
        self.base, self.n, self.per = index * per + start, 0, per

    def leave(self, times):
        assert self.n == self.per, (self.n, self.per)
        base, n = self.outer
        self.base, self.n = base, n + times * self.per


def build(nc, a, out):
    with ExitStack() as ctx:
        def sb(name, shape, dt=F32):
            return ctx.enter_context(nc.sbuf_tensor(name, shape, dt))

        sems = {}

        def sig(name):
            if name not in sems:
                sems[name] = ctx.enter_context(nc.semaphore(name))
            return sems[name]

        ps = ctx.enter_context(nc.psum_tensor("ps", [P, 8, HALF], F32))

        q_dram = nc.dram_tensor("q_dram", [B * H, ROWS, N], F32)
        k_dram = nc.dram_tensor("k_dram", [B * H, ROWS, N], F32)
        o_dram = nc.dram_tensor("o_dram", [B * H, 2 * HD, N], F32)
        mean_dram = nc.dram_tensor("mean_dram", [2, B, C], F32)
        route_dram = nc.dram_tensor("route_dram", [E, N], F32)
        fac_dram = nc.dram_tensor("fac_dram", [B * H, HD], F32)

        wqkv = sb("wqkv", [P, 3 * C]); wproj = sb("wproj", [P, C])
        win = sb("win", [P, C]); wout = sb("wout", [P, C]); wgate = sb("wgate", [P, E])
        wmod = sb("wmod", [P, 6 * C]); cmod = sb("cmod", [B, C])
        b1rows = sb("b1rows", [E * CH, P]); b2 = sb("b2", [E, C])
        bproj_bc = sb("bproj_bc", [P, C]); bout_bc = sb("bout_bc", [P, C])
        bin_col = sb("bin_col", [P, 1]); bgate_bc = sb("bgate_bc", [P, E])
        beta_bc = sb("beta_bc", [P, B * H]); alpha_col = sb("alpha_col", [P, 1])
        ka_a = sb("ka_a", [KI, T, KI]); ka_phi1 = sb("ka_phi1", [KI, T, KH])
        ka_bphi1 = sb("ka_bphi1", [T * KH, 1]); ka_phi2 = sb("ka_phi2", [T * KH, HD])
        ka_psi1 = sb("ka_psi1", [T * KI, T * KI]); ka_psi2 = sb("ka_psi2", [T * KI, HD])
        MB = B * H
        bphi2_bc = sb("bphi2_bc", [MB, HD]); bpsi1_bc = sb("bpsi1_bc", [MB, T * KI])
        lng_bc = sb("lng_bc", [MB, T * KI]); lnb_bc = sb("lnb_bc", [MB, T * KI])
        bpsi2_bc = sb("bpsi2_bc", [MB, HD]); mix_bc = sb("mix_bc", [MB, T])
        temp_bc = sb("temp_bc", [MB, 1]); gamma_col = sb("gamma_col", [MB, 1])

        ident = sb("ident", [P, P]); rev = sb("rev", [P, E])
        siluT = sb("siluT", [P, B])
        mod_col = sb("mod_col", [P, 4, B])
        gate_bc = sb("gate_bc", [P, 2, B * C])
        wproj_g = sb("wproj_g", [P, B, C]); wout_g = sb("wout_g", [P, B, C])
        bproj_g = sb("bproj_g", [P, B, C]); bout_g = sb("bout_g", [P, B, C])
        b1T = sb("b1T", [P, E * CH])

        eps_col = sb("eps_col", [P, 1]); qk_scale = sb("qk_scale", [P, 2]); credit = sb("credit", [P, len(CREDIT) + 1])
        pool_wait = sb("pool_wait", [P, 1])

        x_all = sb("x_all", [P, B * NT, C]); v_all = sb("v_all", [P, NI, NT, GH * HD])
        stats = sb("stats", [P, B * NT, 6]); mv = sb("mv", [P, B * NT, 2])
        std = sb("std", [P, B * NT]); rstd = sb("rstd", [P, B * NT])
        xn = sb("xn", [P, NT, C]); hT = sb("hT", [P, N])
        hsum = sb("hsum", [P, 2 * B]); hmean = sb("hmean", [P, B])
        qk_hi = sb("qk_hi", [P, 2, N], F32R); qk_lo = sb("qk_lo", [P, 2, N], F32R)

        qkm = sb("qkm", [B, 2, C]); qk = sb("qk", [MB, KI]); qkT = sb("qkT", [KI, MB])
        axT = sb("axT", [T * KI, MB]); phiT = sb("phiT", [T * KH, MB]); phi = sb("phi", [MB, HD])
        psi = sb("psi", [MB, T, KI]); psq = sb("psq", [MB, T, KI]); psm = sb("psm", [MB, T])
        psv = sb("psv", [MB, T]); pst = sb("pst", [MB, T]); psiT = sb("psiT", [T * KI, MB])
        psi_o = sb("psi_o", [MB, HD]); fac = sb("fac", [MB, HD]); vfac = sb("vfac", [P, B])

        Q = [sb(f"Q{i}", [P, N], F32R) for i in range(2)]
        K = [sb(f"K{i}", [P, GH, N], F32R) for i in range(2)]
        V = [sb(f"V{i}", [P, NT, GH, 32]) for i in range(2)]
        beta_g = [sb(f"beta_g{i}", [P, GH]) for i in range(2)]
        probs = sb("probs", [P, 8, HALF])
        gt0, gt1 = probs[:, 0:2, :], probs[:, 2:4, :]
        silu_bc = probs[:, 4, :].rearrange("p (b n) -> p b n", b=B)
        mxp = sb("mxp", [P, NT, 2, GH]); mx = sb("mx", [P, 16]); mxb = sb("mxb", [P, 16])
        mrow = sb("mrow", [P, 16]); mparts = sb("mparts", [P, 2, 16], F32R)
        mrows = sb("mrows", [32, P])
        oT = sb("oT", [P, 2, HALF])
        w_raw = [sb(f"w_raw{i}", [P, DM + CH * C]) for i in range(2)]
        w_hi, w_lo = qk_hi, qk_lo
        b1s = [sb(f"b1s{i}", [P, 2, CH]) for i in range(2)]
        mid_hi = sb("mid_hi", [P, 2, HALF], F32R); mid_lo = sb("mid_lo", [P, 2, HALF], F32R)
        x_space = x_all[:, :, :].rearrange("p t c -> p (t c)")
        route_bc = [x_space[:, N * i:N * (i + 1)] for i in range(2)]
        weighted = x_space[:, 2 * N:3 * N].rearrange("p (i n) -> p i n", i=2)
        mid = x_space[:, 3 * N:4 * N].rearrange("p (i n) -> p i n", i=2)

        oc = sb("oc", [P, N]); den = sb("den", [P, N])
        xg = sb("xg", [P, NT, C]); x1 = sb("x1", [P, NT, C])
        st2 = sb("st2", [P, NT, 6]); mv2 = sb("mv2", [P, NT, 2]); sd2 = sb("sd2", [P, NT])
        t_raw = oc
        t_hi = sb("t_hi", [P, N], F32R); t_lo = sb("t_lo", [P, N], F32R)
        lg = sb("lg", [P, NT, E]); pr = sb("pr", [P, NT, E]); g0 = sb("g0", [P, NT, E])
        g1 = sb("g1", [P, NT, E]); g2 = sb("g2", [P, NT, E]); gm = sb("gm", [P, NT])
        route = sb("route", [P, NT, E]); routeT = sb("routeT", [E, N])
        accT = sb("accT", [P, N]); y = sb("y", [P, NT, C])

        def bank(i):
            return ps[:, i, :]

        def b_bank(s):
            return (2, 3, 7)[B_BANK[s]]

        def a_bank(s, ffn):
            return s % 2 if ffn else (0, 1, 5)[A_BANK[s]]

        def tiles(i):
            return ps[:, i, :].rearrange("p (t c) -> p t c", c=P)

        def over_experts(t):
            return t[:, :].unsqueeze(2).broadcast_to([P, NT, E])

        def over_tiles(t):
            return t[:, :].unsqueeze(1).broadcast_to([P, NT, E])

        row = lambda v, n: v.partition_broadcast(n)
        loads = [(cmod[:, :], a["L0_c"]), (wmod[:, :], a["L0_wmod"])]
        loads += [(wqkv[:, :], a["L0_attn_Wqkv"]), (wproj[:, :], a["L0_attn_Wproj"]),
                  (win[:, :], a["L0_ffn_W_in"]), (wout[:, :], a["L0_ffn_W_out"]),
                  (wgate[:, :], a["L0_ffn_W_gate"]),
                  (b1rows[:, :], a["L0_ffn_b1"].rearrange("e (c p) -> (e c) p", p=P)),
                  (b2[:, :], a["L0_ffn_b2"]),
                  (bproj_bc[:, :], row(a["L0_attn_bproj"], P)),
                  (bout_bc[:, :], row(a["L0_ffn_b_out"], P)),
                  (bin_col[:, :], a["L0_ffn_b_in"].rearrange("(p o) -> p o", o=1)),
                  (bgate_bc[:, :], row(a["L0_ffn_b_gate"], P)),
                  (ka_a[:, :, :], a["L0_attn_A"].rearrange("t d e -> d t e")),
                  (ka_phi1[:, :, :], a["L0_attn_Wphi1"].rearrange("t d e -> d t e")),
                  (ka_bphi1[:, :], a["L0_attn_bphi1"].rearrange("t (h o) -> (t h) o", o=1)),
                  (bphi2_bc[:, :], row(a["L0_attn_bphi2"].rearrange("t o -> (t o)"), MB)),
                  (bpsi1_bc[:, :], row(a["L0_attn_bpsi1"].rearrange("t o -> (t o)"), MB)),
                  (lng_bc[:, :], row(a["L0_attn_ln_g"].rearrange("t o -> (t o)"), MB)),
                  (lnb_bc[:, :], row(a["L0_attn_ln_b"].rearrange("t o -> (t o)"), MB)),
                  (bpsi2_bc[:, :], row(a["L0_attn_bpsi2"].rearrange("t o -> (t o)"), MB)),
                  (mix_bc[:, :], row(a["L0_attn_mixing"], MB)),
                  (temp_bc[:, :], row(a["L0_attn_temp_scale"].rearrange("(o) -> o", o=1), MB))]
        loads += [(alpha_col[h * HD:(h + 1) * HD, :], row(a["L0_attn_alpha"][h:h + 1], HD)) for h in range(H)]
        loads += [(beta_bc[:, b * H:(b + 1) * H], row(a["L0_attn_beta"], P)) for b in range(B)]
        loads += [(gamma_col[b * H:(b + 1) * H, :], a["L0_attn_gamma"].rearrange("(h o) -> h o", o=1))
                  for b in range(B)]
        blocks = []
        for t in range(T):
            blocks += [(ka_phi2[t * KH:(t + 1) * KH, t * KO:(t + 1) * KO], a["L0_attn_Wphi2"][t]),
                       (ka_psi1[t * KI:(t + 1) * KI, t * KI:(t + 1) * KI], a["L0_attn_Wpsi1"][t]),
                       (ka_psi2[t * KI:(t + 1) * KI, t * KO:(t + 1) * KO], a["L0_attn_Wpsi2"][t])]

        block = ctx.enter_context(nc.Block())

        @block.sync
        def _(sp):
            def load_group(it, p):
                for j in range(GH):
                    head = it * GH + j
                    sp.dma_start(Q[p][32 * j:32 * j + ROWS, :].bitcast(F32), q_dram[head]).then_inc(sig("qk_loaded"), 16)
                    sp.dma_start(K[p][32 * j:32 * j + ROWS, j, :].bitcast(F32), k_dram[head]).then_inc(sig("qk_loaded"), 16)

            def load_expert(e, u):
                sp.dma_start(w_raw[u][:, 0:DM], a["L0_ffn_W1"][e]).then_inc(sig(f"w_loaded{u}"), 16)
                sp.dma_start(w_raw[u][:, DM:].rearrange("p (c d) -> p c d", d=C), a["L0_ffn_W2"][e].rearrange("(c p) d -> p c d", p=P)).then_inc(sig(f"w_loaded{u}"), 16)

            def load_next_experts(g, fi):
                sp.wait_ge(sig("w_split0"), fi + 1)
                load_expert((g * 2 + 2) % E, 0)
                sp.wait_ge(sig("w_split1"), fi + 2)
                load_expert((g * 2 + 3) % E, 1)

            def load_routes(g, fi, batches):
                sp.wait_ge(sig("route_stored"), batches * 16)
                sp.wait_ge(sig("moe_taken"), fi * 4 + 1)
                for u in range(2):
                    sp.dma_start(route_bc[u], row(route_dram[g * 2 + u], P)).then_inc(sig("route_loaded"), 16)

            def load_residual(b):
                sp.wait_ge(sig("h2_normed"), b * NT)
                sp.dma_start(xg[:, :, :], a["L0_attn_x"][b].rearrange("(t p) c -> p t c", p=P)).then_inc(sig("xg_loaded"), 16)

            def max_rows(count, p, half):
                sp.wait_ge(sig("max_moved"), count + 1)
                for part in range(2):
                    sp.dma_start(Q[p][PARTS + part:P:32, HALF * half:HALF * (half + 1)].rearrange(
                        "j (t n) -> j t n", n=P).bitcast(F32), mrows[16 * part:16 * part + 16, :]).then_inc(sig("max_rows"), 16)

            def store_heads(it, half):
                sp.wait_ge(sig("o_moved"), it * 2 + half + 2)
                for j in range(GH):
                    sp.dma_start(o_dram[it * GH + j, :, HALF * half:HALF * (half + 1)],
                                 oT[32 * j:32 * j + 2 * HD, half, :]).then_inc(sig(f"o_stored{half}"), 16)

            def main(it, p, ffn, g, fi, b=None):
                sp.wait_ge(sig("exps"), it * STEPS + CREDIT["exps"])
                load_group((it + 1) % NI, 1 - p)
                if ffn:
                    load_routes(g, fi, b)
                max_rows(it * 2 + 1, p, 1)
                if ffn:
                    load_next_experts(g, fi)
                store_heads(it, 0)
                max_rows(it * 2 + 2, 1 - p, 0)
                store_heads(it, 1)

            def post(b):
                sp.wait_ge(sig("logits"), b)
                sp.wait_ge(sig("o_stored0"), (b + 1) * NG * GH * 16 + 1)
                sp.wait_ge(sig("o_stored1"), (b + 1) * NG * GH * 16 + 1)
                o_b = o_dram[:, :, :].rearrange("(b h) r n -> b h r n", h=H)[b]
                sp.dma_start(oc[:, :], o_b[:, 0:HD, :]).then_inc(sig("o_loaded"), 16)
                sp.dma_start(den[:, :], o_b[:, HD:2 * HD, :]).then_inc(sig("o_loaded"), 16)
                sp.wait_ge(sig("route_rows"), b * 2 + 2)
                sp.dma_start(route_dram[:, :], routeT[:, :]).then_inc(sig("route_stored"), 16)

            def finish(b, n):
                sp.wait_ge(sig("y_ready"), 2 * n + 2)
                sp.dma_start(out[b].rearrange("(t p) c -> p t c", p=P), y[:, :, :]).then_inc(sig("stored"), 16)

            for dst, src in loads[:2]:
                sp.dma_start(dst, src).then_inc(sig("mod_loaded"), 16)
            for b in range(B):
                sp.dma_start(x_all[:, b * NT:(b + 1) * NT, :], a["L0_attn_x"][b].rearrange("(t p) c -> p t c", p=P)).then_inc(sig(f"x_loaded{b}"), 16)
            for dst, src in loads[2:]:
                sp.dma_start(dst, src).then_inc(sig("loaded"), 16)
            sp.wait_ge(sig("row_values"), 2)
            for dram, src in ((q_dram, accT[0:B * H, :]), (k_dram, y[0:B * H, :, :].rearrange("p t c -> p (t c)"))):
                for part in range(2):
                    sp.dma_start(dram[:, PARTS + part, :], src).then_inc(sig("rows_stored"), 16)
            sp.wait_ge(sig("blocks_zero"), 3)
            for dst, src in blocks:
                sp.dma_start(dst, src).then_inc(sig("blocks_loaded"), 16)
            load_expert(0, 0)
            load_expert(1, 1)

            with sp.Fori(0, B) as b:
                for r in range(2):
                    dram = (q_dram, k_dram)[r][:, :, :].rearrange("(b h) r n -> b h r n", h=H)[b]
                    sp.wait_ge(sig("lo_ready"), b * 4 + 3 + r + 1)
                    for part, src in enumerate(((qk_hi, qk_hi, qk_lo), (qk_hi, qk_lo, qk_hi))[r]):
                        sp.dma_start(dram[:, HD * part:HD * (part + 1), :], src[:, r, :].bitcast(F32)).then_inc(sig("qk_stored"), 16)

            sp.wait_ge(sig("means_ready"), 2)
            sp.dma_start(mean_dram[:, :, :].rearrange("r b c -> b r c"), qkm[:, :, :]).then_inc(sig("means_stored"), 16)
            sp.wait_ge(sig("means_stored"), 16)
            for r in range(2):
                sp.dma_start(qk[:, r * HD:(r + 1) * HD], mean_dram[r].rearrange("b (h d) -> (b h) d", d=HD)).then_inc(sig("qk_means"), 16)
            sp.wait_ge(sig("qk_stored"), B * 6 * 16 + 1)
            sp.wait_ge(sig("qk_zero"), 4)
            sp.wait_ge(sig("rows_stored"), 64)
            load_group(0, 0)
            sp.wait_ge(sig("fac_ready"), 1)
            sp.dma_start(fac_dram[:, :], fac[:, :]).then_inc(sig("fac_stored"), 16)
            sp.wait_ge(sig("fac_stored"), 16)
            for b in range(B):
                sp.dma_start(vfac[:, b:b + 1], fac_dram[b * H:(b + 1) * H, :].rearrange("h (d o) -> (h d) o", o=1)).then_inc(sig("fac_loaded"), 16)
            max_rows(0, 0, 0)
            load_residual(0)

            with sp.Fori(0, NG // 2) as gp:
                for p in range(2):
                    main(gp * 2 + p, p, False, None, None)
            post(0)
            with sp.Fori(1, B) as b:
                load_residual(b)
                with sp.Fori(0, NG // 2) as gp:
                    for p in range(2):
                        g = gp * 2 + p
                        main(b * NG + g, p, True, g, b * NG + g - NG, b)
                finish(b - 1, b - 1)
                post(b)
            with sp.Fori(0, NG) as g:
                load_routes(g, g + (NI - NG), B)
                load_next_experts(g, g + (NI - NG))
            finish(B - 1, B - 1)
            sp.wait_ge(sig("stored"), B * 16 + 1)
            sp.wait_ge(sig("w_loaded0"), 32 * (NI + 1))
            sp.wait_ge(sig("w_loaded1"), 32 * (NI + 1))
            sp.wait_ge(sig("qk_loaded"), 128 * (NI + 1))
            sp.wait_ge(sig("max_rows"), 32 * (2 * NI + 1))

        @block.tensor
        def _(pe):
            mm = nc.tensor.matmul

            def a_back(s, ffn):
                return 2 if ffn else A_BACK[s]

            def score_max(a_i, to, p):
                nt, mh, j = a_i // 8, a_i // 4 % 2, a_i % 4
                mm(bank(to), Q[p][:, P * nt:P * (nt + 1)], K[p][:, j, HALF * mh:HALF * (mh + 1)],
                   start=True, stop=True).then_inc(sig("max_scores"), 1)

            def move_max(count, n):
                pe.wait_ge(sig("max_parts"), count + 1)
                nc.tensor.transpose(ps[0:32, 7, 0:P], mparts[:, :, :].rearrange("p a b -> p (a b)").bitcast(F32), ident[:, :]).then_inc(sig("max_turned"), 1)

            def in_parts(to, w, w_other, x, x_other, start, stop):
                mm(to, w, x, start=start, stop=False)
                mm(to, w_other, x, start=False, stop=False)
                return mm(to, w, x_other, start=False, stop=stop)

            def expert_up(q, to, fi, depth=1):
                u, th, c = q // 8, q // 4 % 2, q % 4
                if q % 8 == 0:
                    pe.wait_ge(sig(f"w_split{u}"), fi + 1 + u)
                pe.wait_ge(sig("relus"), fi * UNITS + q + 2 - depth)
                w, tok = slice(P * c, P * (c + 1)), slice(HALF * th, HALF * (th + 1))
                in_parts(bank(to), w_hi[:, u, w], w_lo[:, u, w], t_hi[:, tok], t_lo[:, tok], True, True).then_inc(sig("w1_done"), 1)

            def expert_down(q, fi):
                u, th, c = q // 8, q // 4 % 2, q % 4
                pe.wait_ge(sig("mid_split"), fi * UNITS + q + 1)
                if c == 0:
                    pe.wait_ge(sig("moe_taken"), fi * 4 + q // 4 + 1)
                w = slice(DM + C * c, DM + C * (c + 1))
                in_parts(bank(6), w_hi[:, u, w], w_lo[:, u, w], mid_hi[:, q % 2, :], mid_lo[:, q % 2, :], c == 0, c == CH - 1).then_inc(sig("w2_done"), 1)

            def main(it, p, ffn, fi):
                def pv(v):
                    half, mt = v // NT, v % NT
                    pe.wait_ge(sig("exps"), it * STEPS + 4 * (v + 1) + CREDIT["exps"])
                    if v == 0:
                        pe.wait_ge(sig("v_staged"), it + 1)
                    if mt == 0:
                        pe.wait_ge(sig("o_moved"), it * 2 + half + 1)
                    for j in range(GH):
                        m = mm(ps[32 * j:32 * j + 32, 4, :], V[p][:, mt, j, :], probs[:, 4 * (mt % 2) + j, :],
                               start=(mt == 0), stop=(mt == NT - 1), tile_position=(0, 32 * j))
                    m.then_inc(sig("pv_done"), 1)

                for s in range(STEPS):
                    if s == LAG:
                        pe.wait_ge(sig("qk_loaded"), it * 128 + 256)
                    pe.wait_ge(sig("maxed"), it * STEPS + AHEAD + s + 1 - a_back(s, ffn))
                    score_max((s - LAG) % STEPS, a_bank(s, ffn), p if s < LAG else 1 - p)
                    half, mt, j = s // 32, s % 32 // 4, s % 4
                    if s % 32 == 0:
                        pe.wait_ge(sig("max_rows"), it * 64 + 32 * half + 32)
                    pe.wait_ge(sig("exps"), it * STEPS + s + 1 - B_BACK[s] + CREDIT["exps"])
                    if s == TURN[0] + 4:
                        pe.wait_ge(sig("max_moved"), it * 2 + 2)
                    if s == TURN[1] + 4:
                        pe.wait_ge(sig("max_moved"), it * 2 + 3)
                    mm(bank(b_bank(s)), K[p][:, j, P * mt:P * (mt + 1)], Q[p][:, HALF * half:HALF * (half + 1)],
                       start=True, stop=True).then_inc(sig("scores"), 1)
                    if ffn and s % 4 == 0:
                        expert_up(s // 4, 5, fi)
                    if s % 4 == 3 and s > 3:
                        pv(s // 4 - 1)
                    if ffn and s % 4 == 2 and s > 4:
                        expert_down(s // 4 - 1, fi)
                    if s in TURN:
                        last = max(i for i in range(s) if B_BANK[i] == 2)
                        pe.wait_ge(sig("exps"), it * STEPS + last + 1 + CREDIT["exps"])
                        move_max(it * 2 + 1 + TURN.index(s), None)
                if ffn:
                    expert_down(UNITS - 1, fi)
                pv(2 * NT - 1)

            def post(b):
                pe.wait_ge(sig("o_normed"), b + 1)
                for t in range(NT):
                    m = mm(ps[:, 4 + t // 4, P * (t % 4):P * (t % 4 + 1)], oc[:, P * t:P * (t + 1)], wproj_g[:, b, :], start=True, stop=True)
                    if t % 4 == 3:
                        m.then_inc(sig("proj_done"), 1)
                for t in range(NT):
                    pe.wait_ge(sig("h2_normed"), b * NT + t + 1)
                    m = nc.tensor.transpose(ps[:, 6 + t // 4, P * (t % 4):P * (t % 4 + 1)], xn[:, t, :], ident[:, :])
                    if t % 4 == 3:
                        m.then_inc(sig("h2_turned"), 1)
                for f in range(2):
                    pe.wait_ge(sig("h2_modded"), b * 2 + f + 1)
                    mm(bank(f), win[:, :], hT[:, HALF * f:HALF * (f + 1)], start=True, stop=True).then_inc(sig("win_done"), 1)
                pe.wait_ge(sig("t_ready"), b * 2 + 2)
                for t in range(NT):
                    m = mm(ps[:, 2, E * t:E * (t + 1)], t_raw[:, P * t:P * (t + 1)], wgate[:, :], start=True, stop=True)
                m.then_inc(sig("logits"), 1)
                pe.wait_ge(sig("routed"), b + 1)
                for t in range(NT):
                    m = nc.tensor.transpose(ps[0:E, 4 + t // 4, P * (t % 4):P * (t % 4 + 1)], route[:, t, :], ident[:, :])
                m.then_inc(sig("route_turned"), 1)
                pe.wait_ge(sig("route_rows"), b * 2 + 2)
                for f in range(2):
                    m = mm(bank(6 + f), b2[:, :], routeT[:, HALF * f:HALF * (f + 1)], start=True, stop=True)
                m.then_inc(sig("b2_mixed"), 1)
                pe.wait_ge(sig("moe_started"), b * 2 + 2)
                pe.wait_ge(sig("t_split"), b * 2 + 2)

            def finish(b):
                pe.wait_ge(sig("moe_added"), b * 16 + 16 + CREDIT["moe_added"])
                for t in range(NT):
                    m = mm(ps[:, 5 + t // 4, P * (t % 4):P * (t % 4 + 1)], accT[:, P * t:P * (t + 1)], wout_g[:, b, :], start=True, stop=True)
                    if t % 4 == 3:
                        m.then_inc(sig("wout_done"), 1)
                pe.wait_ge(sig("y_ready"), b * 2 + 2)

            pe.wait_ge(sig("ident"), 2)
            pe.wait_ge(sig("mod_loaded"), 32)
            nc.tensor.transpose(ps[:, 0, 0:B], cmod[:, :], ident[0:B, 0:B]).then_inc(sig("c_turned"), 1)
            pe.wait_ge(sig("silu_ready"), 2)
            for i, chunk in enumerate((0, 1, 3, 4)):
                m = mm(ps[:, 1, B * i:B * (i + 1)], wmod[:, chunk * C:(chunk + 1) * C], siluT[:, :], start=True, stop=True)
            for i, chunk in enumerate((2, 5)):
                for b in range(B):
                    m = mm(ps[:, 2 + i, C * b:C * (b + 1)], silu_bc[:, b, :], wmod[:, chunk * C:(chunk + 1) * C], start=True, stop=True)
            m.then_inc(sig("mod_done"), 1)
            pe.wait_ge(sig("loaded"), 16 * len(loads[2:]))
            nc.tensor.transpose(ps[:, 4, 0:E * CH], b1rows[:, :], ident[0:E * CH, 0:E * CH]).then_inc(sig("b1_turned"), 1)
            pe.wait_ge(sig("b1_ready"), 1)

            with pe.Fori(0, B) as b:
                for t in range(NT):
                    pe.wait_ge(sig("x_normed"), b * NT + t + 1)
                    m = nc.tensor.transpose(ps[:, t // 4, P * (t % 4):P * (t % 4 + 1)], xn[:, t, :], ident[:, :])
                    if t % 4 == 3:
                        m.then_inc(sig("x_turned"), 1)
                pe.wait_ge(sig("lo_ready"), b * 4 + 1)
                pe.wait_ge(sig("v_kept"), b * 2 + 1)
                for f in range(2):
                    pe.wait_ge(sig("h_ready"), b * 2 + f + 1)
                    for r in range(2):
                        mm(bank(2 + 2 * r + f), wqkv[:, C * r:C * (r + 1)], hT[:, HALF * f:HALF * (f + 1)], start=True, stop=True).then_inc(sig("qk_done"), 1)
                for t in range(NT):
                    m = mm(ps[:, 6 + t // 4, P * (t % 4):P * (t % 4 + 1)], hT[:, P * t:P * (t + 1)], wqkv[:, 2 * C:3 * C], start=True, stop=True)
                    if t % 4 == 3:
                        m.then_inc(sig("v_done"), 1)

            pe.wait_ge(sig("hmean_ready"), 1)
            pe.wait_ge(sig("h_ready"), 2 * B)
            for r in range(2):
                m = mm(ps[0:B, 0, C * r:C * (r + 1)], hmean[:, :], wqkv[:, C * r:C * (r + 1)], start=True, stop=True)
            m.then_inc(sig("means_done"), 1)
            pe.wait_ge(sig("qk_means"), 32)
            pe.wait_ge(sig("means_ready"), 2)
            nc.tensor.transpose(ps[0:KI, 1, 0:MB], qk[:, :], ident[0:MB, 0:MB]).then_inc(sig("ka_pe"), 1)
            pe.wait_ge(sig("ka_sb"), 1)
            mm(ps[0:T * KI, 0, 0:MB], ka_a[:, :, :].rearrange("d t e -> d (t e)"), qkT[:, :], start=True, stop=True).then_inc(sig("ka_pe"), 1)
            pe.wait_ge(sig("lo_ready"), 4 * B + 1)
            mm(ps[0:T * KH, 2, 0:MB], ka_phi1[:, :, :].rearrange("d t e -> d (t e)"), qkT[:, :], start=True, stop=True).then_inc(sig("ka_pe"), 1)
            pe.wait_ge(sig("blocks_loaded"), 16 * len(blocks))
            pe.wait_ge(sig("ka_sb"), 2)
            mm(ps[0:MB, 3, 0:T * KI], axT[:, :], ka_psi1[:, :], start=True, stop=True).then_inc(sig("ka_pe"), 1)
            pe.wait_ge(sig("ka_phi"), 1)
            mm(ps[0:MB, 4, 0:HD], phiT[:, :], ka_phi2[:, :], start=True, stop=True).then_inc(sig("ka_pe"), 1)
            pe.wait_ge(sig("ka_gelu"), 1)
            nc.tensor.transpose(ps[0:T * KI, 5, 0:MB], psi[:, :, :].rearrange("m t g -> m (t g)"), ident[0:MB, 0:MB]).then_inc(sig("ka_pe"), 1)
            pe.wait_ge(sig("v_kept"), 2 * B + 1)
            pe.wait_ge(sig("ka_sb"), 3)
            mm(ps[0:MB, 6, 0:HD], psiT[:, :], ka_psi2[:, :], start=True, stop=True).then_inc(sig("ka_pe"), 1)
            pe.wait_ge(sig("fac_ready"), 1)

            pe.wait_ge(sig("qk_loaded"), 128)
            for a_i in range(AHEAD):
                if a_i >= A_BACK[a_i + LAG]:
                    pe.wait_ge(sig("maxed"), a_i + 1 - A_BACK[a_i + LAG])
                score_max(a_i, a_bank(a_i + LAG, False), 0)
            move_max(0, None)

            with pe.Fori(0, NG // 2) as gp:
                for p in range(2):
                    main(gp * 2 + p, p, False, None)
            post(0)
            with pe.Fori(1, B) as b:
                with pe.Fori(0, NG // 2) as gp:
                    for p in range(2):
                        main(b * NG + gp * 2 + p, p, True, b * NG + gp * 2 + p - NG)
                finish(b - 1)
                post(b)
            with pe.Fori(0, NG) as g:
                fi = g + (NI - NG)
                for q in range(UNITS):
                    expert_up(q, (0, 1, 5, 7)[q % 4], fi, 4 if q >= 3 else 1)
                    if q >= 2:
                        expert_down(q - 2, fi)
                for q in range(UNITS - 2, UNITS):
                    expert_down(q, fi)
            finish(B - 1)

        @block.scalar
        def _(act):
            act_fn = nc.scalar.activation

            def relu(q, at, pf, fi):
                u, c = q // 8, q % 4
                if q == 0:
                    act.wait_ge(sig("ffn_staged"), fi + 1)
                act.wait_ge(sig("w1_done"), fi * UNITS + q + 1)
                act.wait_ge(sig("w2_done"), fi * UNITS + q + 1)
                for dst in (mid_hi, mid):
                    m = act_fn(dst[:, q % 2, :], bank(at), ACT.Relu, bias=b1s[pf][:, u, c:c + 1])
                m.then_inc(sig("relus"), 1)

            def main(it, p, ffn, fi):
                for s in range(STEPS):
                    if s % 4 == 0:
                        act.wait_ge(sig("pv_done"), it * 16 + s // 4 + 1)
                    act.wait_ge(sig("scores"), it * STEPS + s + 1)
                    act_fn(probs[:, s % 8, :], bank(b_bank(s)), ACT.Exp).then_inc(sig("exps"), 1)
                    if ffn and s % 4 == 0:
                        relu(s // 4, 5, p, fi)

            def post(b):
                act.wait_ge(sig("var2"), b * NT + NT)
                act_fn(sd2[:, :], mv2[:, :, 1], ACT.Sqrt, bias=eps_col[:, 0:1]).then_inc(sig("std2"), 1)
                act.wait_ge(sig("h2_turned"), b * 2 + 2)
                for f in range(2):
                    act_fn(hT[:, HALF * f:HALF * (f + 1)], bank(6 + f), ACT.Identity, scale=mod_col[:, 3, bass.ds(b, 1)], bias=mod_col[:, 2, bass.ds(b, 1)]).then_inc(sig("h2_modded"), 1)
                for f in range(2):
                    act.wait_ge(sig("win_done"), b * 2 + f + 1)
                    act_fn(t_raw[:, HALF * f:HALF * (f + 1)], bank(f), ACT.Identity, bias=bin_col[:, 0:1]).then_inc(sig("t_ready"), 1)
                for f in range(2):
                    act_fn(t_hi[:, HALF * f:HALF * (f + 1)], bank(f), ACT.Identity, bias=bin_col[:, 0:1]).then_inc(sig("t_hi_ready"), 1)
                act.wait_ge(sig("logits_shifted"), b + 1)
                act_fn(pr[:, :, :], lg[:, :, :], ACT.Exp).then_inc(sig("logit_exps"), 1)
                act.wait_ge(sig("route_turned"), b + 1)
                act.wait_ge(sig("route_stored"), b * 16)
                for f in range(2):
                    act_fn(routeT[:, HALF * f:HALF * (f + 1)], ps[0:E, 4 + f, :], ACT.Copy).then_inc(sig("route_rows"), 1)
                act.wait_ge(sig("b2_mixed"), b + 1)
                for f in range(2):
                    act_fn(accT[:, HALF * f:HALF * (f + 1)], bank(6 + f), ACT.Copy).then_inc(sig("moe_started"), 1)

            act.wait_ge(sig("c_turned"), 1)
            act_fn(siluT[:, :], ps[:, 0, 0:B], ACT.Silu).then_inc(sig("silu_ready"), 1)
            act.wait_ge(sig("eps_set"), 1)
            act.wait_ge(sig("var1"), B * NT)
            act_fn(std[:, :], mv[:, :, 1], ACT.Sqrt, bias=eps_col[:, 0:1]).then_inc(sig("std1"), 1)
            act.wait_ge(sig("b1_ready"), 1)

            with act.Fori(0, B) as b:
                for f in range(2):
                    act.wait_ge(sig("x_turned"), b * 2 + f + 2)
                    act_fn(hT[:, HALF * f:HALF * (f + 1)], bank(f), ACT.Identity, scale=mod_col[:, 1, bass.ds(b, 1)], bias=mod_col[:, 0, bass.ds(b, 1)],
                           accum_out=hsum[:, bass.ds(b * 2 + f, 1)]).then_inc(sig("h_ready"), 1)
                act.wait_ge(sig("qk_stored"), b * 96 + 1)
                for f in range(2):
                    for r in range(2):
                        act.wait_ge(sig("qk_done"), b * 4 + 2 * f + r + 1)
                        act_fn(qk_hi[:, r, HALF * f:HALF * (f + 1)], bank(2 + 2 * r + f), ACT.Identity, scale=qk_scale[:, r:r + 1]).then_inc(sig("hi_ready"), 1)
                for f in range(2):
                    act.wait_ge(sig("v_done"), b * 2 + f + 1)
                    act_fn(v_all[:, bass.ds(b * NG, NG), 4 * f:4 * f + 4, :].rearrange("p g t c -> p t g c"), bank(6 + f).rearrange("p (t g c) -> p t g c", t=4, g=NG), ACT.Copy).then_inc(sig("v_kept"), 1)

            act.wait_ge(sig("means_done"), 1)
            for r in range(2):
                act_fn(qkm[:, r, :], ps[0:B, 0, C * r:C * (r + 1)], ACT.Copy).then_inc(sig("means_ready"), 1)
            act.wait_ge(sig("ka_pe"), 3)
            act_fn(phiT[:, :], ps[0:T * KH, 2, 0:MB], ACT.Silu, bias=ka_bphi1[:, 0:1]).then_inc(sig("ka_phi"), 1)
            act.wait_ge(sig("ka_var"), 1)
            act_fn(pst[:, :], psv[:, :], ACT.Sqrt, bias=eps_col[0:MB, 0:1], scale=1.0 / KI).then_inc(sig("ka_std"), 1)
            act.wait_ge(sig("ka_psi"), 1)
            act_fn(psi[:, :, :], psq[:, :, :], ACT.Gelu).then_inc(sig("ka_gelu"), 1)

            with act.Fori(0, NG // 2) as gp:
                for p in range(2):
                    main(gp * 2 + p, p, False, None)
            post(0)
            with act.Fori(1, B) as b:
                with act.Fori(0, NG // 2) as gp:
                    for p in range(2):
                        main(b * NG + gp * 2 + p, p, True, b * NG + gp * 2 + p - NG)
                post(b)
            with act.Fori(0, NG // 2) as gp:
                for p in range(2):
                    for q in range(UNITS):
                        relu(q, (0, 1, 5, 7)[q % 4], p, gp * 2 + p + (NI - NG))

        @block.vector
        def _(dve):
            ch = Chain(dve, sig("dve_steps"))
            tt, tsc, stt = nc.vector.tensor_tensor, nc.vector.tensor_scalar, nc.vector.scalar_tensor_tensor
            red = nc.vector.tensor_reduce

            def take_max(a_i, at, count):
                nt, mh, j = a_i // 8, a_i // 4 % 2, a_i % 4
                dve.wait_ge(sig("max_scores"), count + 1)
                red(mxp[:, nt, mh, j:j + 1], bank(at), X, ALU.max).then_inc(sig("maxed"), 1)

            def split_max(half, done, p, k, staged):
                dve.wait_ge(sig("maxed"), done)
                if k is not None:
                    dve.wait_ge(sig("max_turned"), k)
                dve.wait_ge(sig("beta_staged"), staged)
                m4 = mx[:, :].rearrange("p (j t) -> p j t", j=GH)
                ch.link(tt(m4, mxp[:, 4 * half:4 * half + 4, 0, :].rearrange("p t j -> p j t"),
                           mxp[:, 4 * half:4 * half + 4, 1, :].rearrange("p t j -> p j t"), ALU.max))
                bg = beta_g[p][:, :].unsqueeze(2).broadcast_to([P, GH, 4])
                ch.link(tt(mxb[:, :].rearrange("p (j t) -> p j t", j=GH), m4, bg, ALU.add))
                ch.link(tt(mrow[:, :].rearrange("p (j t) -> p j t", j=GH), bg, mxb[:, :].rearrange("p (j t) -> p j t", j=GH), ALU.subtract))
                ch.link(nc.vector.tensor_copy(mparts[:, 0, :], mrow[:, :]))
                tt(mparts[:, 1, :], mrow[:, :], mparts[:, 0, :].bitcast(F32), ALU.subtract).then_inc(sig("max_parts"), 1)

            def move_max(count, stored):
                dve.wait_ge(sig("max_turned"), count + 1)
                if stored is not None:
                    dve.wait_ge(sig("max_rows"), stored)
                nc.vector.tensor_copy(mrows[:, :], ps[0:32, 7, 0:P]).then_inc(sig("max_moved"), 1)

            def weigh(k, fi):
                u, th = k // 2, k % 2
                dve.wait_ge(sig("w2_done"), fi * UNITS + 4 * k + 6)
                dve.wait_ge(sig("route_loaded"), fi * 32 + 32)
                dve.wait_ge(sig("moe_added"), fi * 4 + k + 1)
                tt(weighted[:, k % 2, :], bank(6), route_bc[u][:, HALF * th:HALF * (th + 1)], ALU.mult).then_inc(sig("moe_taken"), 1)

            def main(it, p, ffn, fi, b):
                def o_move(half):
                    dve.wait_ge(sig("pv_done"), it * 16 + 8 * half + 10)
                    dve.wait_ge(sig(f"o_stored{half}"), it * 64 + 1)
                    nc.vector.tensor_copy(oT[:, half, :], bank(4)).then_inc(sig("o_moved"), 1)

                for s in range(STEPS):
                    take_max((s - LAG) % STEPS, a_bank(s, ffn), it * STEPS + AHEAD + s)
                    if s == LAG - 1:
                        split_max(1, it * STEPS + AHEAD + s + 1, p, it * 2 + 1, it + 1)
                    if s == LAG + 31:
                        split_max(0, it * STEPS + AHEAD + s + 1, 1 - p, it * 2 + 2, it + 2)
                    if s == 22:
                        move_max(it * 2 + 1, it * 64 + 32)
                    if s == 54:
                        move_max(it * 2 + 2, it * 64 + 64)
                    if s == 37:
                        o_move(0)
                    if ffn and s % 16 == 3 and s > 16:
                        weigh(s // 16 - 1, fi)
                if ffn:
                    weigh(3, fi)
                o_move(1)

            def post(b):
                dve.wait_ge(sig("o_loaded"), b * 32 + 32)
                ch.link(nc.vector.reciprocal(den[:, :], den[:, :]))
                dve.wait_ge(sig("fac_loaded"), 16 * B)
                stt(oc[:, :], oc[:, :], vfac[:, bass.ds(b, 1)], den[:, :], ALU.mult, ALU.mult).then_inc(sig("o_normed"), 1)
                dve.wait_ge(sig("xg_ready"), b + 1)
                dve.wait_ge(sig("y_ready"), b * 2)
                for f in range(2):
                    dve.wait_ge(sig("proj_done"), b * 2 + f + 1)
                    ch.did(tt(x1[:, 4 * f:4 * f + 4, :], tiles(4 + f), xg[:, 4 * f:4 * f + 4, :], ALU.add))
                ch.wait()
                for t in range(NT):
                    ch.did(nc.vector.bn_stats(st2[:, t, :], x1[:, t, :]))
                ch.wait()
                nc.vector.memset(credit[:, len(CREDIT):], 0.0)
                for t in range(NT):
                    nc.vector.bn_aggr(mv2[:, t, :], st2[:, t, :]).then_inc(sig("var2"), 1)
                dve.wait_ge(sig("var2"), b * NT + NT)
                dve.wait_ge(sig("std2"), b + 1)
                ch.link(nc.vector.reciprocal(sd2[:, :], sd2[:, :]))
                dve.wait_ge(sig("h2_turned"), b * 2)
                for t in range(NT):
                    tsc(xn[:, t, :], x1[:, t, :], mv2[:, t, 0:1], sd2[:, t:t + 1], ALU.subtract, ALU.mult).then_inc(sig("h2_normed"), 1)
                for f in range(2):
                    dve.wait_ge(sig("t_hi_ready"), b * 2 + f + 1)
                    tt(t_lo[:, HALF * f:HALF * (f + 1)], t_raw[:, HALF * f:HALF * (f + 1)], t_hi[:, HALF * f:HALF * (f + 1)].bitcast(F32), ALU.subtract).then_inc(sig("t_split"), 1)
                dve.wait_ge(sig("logits"), b + 1)
                ch.link(tt(lg[:, :, :], ps[:, 2, 0:NT * E].rearrange("p (t e) -> p t e", e=E), over_tiles(bgate_bc), ALU.add))
                ch.link(red(gm[:, :], lg[:, :, :], X, ALU.max))
                tt(lg[:, :, :], lg[:, :, :], over_experts(gm), ALU.subtract).then_inc(sig("logits_shifted"), 1)
                dve.wait_ge(sig("logit_exps"), b + 1)
                ch.link(red(gm[:, :], pr[:, :, :], X, ALU.add))
                ch.link(nc.vector.reciprocal(gm[:, :], gm[:, :]))
                ch.link(tt(pr[:, :, :], pr[:, :, :], over_experts(gm), ALU.mult))
                for src, pick in ((pr, g1), (g0, g2)):
                    ch.link(red(gm[:, :], src[:, :, :], X, ALU.max))
                    ch.link(tt(pick[:, :, :], src[:, :, :], over_experts(gm), ALU.is_ge))
                    ch.link(tt(pick[:, :, :], pick[:, :, :], over_tiles(rev), ALU.mult))
                    ch.link(red(gm[:, :], pick[:, :, :], X, ALU.max))
                    ch.link(tt(pick[:, :, :], pick[:, :, :], over_experts(gm), ALU.is_equal))
                    if pick is g1:
                        ch.link(stt(g0[:, :, :], g1[:, :, :], -2.0, pr[:, :, :], ALU.mult, ALU.add))
                ch.link(tt(g1[:, :, :], g1[:, :, :], g2[:, :, :], ALU.add))
                ch.link(tt(pr[:, :, :], pr[:, :, :], g1[:, :, :], ALU.mult))
                ch.link(red(gm[:, :], pr[:, :, :], X, ALU.add))
                ch.link(nc.vector.reciprocal(gm[:, :], gm[:, :]))
                dve.wait_ge(sig("route_turned"), b)
                tt(route[:, :, :], pr[:, :, :], over_experts(gm), ALU.mult).then_inc(sig("routed"), 1)

            POST = 1 + 2 + NT + 1 + 2 + 3 + 11 + 4

            def finish(b):
                dve.wait_ge(sig("stored"), b * 16 + 1)
                dve.wait_ge(sig("x1b_ready"), b + 1)
                for f in range(2):
                    dve.wait_ge(sig("wout_done"), b * 2 + f + 2)
                    tt(y[:, 4 * f:4 * f + 4, :], tiles(5 + f), x1[:, 4 * f:4 * f + 4, :], ALU.add).then_inc(sig("y_ready"), 1)

            nc.vector.memset(eps_col[:, :], EPS).then_inc(sig("eps_set"), 1)
            for i in range(E):
                nc.vector.memset(rev[:, i:i + 1], float(E - i)).then_inc(sig("rev_set"), 1)
            dve.wait_ge(sig("rev_set"), E)
            ch.did(nc.vector.memset(qk_scale[:, 1:2], 1.0))
            nc.vector.memset(accT[:, :], 0.0).then_inc(sig("row_values"), 1)
            nc.vector.memset(y[:, :, :], 1.0).then_inc(sig("row_values"), 1)
            for i, (name, n) in enumerate(CREDIT.items()):
                nc.vector.memset(credit[:, i:i + 1], 0.0).then_inc(sig(name), n)
            for i in range(2):
                nc.vector.memset(K[i][:, :, :].bitcast(F32), 0.0).then_inc(sig("qk_zero"), 1)
                nc.vector.memset(Q[i][:, :].bitcast(F32), 0.0).then_inc(sig("qk_zero"), 1)
                nc.vector.memset(V[i][:, :, :, :], 1.0).then_inc(sig("v_ones"), 1)
            dve.wait_ge(sig("silu_ready"), 1)
            for b in range(B):
                m = nc.vector.tensor_copy(silu_bc[:, b, :], siluT[:, b:b + 1].broadcast_to([P, P]))
            m.then_inc(sig("silu_ready"), 1)
            for t in range(B * NT):
                if t % NT == 0:
                    dve.wait_ge(sig(f"x_loaded{t // NT}"), 16)
                ch.did(nc.vector.bn_stats(stats[:, t, :], x_all[:, t, :]))
            ch.wait()
            for t in range(B * NT):
                nc.vector.bn_aggr(mv[:, t, :], stats[:, t, :]).then_inc(sig("var1"), 1)
            dve.wait_ge(sig("mod_done"), 1)
            ch.did(nc.vector.tensor_copy(mod_col[:, 0, :], ps[:, 1, 0:B]))
            ch.did(tsc(mod_col[:, 1, :], ps[:, 1, B:2 * B], 1.0, None, ALU.add))
            ch.did(nc.vector.tensor_copy(mod_col[:, 2, :], ps[:, 1, 2 * B:3 * B]))
            ch.did(tsc(mod_col[:, 3, :], ps[:, 1, 3 * B:4 * B], 1.0, None, ALU.add))
            ch.link(nc.vector.tensor_copy(gate_bc[:, :, :], ps[:, 2:4, :]))
            ch.link(tsc(gt0[:, :, :], gate_bc[:, :, :], 0.0, 2.0, ALU.is_ge, ALU.mult))
            ch.link(stt(gt1[:, :, :], gate_bc[:, :, :], -1.0, gate_bc[:, :, :], ALU.mult, ALU.max))
            ch.link(tsc(gt1[:, :, :], gt1[:, :, :], 0.25, None, ALU.max))
            ch.link(stt(gate_bc[:, :, :], gt0[:, :, :], -1.0, gt1[:, :, :], ALU.add, ALU.mult))
            dve.wait_ge(sig("loaded"), 16 * len(loads[2:]))
            for b in range(B):
                g_a, g_b = gate_bc[:, 0, C * b:C * (b + 1)], gate_bc[:, 1, C * b:C * (b + 1)]
                ch.did(tt(wproj_g[:, b, :], wproj[:, :], g_a, ALU.mult))
                ch.did(tt(wout_g[:, b, :], wout[:, :], g_b, ALU.mult))
                ch.did(tt(bproj_g[:, b, :], bproj_bc[:, :], g_a, ALU.mult))
                ch.did(tt(bout_g[:, b, :], bout_bc[:, :], g_b, ALU.mult))
            ch.did(tsc(qk_scale[:, 0:1], alpha_col[:, :], ATTN_SCALE, None, ALU.mult))
            ch.wait()
            dve.wait_ge(sig("std1"), 1)
            dve.wait_ge(sig("var1"), B * NT)
            ch.link(nc.vector.reciprocal(rstd[:, :], std[:, :]))
            dve.wait_ge(sig("b1_turned"), 1)
            nc.vector.tensor_copy(b1T[:, :], ps[:, 4, 0:E * CH]).then_inc(sig("b1_ready"), 1)

            with dve.Fori(0, B) as b:
                dve.wait_ge(sig("x_turned"), b * 2 + 1)
                for t in range(NT):
                    i = b * NT + t
                    tsc(xn[:, t, :], x_all[:, i, :], mv[:, bass.ds(i, 1), 0], rstd[:, bass.ds(i, 1)], ALU.subtract, ALU.mult).then_inc(sig("x_normed"), 1)
                dve.wait_ge(sig("qk_stored"), b * 96 + 1)
                for f in range(2):
                    for r in range(2):
                        dve.wait_ge(sig("hi_ready"), b * 4 + 2 * f + r + 1)
                        stt(qk_lo[:, r, HALF * f:HALF * (f + 1)], bank(2 + 2 * r + f), qk_scale[:, r:r + 1],
                            qk_hi[:, r, HALF * f:HALF * (f + 1)].bitcast(F32), ALU.mult, ALU.subtract).then_inc(sig("lo_ready"), 1)

            dve.wait_ge(sig("h_ready"), 2 * B)
            hs = hsum[:, :].rearrange("p (b f) -> p b f", f=2)
            ch.link(red(hmean[:, :], hs, X, ALU.add))
            tsc(hmean[:, :], hmean[:, :], 1.0 / N, None, ALU.mult).then_inc(sig("hmean_ready"), 1)
            dve.wait_ge(sig("ka_pe"), 1)
            nc.vector.tensor_copy(qkT[:, :], ps[0:KI, 1, 0:MB]).then_inc(sig("ka_sb"), 1)
            dve.wait_ge(sig("ka_pe"), 2)
            nc.vector.tensor_copy(axT[:, :], ps[0:T * KI, 0, 0:MB]).then_inc(sig("ka_sb"), 1)
            dve.wait_ge(sig("ka_pe"), 4)
            grp = lambda t: t[:, :].rearrange("m (t g) -> m t g", g=KI)
            wide = lambda t: t[:, :].unsqueeze(2).broadcast_to([MB, T, KI])
            ch.link(tt(psi[:, :, :], ps[0:MB, 3, 0:T * KI].rearrange("m (t g) -> m t g", g=KI), grp(bpsi1_bc), ALU.add))
            ch.link(red(psm[:, :], psi[:, :, :], X, ALU.add))
            ch.link(tsc(psm[:, :], psm[:, :], 1.0 / KI, None, ALU.mult))
            ch.link(tt(psi[:, :, :], psi[:, :, :], wide(psm), ALU.subtract))
            ch.link(tt(psq[:, :, :], psi[:, :, :], psi[:, :, :], ALU.mult))
            red(psv[:, :], psq[:, :, :], X, ALU.add).then_inc(sig("ka_var"), 1)
            dve.wait_ge(sig("ka_std"), 1)
            ch.link(nc.vector.reciprocal(pst[:, :], pst[:, :]))
            ch.link(tt(psq[:, :, :], psi[:, :, :], wide(pst), ALU.mult))
            ch.link(tt(psq[:, :, :], psq[:, :, :], grp(lng_bc), ALU.mult))
            tt(psq[:, :, :], psq[:, :, :], grp(lnb_bc), ALU.add).then_inc(sig("ka_psi"), 1)
            dve.wait_ge(sig("ka_pe"), 5)
            ch.link(tt(phi[:, :], ps[0:MB, 4, 0:HD], bphi2_bc[:, :], ALU.add))
            dve.wait_ge(sig("ka_pe"), 6)
            nc.vector.tensor_copy(psiT[:, :], ps[0:T * KI, 5, 0:MB]).then_inc(sig("ka_sb"), 1)
            dve.wait_ge(sig("ka_pe"), 7)
            ch.link(tt(psi_o[:, :], ps[0:MB, 6, 0:HD], bpsi2_bc[:, :], ALU.add))
            ch.link(tt(phi[:, :], phi[:, :], psi_o[:, :], ALU.mult))
            ch.link(tsc(phi[:, :], phi[:, :], temp_bc[:, 0:1], None, ALU.mult))
            ch.link(tt(fac[:, :].rearrange("m (t o) -> m t o", o=KO), phi[:, :].rearrange("m (t o) -> m t o", o=KO), mix_bc[:, :].unsqueeze(2).broadcast_to([MB, T, KO]), ALU.mult))
            tsc(fac[:, :], fac[:, :], 1.0, gamma_col[:, 0:1], ALU.add, ALU.mult).then_inc(sig("fac_ready"), 1)

            for a_i in range(AHEAD):
                take_max(a_i, a_bank(a_i + LAG, False), a_i)
                if a_i == 31:
                    split_max(0, a_i + 1, 0, None, 1)
            move_max(0, None)

            PER = 2 * 4
            with dve.Fori(0, NG // 2) as gp:
                ch.enter(gp, 2 * PER)
                for p in range(2):
                    main(gp * 2 + p, p, False, None, 0)
                ch.leave(NG // 2)
            post(0)
            with dve.Fori(1, B) as b:
                ch.enter(b - 1, NG * PER + POST)
                with dve.Fori(0, NG // 2) as gp:
                    inner = Chain(dve, ch.sem)
                    inner.base, inner.n = ch.base + gp * (2 * PER), 0
                    keep, ch = ch, inner
                    for p in range(2):
                        main(b * NG + gp * 2 + p, p, True, b * NG + gp * 2 + p - NG, b)
                    assert inner.n == 2 * PER
                    ch = keep
                ch.n += NG * PER
                finish(b - 1)
                post(b)
                ch.leave(B - 1)
            with dve.Fori(0, NG // 2) as gp:
                for p in range(2):
                    fi = gp * 2 + p + (NI - NG)
                    for q in range(UNITS):
                        dve.wait_ge(sig("relus"), fi * UNITS + q + 2)
                        tt(mid_lo[:, q % 2, :], mid[:, q % 2, :], mid_hi[:, q % 2, :].bitcast(F32), ALU.subtract).then_inc(sig("mid_split"), 1)
                        if q % 4 == 1 and q > 1:
                            weigh(q // 4 - 1, fi)
                    weigh(3, fi)
            finish(B - 1)

        @block.gpsimd
        def _(pool):
            ch = Chain(pool, sig("pool_steps"))

            def stage(group, p):
                for j in range(GH):
                    m = nc.gpsimd.tensor_copy(V[p][:, :, j, 0:HD], v_all[:, group, :, HD * j:HD * (j + 1)])
                m.then_inc(sig("v_staged"), 1)
                nc.gpsimd.tensor_copy(beta_g[p][:, :], beta_bc[:, bass.ds(group * GH, GH)]).then_inc(sig("beta_staged"), 1)

            def stage_biases(p, g):
                nc.gpsimd.tensor_copy(b1s[p][:, :, :].rearrange("p u c -> p (u c)"), b1T[:, bass.ds(g * 2 * CH, 2 * CH)]).then_inc(sig("ffn_staged"), 1)

            PIECES = 4
            sub = nc.gpsimd.tensor_tensor

            def split_weights(u, piece, loaded, free):
                if piece == 0:
                    pool.wait_ge(sig(f"w_loaded{u}"), loaded)
                    if free is not None:
                        pool.wait_ge(sig("w2_done"), free)
                        sub(pool_wait[:, :], ident[:, 0:1], ident[:, 0:1], ALU.mult)
                size = (DM + CH * C) // PIECES
                part = slice(piece * size, (piece + 1) * size)
                ch.link(nc.gpsimd.tensor_copy(w_hi[:, u, part], w_raw[u][:, part]))
                m = sub(w_lo[:, u, part], w_raw[u][:, part], w_hi[:, u, part].bitcast(F32), ALU.subtract)
                if piece == PIECES - 1:
                    m.then_inc(sig(f"w_split{u}"), 1)

            def add_weighted(k, fi, batches):
                pool.wait_ge(sig("moe_taken"), fi * 4 + k + 2)
                if k == 0:
                    pool.wait_ge(sig("moe_started"), batches * 2)
                th = slice(HALF * (k % 2), HALF * (k % 2 + 1))
                pool.wait_ge(sig("moe_added"), fi * 4 + k + CREDIT["moe_added"])
                sub(accT[:, th], accT[:, th], weighted[:, k % 2, :], ALU.add).then_inc(sig("moe_added"), 1)

            def ffn_steps(fi, batches, split):
                for q in range(UNITS):
                    if split:
                        pool.wait_ge(sig("relus"), fi * UNITS + q + 2)
                        sub(mid_lo[:, q % 2, :], mid[:, q % 2, :], mid_hi[:, q % 2, :].bitcast(F32), ALU.subtract).then_inc(sig("mid_split"), 1)
                    if q < PIECES:
                        split_weights(1, q, fi * 32 + 32, fi * UNITS + 2)
                    if 10 <= q < 10 + PIECES:
                        split_weights(0, q - 10, fi * 32 + 64, fi * UNITS + 10)
                    if q % 4 == 1 and q > 1:
                        add_weighted(q // 4 - 1, fi, batches)
                add_weighted(3, fi, batches)

            def main(it, p, ffn, b, g):
                if ffn:
                    pool.wait_ge(sig("exps"), it * STEPS - STEPS + CREDIT["exps"])
                    stage_biases(p, g)
                pool.wait_ge(sig("pv_done"), it * 16 + 2)
                pool.wait_ge(sig("maxed"), it * STEPS + AHEAD)
                stage((it + 1) % NI, 1 - p)
                if ffn:
                    ffn_steps(it - NG, b, True)

            def residual(b):
                pool.wait_ge(sig("xg_loaded"), b * 16 + 16)
                for t in range(NT):
                    m = nc.gpsimd.tensor_tensor(xg[:, t, :], xg[:, t, :], bproj_g[:, b, :], ALU.add)
                m.then_inc(sig("xg_ready"), 1)

            def residual2(b):
                pool.wait_ge(sig("h2_normed"), b * NT + NT)
                for t in range(NT):
                    m = nc.gpsimd.tensor_tensor(x1[:, t, :], x1[:, t, :], bout_g[:, b, :], ALU.add)
                m.then_inc(sig("x1b_ready"), 1)

            nc.gpsimd.memset(ident[:, :], 0.0).then_inc(sig("ident"), 1)
            for w in (ka_phi2, ka_psi1, ka_psi2):
                nc.gpsimd.memset(w[:, :], 0.0).then_inc(sig("blocks_zero"), 1)
            pool.wait_ge(sig("ident"), 1)
            nc.gpsimd.affine_select(out=ident[:, :], in_=ident[:, :], compare_op=ALU.not_equal, fill=1.0,
                                    base=0, pattern=[[-1, P]], channel_multiplier=1).then_inc(sig("ident"), 1)
            pool.wait_ge(sig("v_ones"), 2)
            pool.wait_ge(sig("loaded"), 16 * len(loads[2:]))
            pool.wait_ge(sig("b1_ready"), 1)
            pool.wait_ge(sig("v_kept"), 2 + 1)
            stage(0, 0)
            pool.wait_ge(sig("v_kept"), 2 * B + 1)

            pool.wait_ge(sig("qk_stored"), B * 6 * 16 + 1)
            for piece in range(PIECES):
                split_weights(0, piece, 32, None)
            residual(0)
            with pool.Fori(0, NG // 2) as gp:
                for p in range(2):
                    main(gp * 2 + p, p, False, 0, gp * 2 + p)
            residual2(0)
            with pool.Fori(1, B) as b:
                residual(b)
                ch.enter(b - 1, NG * 2 * PIECES)
                with pool.Fori(0, NG // 2) as gp:
                    inner = Chain(pool, ch.sem)
                    inner.base = ch.base + gp * (4 * PIECES)
                    keep, ch = ch, inner
                    for p in range(2):
                        main(b * NG + gp * 2 + p, p, True, b, gp * 2 + p)
                    assert inner.n == 4 * PIECES
                    ch = keep
                ch.n += NG * 2 * PIECES
                ch.leave(B - 1)
                residual2(b)
            with pool.Fori(0, NG // 2) as gp:
                ch.enter(gp, 4 * PIECES)
                for p in range(2):
                    fi = gp * 2 + p + (NI - NG)
                    pool.wait_ge(sig("relus"), fi * UNITS - UNITS + 1)
                    stage_biases(p, gp * 2 + p)
                    ffn_steps(fi, B, False)
                ch.leave(NG // 2)


def kernel(**inputs):
    import numpy as _np
    import concourse.bacc as _bacc
    from concourse import mybir as _mybir
    from concourse.bass_utils import run_bass_kernel_spmd as _run

    nc = _bacc.Bacc("TRN2", target_bir_lowering=False, num_devices=1)
    arrays, args = {}, {}
    for name, value in inputs.items():
        v = _np.ascontiguousarray(value).reshape(_np.shape(value) or (1,))
        arrays[f"in_{name}"] = v
        args[name] = nc.dram_tensor(f"in_{name}", v.shape, _mybir.dt.from_np(v.dtype), kind="ExternalInput").ap()
    out = nc.dram_tensor("out_0", (B, N, C), F32, kind="ExternalOutput").ap()
    build(nc, args, out)
    r = _run(nc, [arrays], core_ids=[0])
    return r.results[0]["out_0"]
```

```python
from contextlib import ExitStack

import concourse.bass as bass
from concourse import mybir

F32 = mybir.dt.float32
F32R = mybir.dt.float32r
ACT = mybir.ActivationFunctionType
ALU = mybir.AluOpType
X = mybir.AxisListType.X

P = 128
B, N, C = 4, 1024, 128
H, HD = 16, 8
T = 4
KI, KH, KO = 16, 8, 2
E, DM = 8, 512
NT = N // P
GH = 4
NG = H // GH
NI = B * NG
PARTS = 3 * HD
ROWS = PARTS + 2
HALF = 512
CH = DM // P
STEPS = 64
LAG = 16
AHEAD = STEPS - LAG
UNITS = 16
ALL_UNITS = NG * UNITS
PIECES = 4
TAIL = 4
EPS = 1e-5
ATTN_SCALE = HD ** -0.5 / 0.72


def ffn_unit(g, s, offset=0):
    step = (g - 1) * STEPS + s - offset
    return step // UP_EVERY if step >= 0 and step % UP_EVERY == 0 else None


def rotation(reserved):
    order, used = [], [0, 1, 2]
    for s in range(STEPS):
        pick = next(i for i in used if not (i == 2 and s in reserved or s == STEPS - 1 and i == order[0]))
        used = [i for i in used if i != pick] + [pick]
        order.append(pick)
    back = [next(d for d in range(1, STEPS) if order[(s - d) % STEPS] == order[s]) for s in range(STEPS)]
    return order, back


S = dict(load=0, invert=10, heads=18, project=20, residual=22, moments=24, variances=26, root=27, norm=29,
         turn=31, modulate=33, w_in=35, t=37, t_low=39, logits=41, shift=43, exps=44, probs=45, first=46,
         second=48, weights=50, turn_route=53, route_rows=54, store_route=55, mix_b2=56, start_sums=58)

KA = dict(turn_means=14, mix=18, psi_phi=22, psi_norm=30, turn_psi=37, out=41)
FIRST_TURN = 34

TURN = (20, 52)
B_BANK, B_BACK = rotation([s + i for s in TURN for i in range(4)])
A_BANK, A_BACK = rotation(())

UP_EVERY = 3
CREDIT = {"exps": 8, "w2_done": 2, "pv_done": 2, "o_moved": 1, "relus": 1, "w_split1": 1, "moe_taken": 1, "moe_added": 2, "x_turned": 1, "lo_ready": 1, "v_kept": 1, "qk_stored": 1, "wout_done": 1, "stored": 1, "o_stored0": 1, "o_stored1": 1}


class Chain:

    def __init__(self, eng, sem):
        self.eng, self.sem, self.n, self.base = eng, sem, 0, None

    def did(self, ins):
        ins.then_inc(self.sem, 1)
        self.n += 1

    def value(self):
        return self.n if self.base is None else self.base + self.n

    def wait(self):
        self.eng.wait_ge(self.sem, self.value())

    def link(self, ins):
        self.did(ins)
        self.wait()

    def enter(self, index, per):
        self.outer = (self.base, self.n)
        start = self.n if self.base is None else self.base + self.n
        self.base, self.n, self.per = index * per + start, 0, per

    def leave(self, times):
        assert self.n == self.per, (self.n, self.per)
        base, n = self.outer
        self.base, self.n = base, n + times * self.per


def build(nc, a, out):
    with ExitStack() as ctx:
        def sb(name, shape, dt=F32):
            return ctx.enter_context(nc.sbuf_tensor(name, shape, dt))

        sems = {}

        def sig(name):
            if name not in sems:
                sems[name] = ctx.enter_context(nc.semaphore(name))
            return sems[name]

        ps = ctx.enter_context(nc.psum_tensor("ps", [P, 8, HALF], F32))

        q_dram = nc.dram_tensor("q_dram", [B * H, ROWS, N], F32)
        k_dram = nc.dram_tensor("k_dram", [B * H, ROWS, N], F32)
        o_dram = nc.dram_tensor("o_dram", [B * H, HD + 1, N], F32)
        inverse_dram = nc.dram_tensor("inverse_dram", [H, N], F32)
        mean_dram = nc.dram_tensor("mean_dram", [2, B, C], F32)
        route_dram = nc.dram_tensor("route_dram", [E, N], F32)
        fac_dram = nc.dram_tensor("fac_dram", [B * H, HD], F32)

        wqkv = sb("wqkv", [P, 3 * C]); wproj = sb("wproj", [P, C])
        win = sb("win", [P, C]); wout = sb("wout", [P, C]); wgate = sb("wgate", [P, E])
        wmod = sb("wmod", [P, 6 * C]); cmod = sb("cmod", [B, C])
        b1rows = sb("b1rows", [E * CH, P]); b2 = sb("b2", [E, C])
        bproj_bc = sb("bproj_bc", [P, C]); bout_bc = sb("bout_bc", [P, C])
        bin_col = sb("bin_col", [P, 1]); bgate_bc = sb("bgate_bc", [P, E])
        beta_bc = sb("beta_bc", [P, B * H]); alpha_col = sb("alpha_col", [P, 1])
        ka_a = sb("ka_a", [KI, T, KI]); ka_phi1 = sb("ka_phi1", [KI, T, KH])
        ka_bphi1 = sb("ka_bphi1", [T * KH, 1]); ka_phi2 = sb("ka_phi2", [T * KH, HD])
        ka_psi1 = sb("ka_psi1", [T * KI, T * KI]); ka_psi2 = sb("ka_psi2", [T * KI, HD])
        MB = B * H
        bphi2_bc = sb("bphi2_bc", [MB, HD]); bpsi1_bc = sb("bpsi1_bc", [MB, T * KI])
        lng_bc = sb("lng_bc", [MB, T * KI]); lnb_bc = sb("lnb_bc", [MB, T * KI])
        bpsi2_bc = sb("bpsi2_bc", [MB, HD]); mix_bc = sb("mix_bc", [MB, T])
        temp_bc = sb("temp_bc", [MB, 1]); gamma_col = sb("gamma_col", [MB, 1])

        ident = sb("ident", [P, P]); rev = sb("rev", [P, E])
        siluT = sb("siluT", [P, B])
        mod_col = sb("mod_col", [P, 4, B])
        gate_bc = sb("gate_bc", [P, 2, B * C])
        wproj_g = sb("wproj_g", [P, B, C]); wout_g = sb("wout_g", [P, B, C])
        bproj_g = sb("bproj_g", [P, B, C]); bout_g = sb("bout_g", [P, B, C])
        b1T = sb("b1T", [P, E * CH])

        eps_col = sb("eps_col", [P, 1]); qk_scale = sb("qk_scale", [P, 2]); credit = sb("credit", [P, len(CREDIT) + 1])
        pool_wait = sb("pool_wait", [P, 1])

        x_all = sb("x_all", [P, B * NT, C]); v_all = sb("v_all", [P, NI, NT, GH * HD])
        stats = sb("stats", [P, B * NT, 6]); mv = sb("mv", [P, B * NT, 2])
        std = sb("std", [P, B * NT]); rstd = sb("rstd", [P, B * NT])
        xn = sb("xn", [P, NT, C]); hT = sb("hT", [P, N])
        hsum = sb("hsum", [P, 2 * B]); hmean = sb("hmean", [P, B])
        qk_hi = sb("qk_hi", [P, 2, N], F32R); qk_lo = sb("qk_lo", [P, 2, N], F32R)

        qkm = sb("qkm", [B, 2, C]); qk = sb("qk", [MB, KI]); qkT = sb("qkT", [KI, MB])
        axT = sb("axT", [T * KI, MB]); phiT = sb("phiT", [T * KH, MB]); phi = sb("phi", [MB, HD])
        psi = sb("psi", [MB, T, KI]); psq = sb("psq", [MB, T, KI]); psm = sb("psm", [MB, T])
        psv = sb("psv", [MB, T]); pst = sb("pst", [MB, T]); psiT = sb("psiT", [T * KI, MB])
        psi_o = sb("psi_o", [MB, HD]); fac = sb("fac", [MB, HD]); vfac = sb("vfac", [P, B])

        Q = [sb(f"Q{i}", [P, N], F32R) for i in range(2)]
        K = [sb(f"K{i}", [P, GH, N], F32R) for i in range(2)]
        V = [sb(f"V{i}", [P, NT, GH, 32]) for i in range(2)]
        beta_g = [sb(f"beta_g{i}", [P, GH]) for i in range(2)]
        probs = sb("probs", [P, 8, HALF])
        gt0, gt1 = probs[:, 0:2, :], probs[:, 2:4, :]
        silu_bc = probs[:, 4, :].rearrange("p (b n) -> p b n", b=B)
        mxp = sb("mxp", [P, NT, 2, GH]); mx = sb("mx", [P, 16]); mxb = sb("mxb", [P, 16])
        mrow = sb("mrow", [P, 16]); mparts = sb("mparts", [P, 2, 16], F32R)
        mrows = sb("mrows", [32, P])
        oT = sb("oT", [P, 2, HALF])
        w_raw = [sb(f"w_raw{i}", [P, DM + CH * C]) for i in range(2)]
        w_hi, w_lo = qk_hi, qk_lo
        b1s = [sb(f"b1s{i}", [P, 2, CH]) for i in range(2)]
        mid_hi = sb("mid_hi", [P, 2, HALF], F32R); mid_lo = sb("mid_lo", [P, 2, HALF], F32R)
        x_space = x_all[:, :, :].rearrange("p t c -> p (t c)")
        route_bc = [x_space[:, N * i:N * (i + 1)] for i in range(2)]
        weighted = x_space[:, 2 * N:3 * N].rearrange("p (i n) -> p i n", i=2)
        mid = x_space[:, 3 * N:4 * N].rearrange("p (i n) -> p i n", i=2)

        tail_hi, tail_lo = (K[0][:, 2 * i:2 * i + 2, :].rearrange("p a (b n) -> p (a b) n", n=HALF) for i in range(2))
        tail_mid = probs[:, 0:TAIL, :]
        TAIL_UP, TAIL_DOWN = (0, 1, 5, 2), (6, 7)

        oc = sb("oc", [P, N]); den = sb("den", [P, N])
        xg = sb("xg", [P, NT, C]); x1 = sb("x1", [P, NT, C])
        st2 = sb("st2", [P, NT, 6]); mv2 = sb("mv2", [P, NT, 2]); sd2 = sb("sd2", [P, NT])
        t_raw = oc
        t_hi = sb("t_hi", [P, N], F32R); t_lo = sb("t_lo", [P, N], F32R)
        lg = sb("lg", [P, NT, E]); pr = sb("pr", [P, NT, E]); g0 = sb("g0", [P, NT, E])
        g1 = sb("g1", [P, NT, E]); g2 = sb("g2", [P, NT, E]); gm = sb("gm", [P, NT])
        route = sb("route", [P, NT, E]); routeT = sb("routeT", [E, N])
        accT = sb("accT", [P, N]); y = sb("y", [P, NT, C])

        def bank(i):
            return ps[:, i, :]

        def b_bank(s):
            return (2, 3, 7)[B_BANK[s]]

        def a_bank(s, kind):
            return (0, 1, 5)[A_BANK[s]] if kind == "attention" else s % 2

        def tiles(i):
            return ps[:, i, :].rearrange("p (t c) -> p t c", c=P)

        def split_piece(eng, ch, u, piece):
            size = (DM + CH * C) // PIECES
            part = slice(piece * size, (piece + 1) * size)
            ch.link(eng.tensor_copy(w_hi[:, u, part], w_raw[u][:, part]))
            m = eng.tensor_tensor(w_lo[:, u, part], w_raw[u][:, part], w_hi[:, u, part].bitcast(F32), ALU.subtract)
            if piece == PIECES - 1:
                m.then_inc(sig(f"w_split{u}"), 1)

        def over_experts(t):
            return t[:, :].unsqueeze(2).broadcast_to([P, NT, E])

        def over_tiles(t):
            return t[:, :].unsqueeze(1).broadcast_to([P, NT, E])

        row = lambda v, n: v.partition_broadcast(n)
        loads = [(cmod[:, :], a["L0_c"]), (wmod[:, :], a["L0_wmod"])]
        loads += [(wqkv[:, :], a["L0_attn_Wqkv"]),
                  (alpha_col[:, :], a["L0_attn_alpha"].rearrange("(h d o) -> h d o", d=1, o=1).broadcast_to([H, HD, 1]))]
        loads += [(wproj[:, :], a["L0_attn_Wproj"]),
                  (win[:, :], a["L0_ffn_W_in"]), (wout[:, :], a["L0_ffn_W_out"]),
                  (wgate[:, :], a["L0_ffn_W_gate"]),
                  (b1rows[:, :], a["L0_ffn_b1"].rearrange("e (c p) -> (e c) p", p=P)),
                  (b2[:, :], a["L0_ffn_b2"]),
                  (bproj_bc[:, :], row(a["L0_attn_bproj"], P)),
                  (bout_bc[:, :], row(a["L0_ffn_b_out"], P)),
                  (bin_col[:, :], a["L0_ffn_b_in"].rearrange("(p o) -> p o", o=1)),
                  (bgate_bc[:, :], row(a["L0_ffn_b_gate"], P)),
                  (ka_a[:, :, :], a["L0_attn_A"].rearrange("t d e -> d t e")),
                  (ka_phi1[:, :, :], a["L0_attn_Wphi1"].rearrange("t d e -> d t e")),
                  (ka_bphi1[:, :], a["L0_attn_bphi1"].rearrange("t (h o) -> (t h) o", o=1)),
                  (bphi2_bc[:, :], row(a["L0_attn_bphi2"].rearrange("t o -> (t o)"), MB)),
                  (bpsi1_bc[:, :], row(a["L0_attn_bpsi1"].rearrange("t o -> (t o)"), MB)),
                  (lng_bc[:, :], row(a["L0_attn_ln_g"].rearrange("t o -> (t o)"), MB)),
                  (lnb_bc[:, :], row(a["L0_attn_ln_b"].rearrange("t o -> (t o)"), MB)),
                  (bpsi2_bc[:, :], row(a["L0_attn_bpsi2"].rearrange("t o -> (t o)"), MB)),
                  (mix_bc[:, :], row(a["L0_attn_mixing"], MB)),
                  (temp_bc[:, :], row(a["L0_attn_temp_scale"].rearrange("(o) -> o", o=1), MB))]
        loads += [(beta_bc[:, :].rearrange("p (b h) -> p b h", b=B), row(row(a["L0_attn_beta"], B), P))]
        loads += [(gamma_col[:, :], row(a["L0_attn_gamma"].rearrange("(h o) -> h o", o=1), B))]
        blocks = []
        for t in range(T):
            blocks += [(ka_phi2[t * KH:(t + 1) * KH, t * KO:(t + 1) * KO], a["L0_attn_Wphi2"][t]),
                       (ka_psi1[t * KI:(t + 1) * KI, t * KI:(t + 1) * KI], a["L0_attn_Wpsi1"][t]),
                       (ka_psi2[t * KI:(t + 1) * KI, t * KO:(t + 1) * KO], a["L0_attn_Wpsi2"][t])]

        block = ctx.enter_context(nc.Block())

        @block.sync
        def _(sp):
            def load_group(it, p):
                for j in range(GH):
                    head = it * GH + j
                    sp.dma_start(Q[p][32 * j:32 * j + ROWS, :].bitcast(F32), q_dram[head]).then_inc(sig("qk_loaded"), 16)
                    sp.dma_start(K[p][32 * j:32 * j + ROWS, j, :].bitcast(F32), k_dram[head]).then_inc(sig("qk_loaded"), 16)

            def load_expert(e, u):
                sp.dma_start(w_raw[u][:, 0:DM], a["L0_ffn_W1"][e]).then_inc(sig(f"w_loaded{u}"), 16)
                sp.dma_start(w_raw[u][:, DM:].rearrange("p (c d) -> p c d", d=C), a["L0_ffn_W2"][e].rearrange("(c p) d -> p c d", p=P)).then_inc(sig(f"w_loaded{u}"), 16)

            def load_route(e, b):
                if e == 0:
                    sp.wait_ge(sig("route_stored"), b * 16 + 16)
                else:
                    sp.wait_ge(sig("moe_taken"), b * (2 * E) + 2 * (e - 1) + 1)
                sp.dma_start(route_bc[e % 2], row(route_dram[e], P)).then_inc(sig(f"route_loaded{e % 2}"), 16)

            def load_residual(b):
                if not (isinstance(b, int) and b == 0):
                    sp.wait_ge(sig("h2_normed"), b * NT)
                sp.dma_start(xg[:, :, :], a["L0_attn_x"][b].rearrange("(t p) c -> p t c", p=P)).then_inc(sig("xg_loaded"), 16)

            def max_rows(count, p, half):
                sp.wait_ge(sig("max_moved"), count + 1)
                for part in range(2):
                    sp.dma_start(Q[p][PARTS + part:P:32, HALF * half:HALF * (half + 1)].rearrange(
                        "j (t n) -> j t n", n=P).bitcast(F32), mrows[16 * part:16 * part + 16, :]).then_inc(sig("max_rows"), 16)

            def store_heads(it, half):
                sp.wait_ge(sig("o_moved"), it * 2 + half + 2)
                for j in range(GH):
                    sp.dma_start(o_dram[it * GH + j, :, HALF * half:HALF * (half + 1)],
                                 oT[32 * j:32 * j + HD + 1, half, :]).then_inc(sig(f"o_stored{half}"), 16)

            def main(it, p, kind, g, b):
                for s in range(STEPS):
                    if kind == "post":
                        post(b, s)
                    if s == 0:
                        sp.wait_ge(sig("exps"), it * STEPS + CREDIT["exps"])
                        load_group((it + 1) % NI, 1 - p)
                    if s == TURN[0] + 2:
                        max_rows(it * 2 + 1, p, 1)
                    if s == 38:
                        store_heads(it, 0)
                    if s == TURN[1] + 2:
                        max_rows(it * 2 + 2, 1 - p, 0)
                    if kind == "ffn":
                        step, per = (g - 1) * STEPS + s, UP_EVERY * UNITS // 2
                        if step % per == per // 2:
                            e = step // per + 2
                            sp.wait_ge(sig(f"w_split{e % 2}"), b * NG + e // 2 + (e % 2))
                            load_expert(e % E, e % 2)
                        if step % per == per * 2 // 3 and step // per + 1 < E:
                            load_route(step // per + 1, b)
                store_heads(it, 1)
                if kind == "post":
                    load_route(0, b)

            def post(b, s):
                if s == S["load"]:
                    sp.wait_ge(sig("o_stored0"), (b + 1) * NG * GH * 16 + 1)
                    sp.wait_ge(sig("o_stored1"), (b + 1) * NG * GH * 16 + 1)
                    o_b = o_dram[:, :, :].rearrange("(b h) r n -> b h r n", h=H)[b]
                    sp.dma_start(den[:, 0:P], o_b[:, HD, :].rearrange("h (a n) -> h a n", n=P)).then_inc(sig("sums_loaded"), 16)
                    sp.dma_start(oc[:, :], o_b[:, 0:HD, :]).then_inc(sig("o_loaded"), 16)
                if s == S["invert"]:
                    sp.wait_ge(sig("sums_inverted"), b + 1)
                    sp.dma_start(inverse_dram[:, :].rearrange("h (a n) -> h a n", n=P), den[:, 0:P]).then_inc(sig("inverse_stored"), 16)
                    sp.wait_ge(sig("inverse_stored"), b * 16 + 16)
                    sp.dma_start(den[:, :], inverse_dram[:, :].unsqueeze(1).broadcast_to([H, HD, N])).then_inc(sig("o_loaded"), 16)
                if s == S["store_route"]:
                    sp.wait_ge(sig("route_rows"), b * 2 + 2)
                    sp.dma_start(route_dram[:, :], routeT[:, :]).then_inc(sig("route_stored"), 16)
                if s == S["start_sums"] and not (isinstance(b, int) and b == B - 1):
                    load_residual(b + 1)

            def finish(b):
                sp.wait_ge(sig("y_ready"), b * 2 + 2)
                sp.dma_start(out[b].rearrange("(t p) c -> p t c", p=P), y[:, :, :]).then_inc(sig("stored"), 16)

            for dst, src in loads[:2]:
                sp.dma_start(dst, src).then_inc(sig("mod_loaded"), 16)
            for b in range(B):
                sp.dma_start(x_all[:, b * NT:(b + 1) * NT, :], a["L0_attn_x"][b].rearrange("(t p) c -> p t c", p=P)).then_inc(sig(f"x_loaded{b}"), 16)
            for dst, src in loads[2:4]:
                sp.dma_start(dst, src).then_inc(sig("qkv_loaded"), 16)
            for dst, src in loads[4:]:
                sp.dma_start(dst, src).then_inc(sig("loaded"), 16)
            sp.wait_ge(sig("row_values"), 2)
            for dram, src in ((q_dram, accT[0:B * H, :]), (k_dram, y[0:B * H, :, :].rearrange("p t c -> p (t c)"))):
                for part in range(2):
                    sp.dma_start(dram[:, PARTS + part, :], src).then_inc(sig("rows_stored"), 16)
            def store_parts(b):
                for sem, parts in (("hi_ready", ((0, 0, qk_hi), (0, 1, qk_hi), (1, 0, qk_hi), (1, 2, qk_hi))),
                                   ("lo_ready", ((0, 2, qk_lo), (1, 1, qk_lo)))):
                    sp.wait_ge(sig(sem), b * 4 + 4 + (sem == "lo_ready"))
                    for r, part, src in parts:
                        dram = (q_dram, k_dram)[r][:, :, :].rearrange("(b h) r n -> b h r n", h=H)[b]
                        sp.dma_start(dram[:, HD * part:HD * (part + 1), :], src[:, r, :].bitcast(F32)).then_inc(sig("qk_stored"), 16)

            store_parts(0)
            sp.wait_ge(sig("blocks_zero"), 3)
            for dst, src in blocks:
                sp.dma_start(dst, src).then_inc(sig("blocks_loaded"), 16)
            load_expert(0, 0)
            load_expert(1, 1)
            store_parts(1)
            sp.wait_ge(sig("qk_stored"), 6 * 16 + 1)
            sp.wait_ge(sig("qk_zero"), 4)
            sp.wait_ge(sig("rows_stored"), 64)
            load_group(0, 0)
            with sp.Fori(2, B) as b:
                store_parts(b)

            sp.wait_ge(sig("means_ready"), 2)
            sp.dma_start(mean_dram[:, :, :].rearrange("r b c -> b r c"), qkm[:, :, :]).then_inc(sig("means_stored"), 16)
            sp.wait_ge(sig("means_stored"), 16)
            for r in range(2):
                sp.dma_start(qk[:, r * HD:(r + 1) * HD], mean_dram[r].rearrange("b (h d) -> (b h) d", d=HD)).then_inc(sig("qk_means"), 16)
            sp.wait_ge(sig("qk_stored"), B * 6 * 16 + 1)
            max_rows(0, 0, 0)
            sp.wait_ge(sig("fac_ready"), 1)
            sp.dma_start(fac_dram[:, :], fac[:, :]).then_inc(sig("fac_stored"), 16)
            sp.wait_ge(sig("fac_stored"), 16)
            for b in range(B):
                sp.dma_start(vfac[:, b:b + 1], fac_dram[b * H:(b + 1) * H, :].rearrange("h (d o) -> (h d) o", o=1)).then_inc(sig("fac_loaded"), 16)
            load_residual(0)

            with sp.Fori(0, NG // 2) as gp:
                for p in range(2):
                    main(gp * 2 + p, p, "attention", None, None)
            with sp.Fori(0, B - 1) as b:
                main(b * NG + NG, 0, "post", 0, b)
                for g in range(1, NG):
                    main(b * NG + (NG + g), g % 2, "ffn", g, b)
                finish(b)
            for s in range(STEPS):
                post(B - 1, s)
            load_route(0, B - 1)
            with sp.Fori(0, NG) as g:
                fi = g + (NI - NG)
                sp.wait_ge(sig("moe_taken"), fi * 4 + 1)
                sp.dma_start(route_bc[1], row(route_dram[g * 2 + 1], P)).then_inc(sig("route_loaded1"), 16)
                sp.wait_ge(sig("w_split0"), fi + 1)
                load_expert((g * 2 + 2) % E, 0)
                sp.wait_ge(sig("w_split1"), fi + 2)
                load_expert((g * 2 + 3) % E, 1)
                sp.wait_ge(sig("moe_taken"), fi * 4 + 3)
                sp.dma_start(route_bc[0], row(route_dram[(g * 2 + 2) % E], P)).then_inc(sig("route_loaded0"), 16)
            finish(B - 1)
            sp.wait_ge(sig("route_loaded0"), (NI + 1) * 16)
            sp.wait_ge(sig("stored"), B * 16 + 1)
            sp.wait_ge(sig("w_loaded0"), 32 * (NI + 1))
            sp.wait_ge(sig("w_loaded1"), 32 * (NI + 1))
            sp.wait_ge(sig("qk_loaded"), 128 * (NI + 1))
            sp.wait_ge(sig("max_rows"), 32 * (2 * NI + 1))

        @block.tensor
        def _(pe):
            mm = nc.tensor.matmul

            def a_back(s, kind):
                return A_BACK[s] if kind == "attention" else 2

            def score_max(a_i, to, p):
                nt, mh, j = a_i // 8, a_i // 4 % 2, a_i % 4
                mm(bank(to), Q[p][:, P * nt:P * (nt + 1)], K[p][:, j, HALF * mh:HALF * (mh + 1)],
                   start=True, stop=True).then_inc(sig("max_scores"), 1)

            def move_max(count, n):
                pe.wait_ge(sig("max_parts"), count + 1)
                nc.tensor.transpose(ps[0:32, 7, 0:P], mparts[:, :, :].rearrange("p a b -> p (a b)").bitcast(F32), ident[:, :]).then_inc(sig("max_turned"), 1)

            def in_parts(to, w, w_other, x, x_other, start, stop):
                mm(to, w, x, start=start, stop=False)
                mm(to, w_other, x, start=False, stop=False)
                return mm(to, w, x_other, start=False, stop=stop)

            def expert_up(q, to, fi, depth=1):
                u, th, c = q // 8, q // 4 % 2, q % 4
                if q % 8 == 0:
                    pe.wait_ge(sig(f"w_split{u}"), fi + 1 + u)
                pe.wait_ge(sig("relus"), fi * UNITS + q + 2 - depth)
                w, tok = slice(P * c, P * (c + 1)), slice(HALF * th, HALF * (th + 1))
                in_parts(bank(to), w_hi[:, u, w], w_lo[:, u, w], t_hi[:, tok], t_lo[:, tok], True, True).then_inc(sig("w1_done"), 1)

            def expert_down(q, fi, to=6, hi=mid_hi, lo=mid_lo, depth=2, sums=1):
                u, th, c = q // 8, q // 4 % 2, q % 4
                pe.wait_ge(sig("mid_split"), fi * UNITS + q + 1)
                if c == 0:
                    pe.wait_ge(sig("moe_taken"), fi * 4 + q // 4 + 2 - sums)
                w = slice(DM + C * c, DM + C * (c + 1))
                in_parts(bank(to), w_hi[:, u, w], w_lo[:, u, w], hi[:, q % depth, :], lo[:, q % depth, :], c == 0, c == CH - 1).then_inc(sig("w2_done"), 1)

            def main(it, p, kind, g, b):
                def pv(v):
                    half, mt = v // NT, v % NT
                    pe.wait_ge(sig("exps"), it * STEPS + 4 * (v + 1) + CREDIT["exps"])
                    if v == 0:
                        pe.wait_ge(sig("v_staged"), it + 1)
                    if mt == 0:
                        pe.wait_ge(sig("o_moved"), it * 2 + half + 1)
                    for j in range(GH):
                        m = mm(ps[32 * j:32 * j + 32, 4, :], V[p][:, mt, j, :], probs[:, 4 * (mt % 2) + j, :],
                               start=(mt == 0), stop=(mt == NT - 1), tile_position=(0, 32 * j))
                    m.then_inc(sig("pv_done"), 1)

                for s in range(STEPS):
                    if s == LAG:
                        pe.wait_ge(sig("qk_loaded"), it * 128 + 256)
                    pe.wait_ge(sig("maxed"), it * STEPS + AHEAD + s + 1 - a_back(s, kind))
                    score_max((s - LAG) % STEPS, a_bank(s, kind), p if s < LAG else 1 - p)
                    half, mt, j = s // 32, s % 32 // 4, s % 4
                    if s % 32 == 0:
                        pe.wait_ge(sig("max_rows"), it * 64 + 32 * half + 32)
                    pe.wait_ge(sig("exps"), it * STEPS + s + 1 - B_BACK[s] + CREDIT["exps"])
                    if s == TURN[0] + 4:
                        pe.wait_ge(sig("max_moved"), it * 2 + 2)
                    if s == TURN[1] + 4:
                        pe.wait_ge(sig("max_moved"), it * 2 + 3)
                    mm(bank(b_bank(s)), K[p][:, j, P * mt:P * (mt + 1)], Q[p][:, HALF * half:HALF * (half + 1)],
                       start=True, stop=True).then_inc(sig("scores"), 1)
                    if kind == "ffn":
                        u = ffn_unit(g, s)
                        if u is not None:
                            expert_up(u % UNITS, 5, b * NG + u // UNITS)
                        u = ffn_unit(g, s, 2)
                        if u:
                            expert_down((u - 1) % UNITS, b * NG + (u - 1) // UNITS)
                    if kind == "post":
                        post(b, s)
                    if s % 4 == 3 and s > 3:
                        pv(s // 4 - 1)
                    if s in TURN:
                        last = max(i for i in range(s) if B_BANK[i] == 2)
                        pe.wait_ge(sig("exps"), it * STEPS + last + 1 + CREDIT["exps"])
                        move_max(it * 2 + 1 + TURN.index(s), None)
                if kind == "post":
                    pe.wait_ge(sig("moe_started"), b * 2 + 2)
                    pe.wait_ge(sig("t_split"), b * 2 + 2)
                if kind == "ffn" and g == NG - 1:
                    expert_down(UNITS - 1, b * NG + NG - 1)
                pv(2 * NT - 1)

            def post(b, s):
                def into(t):
                    return ps[:, 5 + t // 4, P * (t % 4):P * (t % 4 + 1)]

                def half(name):
                    return s - S[name] if s in (S[name], S[name] + 1) else None

                f = half("project")
                if f is not None:
                    pe.wait_ge(sig("o_normed"), b * 2 + f + 1)
                    for t in range(4 * f, 4 * f + 4):
                        m = mm(into(t), oc[:, P * t:P * (t + 1)], wproj_g[:, bass.ds(b, 1), :], start=True, stop=True)
                    m.then_inc(sig("proj_done"), 1)
                f = half("turn")
                if f is not None:
                    pe.wait_ge(sig("h2_normed"), b * NT + 4 * f + 4)
                    for t in range(4 * f, 4 * f + 4):
                        m = nc.tensor.transpose(into(t), xn[:, t, :], ident[:, :])
                    m.then_inc(sig("h2_turned"), 1)
                f = half("w_in")
                if f is not None:
                    pe.wait_ge(sig("h2_modded"), b * 2 + f + 1)
                    mm(bank(5 + f), win[:, :], hT[:, HALF * f:HALF * (f + 1)], start=True, stop=True).then_inc(sig("win_done"), 1)
                if s == S["logits"]:
                    pe.wait_ge(sig("t_hi_ready"), b * 2 + 2)
                    for t in range(NT):
                        m = mm(ps[:, 5, E * t:E * (t + 1)], t_raw[:, P * t:P * (t + 1)], wgate[:, :], start=True, stop=True)
                    m.then_inc(sig("logits"), 1)
                if s == S["turn_route"]:
                    pe.wait_ge(sig("routed"), b + 1)
                    for t in range(NT):
                        m = nc.tensor.transpose(ps[0:E, 5 + t // 4, P * (t % 4):P * (t % 4 + 1)], route[:, t, :], ident[:, :])
                    m.then_inc(sig("route_turned"), 1)
                f = half("mix_b2")
                if f is not None:
                    pe.wait_ge(sig("route_rows"), b * 2 + 2)
                    mm(bank(5 + f), b2[:, :], routeT[:, HALF * f:HALF * (f + 1)], start=True, stop=True).then_inc(sig("b2_mixed"), 1)

            def finish(b):
                pe.wait_ge(sig("moe_added"), b * 16 + 16 + CREDIT["moe_added"])
                for t in range(NT):
                    m = mm(ps[:, 5 + t // 4, P * (t % 4):P * (t % 4 + 1)], accT[:, P * t:P * (t + 1)], wout_g[:, b, :], start=True, stop=True)
                    if t % 4 == 3:
                        m.then_inc(sig("wout_done"), 1)

            pe.wait_ge(sig("ident"), 2)
            pe.wait_ge(sig("mod_loaded"), 32)
            nc.tensor.transpose(ps[:, 0, 0:B], cmod[:, :], ident[0:B, 0:B]).then_inc(sig("c_turned"), 1)
            pe.wait_ge(sig("silu_ready"), 2)
            for i, chunk in enumerate((0, 1, 3, 4)):
                m = mm(ps[:, 1, B * i:B * (i + 1)], wmod[:, chunk * C:(chunk + 1) * C], siluT[:, :], start=True, stop=True)
            for i, chunk in enumerate((2, 5)):
                for b in range(B):
                    m = mm(ps[:, 2 + i, C * b:C * (b + 1)], silu_bc[:, b, :], wmod[:, chunk * C:(chunk + 1) * C], start=True, stop=True)
            m.then_inc(sig("mod_done"), 1)
            pe.wait_ge(sig("qkv_loaded"), 32)
            pe.wait_ge(sig("gates_kept"), 2)

            with pe.Fori(0, B) as b:
                for t in range(NT):
                    pe.wait_ge(sig("x_normed"), b * NT + t + 1)
                    m = nc.tensor.transpose(ps[:, t // 4, P * (t % 4):P * (t % 4 + 1)], xn[:, t, :], ident[:, :])
                    if t % 4 == 3:
                        m.then_inc(sig("x_turned"), 1)
                pe.wait_ge(sig("lo_ready"), b * 4 + 1)
                pe.wait_ge(sig("v_kept"), b * 2 + 1)
                for f in range(2):
                    pe.wait_ge(sig("h_ready"), b * 2 + f + 1)
                    for r in range(2):
                        mm(bank(2 + 2 * r + f), wqkv[:, C * r:C * (r + 1)], hT[:, HALF * f:HALF * (f + 1)], start=True, stop=True).then_inc(sig("qk_done"), 1)
                for t in range(NT):
                    m = mm(ps[:, 6 + t // 4, P * (t % 4):P * (t % 4 + 1)], hT[:, P * t:P * (t + 1)], wqkv[:, 2 * C:3 * C], start=True, stop=True)
                    if t % 4 == 3:
                        m.then_inc(sig("v_done"), 1)

            pe.wait_ge(sig("h_ready"), 2 * B)
            pe.wait_ge(sig("lo_ready"), 4 * B + 1)
            pe.wait_ge(sig("v_kept"), 2 * B + 1)
            pe.wait_ge(sig("loaded"), 16 * len(loads[4:]))
            nc.tensor.transpose(ps[:, 4, 0:E * CH], b1rows[:, :], ident[0:E * CH, 0:E * CH]).then_inc(sig("b1_turned"), 1)
            pe.wait_ge(sig("hmean_ready"), 1)
            for r in range(2):
                m = mm(ps[0:B, 2, C * r:C * (r + 1)], hmean[:, :], wqkv[:, C * r:C * (r + 1)], start=True, stop=True)
            m.then_inc(sig("means_done"), 1)

            def ka(a_i):
                if a_i == KA["turn_means"]:
                    pe.wait_ge(sig("qk_means"), 32)
                    nc.tensor.transpose(ps[0:KI, 3, 0:MB], qk[:, :], ident[0:MB, 0:MB]).then_inc(sig("ka_pe"), 1)
                if a_i == KA["mix"]:
                    pe.wait_ge(sig("ka_sb"), 1)
                    pe.wait_ge(sig("b1_ready"), 1)
                    pe.wait_ge(sig("means_ready"), 2)
                    mm(ps[0:T * KI, 2, 0:MB], ka_a[:, :, :].rearrange("d t e -> d (t e)"), qkT[:, :], start=True, stop=True).then_inc(sig("ka_pe"), 1)
                    mm(ps[0:T * KH, 4, 0:MB], ka_phi1[:, :, :].rearrange("d t e -> d (t e)"), qkT[:, :], start=True, stop=True).then_inc(sig("ka_pe"), 1)
                if a_i == KA["psi_phi"]:
                    pe.wait_ge(sig("blocks_loaded"), 16 * len(blocks))
                    pe.wait_ge(sig("ka_sb"), 2)
                    mm(ps[0:MB, 6, 0:T * KI], axT[:, :], ka_psi1[:, :], start=True, stop=True).then_inc(sig("ka_pe"), 1)
                    pe.wait_ge(sig("ka_phi"), 1)
                    mm(ps[0:MB, 2, 0:HD], phiT[:, :], ka_phi2[:, :], start=True, stop=True).then_inc(sig("ka_pe"), 1)
                if a_i == KA["turn_psi"]:
                    pe.wait_ge(sig("ka_gelu"), 1)
                    nc.tensor.transpose(ps[0:T * KI, 3, 0:MB], psi[:, :, :].rearrange("m t g -> m (t g)"), ident[0:MB, 0:MB]).then_inc(sig("ka_pe"), 1)
                if a_i == KA["out"]:
                    pe.wait_ge(sig("ka_sb"), 3)
                    mm(ps[0:MB, 4, 0:HD], psiT[:, :], ka_psi2[:, :], start=True, stop=True).then_inc(sig("ka_pe"), 1)

            pe.wait_ge(sig("qk_loaded"), 128)
            for a_i in range(AHEAD):
                if a_i >= A_BACK[a_i + LAG]:
                    pe.wait_ge(sig("maxed"), a_i + 1 - A_BACK[a_i + LAG])
                score_max(a_i, a_bank(a_i + LAG, "attention"), 0)
                ka(a_i)
                if a_i == FIRST_TURN:
                    move_max(0, None)

            with pe.Fori(0, NG // 2) as gp:
                for p in range(2):
                    main(gp * 2 + p, p, "attention", None, None)
            with pe.Fori(0, B - 1) as b:
                main(b * NG + NG, 0, "post", 0, b)
                for g in range(1, NG):
                    main(b * NG + (NG + g), g % 2, "ffn", g, b)
                finish(b)
            for s in range(STEPS):
                post(B - 1, s)
            pe.wait_ge(sig("moe_started"), B * 2)
            pe.wait_ge(sig("t_split"), B * 2)
            with pe.Fori(0, NG // 2) as gp:
                for u in range(2 * UNITS + TAIL - 1):
                    if u < 2 * UNITS:
                        expert_up(u % UNITS, TAIL_UP[u % TAIL], gp * 2 + (NI - NG + u // UNITS), TAIL)
                    d = u - (TAIL - 1)
                    if d >= 0:
                        expert_down(d % UNITS, gp * 2 + (NI - NG + d // UNITS), TAIL_DOWN[d // 4 % 2], tail_hi, tail_lo, TAIL, 2)
            finish(B - 1)

        @block.scalar
        def _(act):
            act_fn = nc.scalar.activation

            def relu(q, at, fi, bias, slots=(mid_hi, mid), depth=2):
                act.wait_ge(sig("w1_done"), fi * UNITS + q + 1)
                act.wait_ge(sig("w2_done"), fi * UNITS + q + 3 - depth)
                for dst in slots:
                    m = act_fn(dst[:, q % depth, :], bank(at), ACT.Relu, bias=bias)
                m.then_inc(sig("relus"), 1)

            def main(it, p, kind, g, b):
                for s in range(STEPS):
                    if s % 4 == 0:
                        act.wait_ge(sig("pv_done"), it * 16 + s // 4 + 1)
                    act.wait_ge(sig("scores"), it * STEPS + s + 1)
                    act_fn(probs[:, s % 8, :], bank(b_bank(s)), ACT.Exp).then_inc(sig("exps"), 1)
                    u = ffn_unit(g, s) if kind == "ffn" else None
                    if u is not None:
                        col = u // (UNITS // 2) * CH + u % CH
                        relu(u % UNITS, 5, b * NG + u // UNITS, b1T[:, col:col + 1])
                    if kind == "post":
                        post(b, s)

            def post(b, s):
                def half(name):
                    return s - S[name] if s in (S[name], S[name] + 1) else None

                if s == S["root"]:
                    act.wait_ge(sig("var2"), b * NT + NT)
                    act_fn(sd2[:, :], mv2[:, :, 1], ACT.Sqrt, bias=eps_col[:, 0:1]).then_inc(sig("std2"), 1)
                f = half("modulate")
                if f is not None:
                    act_fn(hT[:, HALF * f:HALF * (f + 1)], bank(5 + f), ACT.Identity, scale=mod_col[:, 3, bass.ds(b, 1)], bias=mod_col[:, 2, bass.ds(b, 1)]).then_inc(sig("h2_modded"), 1)
                if s in (S["modulate"] - 1, S["modulate"]):
                    act.wait_ge(sig("h2_turned"), b * 2 + s - S["modulate"] + 2)
                f = half("t")
                if f is not None:
                    act.wait_ge(sig("win_done"), b * 2 + f + 1)
                    act_fn(t_raw[:, HALF * f:HALF * (f + 1)], bank(5 + f), ACT.Identity, bias=bin_col[:, 0:1])
                    act_fn(t_hi[:, HALF * f:HALF * (f + 1)], bank(5 + f), ACT.Identity, bias=bin_col[:, 0:1]).then_inc(sig("t_hi_ready"), 1)
                if s == S["exps"]:
                    act.wait_ge(sig("logits_shifted"), b + 1)
                    act_fn(pr[:, :, :], lg[:, :, :], ACT.Exp).then_inc(sig("logit_exps"), 1)
                if s == S["route_rows"]:
                    act.wait_ge(sig("route_turned"), b + 1)
                    for f in range(2):
                        act_fn(routeT[:, HALF * f:HALF * (f + 1)], ps[0:E, 5 + f, :], ACT.Copy).then_inc(sig("route_rows"), 1)
                f = half("start_sums")
                if f is not None:
                    act.wait_ge(sig("b2_mixed"), b * 2 + f + 1)
                    act_fn(accT[:, HALF * f:HALF * (f + 1)], bank(5 + f), ACT.Copy).then_inc(sig("moe_started"), 1)

            act.wait_ge(sig("c_turned"), 1)
            act_fn(siluT[:, :], ps[:, 0, 0:B], ACT.Silu).then_inc(sig("silu_ready"), 1)
            act.wait_ge(sig("eps_set"), 1)
            act.wait_ge(sig("var1"), B * NT)
            act_fn(std[:, :], mv[:, :, 1], ACT.Sqrt, bias=eps_col[:, 0:1]).then_inc(sig("std1"), 1)
            act.wait_ge(sig("gates_kept"), 2)

            with act.Fori(0, B) as b:
                for f in range(2):
                    act.wait_ge(sig("x_turned"), b * 2 + f + 2)
                    act_fn(hT[:, HALF * f:HALF * (f + 1)], bank(f), ACT.Identity, scale=mod_col[:, 1, bass.ds(b, 1)], bias=mod_col[:, 0, bass.ds(b, 1)],
                           accum_out=hsum[:, bass.ds(b * 2 + f, 1)]).then_inc(sig("h_ready"), 1)
                act.wait_ge(sig("qk_stored"), b * 96 + 1)
                for f in range(2):
                    for r in range(2):
                        act.wait_ge(sig("qk_done"), b * 4 + 2 * f + r + 1)
                        act_fn(qk_hi[:, r, HALF * f:HALF * (f + 1)], bank(2 + 2 * r + f), ACT.Identity, scale=qk_scale[:, r:r + 1]).then_inc(sig("hi_ready"), 1)
                for f in range(2):
                    act.wait_ge(sig("v_done"), b * 2 + f + 1)
                    act_fn(v_all[:, bass.ds(b * NG, NG), 4 * f:4 * f + 4, :].rearrange("p g t c -> p t g c"), bank(6 + f).rearrange("p (t g c) -> p t g c", t=4, g=NG), ACT.Copy).then_inc(sig("v_kept"), 1)

            act.wait_ge(sig("means_done"), 1)
            act.wait_ge(sig("b1_ready"), 1)
            for r in range(2):
                act_fn(qkm[:, r, :], ps[0:B, 2, C * r:C * (r + 1)], ACT.Copy).then_inc(sig("means_ready"), 1)
            act.wait_ge(sig("ka_pe"), 3)
            act_fn(phiT[:, :], ps[0:T * KH, 4, 0:MB], ACT.Silu, bias=ka_bphi1[:, 0:1]).then_inc(sig("ka_phi"), 1)
            act.wait_ge(sig("ka_var"), 1)
            act_fn(pst[:, :], psv[:, :], ACT.Sqrt, bias=eps_col[0:MB, 0:1], scale=1.0 / KI).then_inc(sig("ka_std"), 1)
            act.wait_ge(sig("ka_psi"), 1)
            act_fn(psi[:, :, :], psq[:, :, :], ACT.Gelu).then_inc(sig("ka_gelu"), 1)

            with act.Fori(0, NG // 2) as gp:
                for p in range(2):
                    main(gp * 2 + p, p, "attention", None, None)
            with act.Fori(0, B - 1) as b:
                main(b * NG + NG, 0, "post", 0, b)
                for g in range(1, NG):
                    main(b * NG + (NG + g), g % 2, "ffn", g, b)
            for s in range(STEPS):
                post(B - 1, s)
            with act.Fori(0, NG // 2) as gp:
                for p in range(2):
                    fi = gp * 2 + p + (NI - NG)
                    act.wait_ge(sig("ffn_staged"), gp * 2 + p + 1)
                    for q in range(UNITS):
                        relu(q, TAIL_UP[q % TAIL], fi, b1s[p][:, q // 8, q % 4:q % 4 + 1], (tail_hi, tail_mid), TAIL)

        @block.vector
        def _(dve):
            ch = Chain(dve, sig("dve_steps"))
            tt, tsc, stt = nc.vector.tensor_tensor, nc.vector.tensor_scalar, nc.vector.scalar_tensor_tensor
            red = nc.vector.tensor_reduce

            def take_max(a_i, at, count):
                nt, mh, j = a_i // 8, a_i // 4 % 2, a_i % 4
                dve.wait_ge(sig("max_scores"), count + 1)
                red(mxp[:, nt, mh, j:j + 1], bank(at), X, ALU.max).then_inc(sig("maxed"), 1)

            def split_max(half, done, p, k, staged):
                dve.wait_ge(sig("maxed"), done)
                if k is not None:
                    dve.wait_ge(sig("max_turned"), k)
                dve.wait_ge(sig("beta_staged"), staged)
                m4 = mx[:, :].rearrange("p (j t) -> p j t", j=GH)
                ch.link(tt(m4, mxp[:, 4 * half:4 * half + 4, 0, :].rearrange("p t j -> p j t"),
                           mxp[:, 4 * half:4 * half + 4, 1, :].rearrange("p t j -> p j t"), ALU.max))
                bg = beta_g[p][:, :].unsqueeze(2).broadcast_to([P, GH, 4])
                ch.link(tt(mxb[:, :].rearrange("p (j t) -> p j t", j=GH), m4, bg, ALU.add))
                ch.link(tt(mrow[:, :].rearrange("p (j t) -> p j t", j=GH), bg, mxb[:, :].rearrange("p (j t) -> p j t", j=GH), ALU.subtract))
                ch.link(nc.vector.tensor_copy(mparts[:, 0, :], mrow[:, :]))
                tt(mparts[:, 1, :], mrow[:, :], mparts[:, 0, :].bitcast(F32), ALU.subtract).then_inc(sig("max_parts"), 1)

            def move_max(count, stored):
                dve.wait_ge(sig("max_turned"), count + 1)
                if stored is not None:
                    dve.wait_ge(sig("max_rows"), stored)
                nc.vector.tensor_copy(mrows[:, :], ps[0:32, 7, 0:P]).then_inc(sig("max_moved"), 1)

            def weigh(k, fi, at=6):
                u, th = k // 2, k % 2
                dve.wait_ge(sig("w2_done"), fi * UNITS + 4 * k + 6)
                dve.wait_ge(sig(f"route_loaded{u}"), fi * 16 + 16)
                dve.wait_ge(sig("moe_added"), fi * 4 + k + 1)
                tt(weighted[:, k % 2, :], bank(at), route_bc[u][:, HALF * th:HALF * (th + 1)], ALU.mult).then_inc(sig("moe_taken"), 1)

            def main(it, p, kind, g, b):
                def o_move(half):
                    dve.wait_ge(sig("pv_done"), it * 16 + 8 * half + 10)
                    dve.wait_ge(sig(f"o_stored{half}"), it * 64 + 1)
                    nc.vector.tensor_copy(oT[:, half, :], bank(4)).then_inc(sig("o_moved"), 1)

                for s in range(STEPS):
                    take_max((s - LAG) % STEPS, a_bank(s, kind), it * STEPS + AHEAD + s)
                    if s == LAG - 1:
                        split_max(1, it * STEPS + AHEAD + s + 1, p, it * 2 + 1, it + 1)
                    if s == LAG + 31:
                        split_max(0, it * STEPS + AHEAD + s + 1, 1 - p, it * 2 + 2, it + 2)
                    if s == 22:
                        move_max(it * 2 + 1, it * 64 + 32)
                    if s == 54:
                        move_max(it * 2 + 2, it * 64 + 64)
                    if s == 37:
                        o_move(0)
                    if kind == "ffn":
                        u = ffn_unit(g, s, 2)
                        if u and u % 4 == 0:
                            k = u // 4 - 1
                            weigh(k % 4, b * NG + k // 4)
                    if kind == "post":
                        post(b, s)
                if kind == "ffn" and g == NG - 1:
                    weigh(3, b * NG + NG - 1)
                o_move(1)

            def post(b, s):
                def half(name):
                    return s - S[name] if s in (S[name], S[name] + 1) else None

                if s == S["invert"]:
                    dve.wait_ge(sig("sums_loaded"), b * 16 + 16)
                    nc.vector.reciprocal(den[:, 0:P], den[:, 0:P]).then_inc(sig("sums_inverted"), 1)
                f = half("heads")
                if f is not None:
                    if f == 0:
                        dve.wait_ge(sig("o_loaded"), b * 32 + 32)
                        dve.wait_ge(sig("fac_loaded"), 16 * B)
                    cols = slice(HALF * f, HALF * (f + 1))
                    stt(oc[:, cols], oc[:, cols], vfac[:, bass.ds(b, 1)], den[:, cols], ALU.mult, ALU.mult).then_inc(sig("o_normed"), 1)
                f = half("residual")
                if f is not None:
                    dve.wait_ge(sig("xg_ready"), b + 1)
                    dve.wait_ge(sig("proj_done"), b * 2 + f + 1)
                    ch.did(tt(x1[:, 4 * f:4 * f + 4, :], tiles(5 + f), xg[:, 4 * f:4 * f + 4, :], ALU.add))
                f = half("moments")
                if f is not None:
                    ch.wait()
                    for t in range(4 * f, 4 * f + 4):
                        ch.did(nc.vector.bn_stats(st2[:, t, :], x1[:, t, :]))
                if s == S["variances"]:
                    ch.wait()
                    nc.vector.memset(credit[:, len(CREDIT):], 0.0)
                    for t in range(NT):
                        nc.vector.bn_aggr(mv2[:, t, :], st2[:, t, :]).then_inc(sig("var2"), 1)
                f = half("norm")
                if f is not None:
                    if f == 0:
                        dve.wait_ge(sig("var2"), b * NT + NT)
                        dve.wait_ge(sig("std2"), b + 1)
                        ch.link(nc.vector.reciprocal(sd2[:, :], sd2[:, :]))
                    for t in range(4 * f, 4 * f + 4):
                        tsc(xn[:, t, :], x1[:, t, :], mv2[:, t, 0:1], sd2[:, t:t + 1], ALU.subtract, ALU.mult).then_inc(sig("h2_normed"), 1)
                f = half("t_low")
                if f is not None:
                    cols = slice(HALF * f, HALF * (f + 1))
                    dve.wait_ge(sig("t_hi_ready"), b * 2 + f + 1)
                    tt(t_lo[:, cols], t_raw[:, cols], t_hi[:, cols].bitcast(F32), ALU.subtract).then_inc(sig("t_split"), 1)
                if s == S["shift"]:
                    dve.wait_ge(sig("logits"), b + 1)
                    ch.link(tt(lg[:, :, :], ps[:, 5, 0:NT * E].rearrange("p (t e) -> p t e", e=E), over_tiles(bgate_bc), ALU.add))
                    ch.link(red(gm[:, :], lg[:, :, :], X, ALU.max))
                    tt(lg[:, :, :], lg[:, :, :], over_experts(gm), ALU.subtract).then_inc(sig("logits_shifted"), 1)
                if s == S["probs"]:
                    dve.wait_ge(sig("logit_exps"), b + 1)
                    ch.link(red(gm[:, :], pr[:, :, :], X, ALU.add))
                    ch.link(nc.vector.reciprocal(gm[:, :], gm[:, :]))
                    ch.link(tt(pr[:, :, :], pr[:, :, :], over_experts(gm), ALU.mult))
                for name, src, pick in (("first", pr, g1), ("second", g0, g2)):
                    if s == S[name]:
                        ch.link(red(gm[:, :], src[:, :, :], X, ALU.max))
                        ch.link(tt(pick[:, :, :], src[:, :, :], over_experts(gm), ALU.is_ge))
                        ch.link(tt(pick[:, :, :], pick[:, :, :], over_tiles(rev), ALU.mult))
                    if s == S[name] + 1:
                        ch.link(red(gm[:, :], pick[:, :, :], X, ALU.max))
                        ch.link(tt(pick[:, :, :], pick[:, :, :], over_experts(gm), ALU.is_equal))
                        if pick is g1:
                            ch.link(stt(g0[:, :, :], g1[:, :, :], -2.0, pr[:, :, :], ALU.mult, ALU.add))
                if s == S["weights"]:
                    ch.link(tt(g1[:, :, :], g1[:, :, :], g2[:, :, :], ALU.add))
                    ch.link(tt(pr[:, :, :], pr[:, :, :], g1[:, :, :], ALU.mult))
                if s == S["weights"] + 1:
                    ch.link(red(gm[:, :], pr[:, :, :], X, ALU.add))
                    ch.link(nc.vector.reciprocal(gm[:, :], gm[:, :]))
                    tt(route[:, :, :], pr[:, :, :], over_experts(gm), ALU.mult).then_inc(sig("routed"), 1)

            POST = 2 + NT + 1 + 2 + 3 + 11 + 4

            def finish(b):
                dve.wait_ge(sig("stored"), b * 16 + 1)
                dve.wait_ge(sig("x1b_ready"), b + 1)
                for f in range(2):
                    dve.wait_ge(sig("wout_done"), b * 2 + f + 2)
                    tt(y[:, 4 * f:4 * f + 4, :], tiles(5 + f), x1[:, 4 * f:4 * f + 4, :], ALU.add).then_inc(sig("y_ready"), 1)

            nc.vector.memset(eps_col[:, :], EPS).then_inc(sig("eps_set"), 1)
            for i in range(E):
                nc.vector.memset(rev[:, i:i + 1], float(E - i)).then_inc(sig("rev_set"), 1)
            dve.wait_ge(sig("rev_set"), E)
            ch.did(nc.vector.memset(qk_scale[:, 1:2], 1.0))
            nc.vector.memset(accT[:, :], 0.0).then_inc(sig("row_values"), 1)
            nc.vector.memset(y[:, :, :], 1.0).then_inc(sig("row_values"), 1)
            for i, (name, n) in enumerate(CREDIT.items()):
                nc.vector.memset(credit[:, i:i + 1], 0.0).then_inc(sig(name), n)
            dve.wait_ge(sig("silu_ready"), 1)
            for b in range(B):
                m = nc.vector.tensor_copy(silu_bc[:, b, :], siluT[:, b:b + 1].broadcast_to([P, P]))
            m.then_inc(sig("silu_ready"), 1)
            for t in range(B * NT):
                if t % NT == 0:
                    dve.wait_ge(sig(f"x_loaded{t // NT}"), 16)
                ch.did(nc.vector.bn_stats(stats[:, t, :], x_all[:, t, :]))
            ch.wait()
            for t in range(B * NT):
                nc.vector.bn_aggr(mv[:, t, :], stats[:, t, :]).then_inc(sig("var1"), 1)
            dve.wait_ge(sig("mod_done"), 1)
            ch.did(nc.vector.tensor_copy(mod_col[:, 0, :], ps[:, 1, 0:B]))
            ch.did(tsc(mod_col[:, 1, :], ps[:, 1, B:2 * B], 1.0, None, ALU.add))
            ch.did(nc.vector.tensor_copy(mod_col[:, 2, :], ps[:, 1, 2 * B:3 * B]))
            ch.did(tsc(mod_col[:, 3, :], ps[:, 1, 3 * B:4 * B], 1.0, None, ALU.add))
            ch.link(nc.vector.tensor_copy(gate_bc[:, :, :], ps[:, 2:4, :]))
            nc.vector.memset(credit[:, len(CREDIT):], 0.0).then_inc(sig("gates_kept"), 1)
            dve.wait_ge(sig("qkv_loaded"), 32)
            ch.link(tsc(qk_scale[:, 0:1], alpha_col[:, :], ATTN_SCALE, None, ALU.mult))
            dve.wait_ge(sig("std1"), 1)
            dve.wait_ge(sig("var1"), B * NT)
            ch.link(nc.vector.reciprocal(rstd[:, :], std[:, :]))
            nc.vector.memset(credit[:, len(CREDIT):], 0.0).then_inc(sig("gates_kept"), 1)

            def fold_gates():
                ch.link(tsc(gt0[:, :, :], gate_bc[:, :, :], 0.0, 2.0, ALU.is_ge, ALU.mult))
                ch.link(stt(gt1[:, :, :], gate_bc[:, :, :], -1.0, gate_bc[:, :, :], ALU.mult, ALU.max))
                ch.link(tsc(gt1[:, :, :], gt1[:, :, :], 0.25, None, ALU.max))
                ch.link(stt(gate_bc[:, :, :], gt0[:, :, :], -1.0, gt1[:, :, :], ALU.add, ALU.mult))
                dve.wait_ge(sig("loaded"), 16 * len(loads[4:]))
                for b in range(B):
                    g_a, g_b = gate_bc[:, 0, C * b:C * (b + 1)], gate_bc[:, 1, C * b:C * (b + 1)]
                    ch.did(tt(wproj_g[:, b, :], wproj[:, :], g_a, ALU.mult))
                    ch.did(tt(wout_g[:, b, :], wout[:, :], g_b, ALU.mult))
                    ch.did(tt(bproj_g[:, b, :], bproj_bc[:, :], g_a, ALU.mult))
                    ch.did(tt(bout_g[:, b, :], bout_bc[:, :], g_b, ALU.mult))
                ch.wait()
                nc.vector.memset(credit[:, len(CREDIT):], 0.0).then_inc(sig("folded"), 1)

            def project(b):
                dve.wait_ge(sig("x_turned"), b * 2 + 1)
                for t in range(NT):
                    i = b * NT + t
                    tsc(xn[:, t, :], x_all[:, i, :], mv[:, bass.ds(i, 1), 0], rstd[:, bass.ds(i, 1)], ALU.subtract, ALU.mult).then_inc(sig("x_normed"), 1)
                dve.wait_ge(sig("qk_stored"), b * 96 + 1)
                for f in range(2):
                    for r in range(2):
                        dve.wait_ge(sig("hi_ready"), b * 4 + 2 * f + r + 1)
                        stt(qk_lo[:, r, HALF * f:HALF * (f + 1)], bank(2 + 2 * r + f), qk_scale[:, r:r + 1],
                            qk_hi[:, r, HALF * f:HALF * (f + 1)].bitcast(F32), ALU.mult, ALU.subtract).then_inc(sig("lo_ready"), 1)

            project(0)
            fold_gates()
            with dve.Fori(1, B) as b:
                project(b)

            dve.wait_ge(sig("h_ready"), 2 * B)
            hs = hsum[:, :].rearrange("p (b f) -> p b f", f=2)
            ch.link(red(hmean[:, :], hs, X, ALU.add))
            tsc(hmean[:, :], hmean[:, :], 1.0 / N, None, ALU.mult).then_inc(sig("hmean_ready"), 1)
            dve.wait_ge(sig("b1_turned"), 1)
            nc.vector.tensor_copy(b1T[:, :], ps[:, 4, 0:E * CH]).then_inc(sig("b1_ready"), 1)

            grp = lambda t: t[:, :].rearrange("m (t g) -> m t g", g=KI)
            wide = lambda t: t[:, :].unsqueeze(2).broadcast_to([MB, T, KI])

            def ka(a_i):
                if a_i == KA["turn_means"] + 1:
                    dve.wait_ge(sig("ka_pe"), 1)
                    nc.vector.tensor_copy(qkT[:, :], ps[0:KI, 3, 0:MB]).then_inc(sig("ka_sb"), 1)
                if a_i == KA["mix"] + 1:
                    dve.wait_ge(sig("ka_pe"), 2)
                    nc.vector.tensor_copy(axT[:, :], ps[0:T * KI, 2, 0:MB]).then_inc(sig("ka_sb"), 1)
                if a_i == KA["psi_phi"] + 1:
                    dve.wait_ge(sig("ka_pe"), 4)
                    ch.link(tt(psi[:, :, :], ps[0:MB, 6, 0:T * KI].rearrange("m (t g) -> m t g", g=KI), grp(bpsi1_bc), ALU.add))
                    ch.link(red(psm[:, :], psi[:, :, :], X, ALU.add))
                    ch.link(tsc(psm[:, :], psm[:, :], 1.0 / KI, None, ALU.mult))
                if a_i == KA["psi_phi"] + 2:
                    ch.link(tt(psi[:, :, :], psi[:, :, :], wide(psm), ALU.subtract))
                    ch.link(tt(psq[:, :, :], psi[:, :, :], psi[:, :, :], ALU.mult))
                    red(psv[:, :], psq[:, :, :], X, ALU.add).then_inc(sig("ka_var"), 1)
                if a_i == KA["psi_norm"]:
                    dve.wait_ge(sig("ka_std"), 1)
                    ch.link(nc.vector.reciprocal(pst[:, :], pst[:, :]))
                    ch.link(tt(psq[:, :, :], psi[:, :, :], wide(pst), ALU.mult))
                    ch.link(tt(psq[:, :, :], psq[:, :, :], grp(lng_bc), ALU.mult))
                    tt(psq[:, :, :], psq[:, :, :], grp(lnb_bc), ALU.add).then_inc(sig("ka_psi"), 1)
                if a_i == KA["turn_psi"]:
                    dve.wait_ge(sig("ka_pe"), 5)
                    ch.link(tt(phi[:, :], ps[0:MB, 2, 0:HD], bphi2_bc[:, :], ALU.add))
                if a_i == KA["turn_psi"] + 1:
                    dve.wait_ge(sig("ka_pe"), 6)
                    nc.vector.tensor_copy(psiT[:, :], ps[0:T * KI, 3, 0:MB]).then_inc(sig("ka_sb"), 1)
                if a_i == KA["out"] + 1:
                    dve.wait_ge(sig("ka_pe"), 7)
                    ch.link(tt(psi_o[:, :], ps[0:MB, 4, 0:HD], bpsi2_bc[:, :], ALU.add))
                    ch.link(tt(phi[:, :], phi[:, :], psi_o[:, :], ALU.mult))
                    ch.link(tsc(phi[:, :], phi[:, :], temp_bc[:, 0:1], None, ALU.mult))
                    ch.link(tt(fac[:, :].rearrange("m (t o) -> m t o", o=KO), phi[:, :].rearrange("m (t o) -> m t o", o=KO), mix_bc[:, :].unsqueeze(2).broadcast_to([MB, T, KO]), ALU.mult))
                    tsc(fac[:, :], fac[:, :], 1.0, gamma_col[:, 0:1], ALU.add, ALU.mult).then_inc(sig("fac_ready"), 1)

            for a_i in range(AHEAD):
                take_max(a_i, a_bank(a_i + LAG, "attention"), a_i)
                if a_i == 31:
                    split_max(0, a_i + 1, 0, None, 1)
                ka(a_i)
                if a_i == FIRST_TURN + 2:
                    move_max(0, None)

            PER = 2 * 4
            with dve.Fori(0, NG // 2) as gp:
                ch.enter(gp, 2 * PER)
                for p in range(2):
                    main(gp * 2 + p, p, "attention", None, None)
                ch.leave(NG // 2)
            with dve.Fori(0, B - 1) as b:
                ch.enter(b, NG * PER + POST)
                main(b * NG + NG, 0, "post", 0, b)
                for g in range(1, NG):
                    main(b * NG + (NG + g), g % 2, "ffn", g, b)
                finish(b)
                ch.leave(B - 1)
            for s in range(STEPS):
                post(B - 1, s)
            with dve.Fori(0, NG // 2) as gp:
                ch.enter(gp, 4 * PIECES)
                for u in range(2 * UNITS):
                    q, fi = u % UNITS, gp * 2 + (NI - NG + u // UNITS)
                    if u % 4 == 3 and u > 3:
                        k = u // 4 - 1
                        weigh(k % 4, gp * 2 + (NI - NG + k // 4), TAIL_DOWN[k % 2])
                    dve.wait_ge(sig("relus"), fi * UNITS + q + 2)
                    tt(tail_lo[:, u % TAIL, :], tail_mid[:, u % TAIL, :], tail_hi[:, u % TAIL, :].bitcast(F32), ALU.subtract).then_inc(sig("mid_split"), 1)
                    for x, first in ((1, TAIL - 1), (0, UNITS // 2 + TAIL - 1)):
                        if q == first:
                            dve.wait_ge(sig(f"w_loaded{x}"), fi * 32 + 64 - 32 * x)
                            dve.wait_ge(sig("w2_done"), fi * UNITS + (1 - x) * UNITS // 2 + 2)
                        if q in (first, first + 1):
                            for piece in range(PIECES // 2):
                                split_piece(nc.vector, ch, x, (q - first) * (PIECES // 2) + piece)
                weigh(3, gp * 2 + (NI - NG + 1), TAIL_DOWN[1])
                ch.leave(NG // 2)
            finish(B - 1)

        @block.gpsimd
        def _(pool):
            ch = Chain(pool, sig("pool_steps"))

            def stage(group, p):
                for j in range(GH):
                    m = nc.gpsimd.tensor_copy(V[p][:, :, j, 0:HD], v_all[:, group, :, HD * j:HD * (j + 1)])
                m.then_inc(sig("v_staged"), 1)
                nc.gpsimd.tensor_copy(beta_g[p][:, :], beta_bc[:, bass.ds(group * GH, GH)]).then_inc(sig("beta_staged"), 1)

            def stage_biases(p, g):
                nc.gpsimd.tensor_copy(b1s[p][:, :, :].rearrange("p u c -> p (u c)"), b1T[:, bass.ds(g * 2 * CH, 2 * CH)]).then_inc(sig("ffn_staged"), 1)

            sub = nc.gpsimd.tensor_tensor

            def split_weights(u, piece, loaded, free):
                if piece == 0:
                    pool.wait_ge(sig(f"w_loaded{u}"), loaded)
                    if free is not None:
                        pool.wait_ge(sig("w2_done"), free)
                        sub(pool_wait[:, :], ident[:, 0:1], ident[:, 0:1], ALU.mult)
                split_piece(nc.gpsimd, ch, u, piece)

            def add_weighted(k, fi, batches):
                pool.wait_ge(sig("moe_taken"), fi * 4 + k + 2)
                if k == 0:
                    pool.wait_ge(sig("moe_started"), batches * 2)
                th = slice(HALF * (k % 2), HALF * (k % 2 + 1))
                pool.wait_ge(sig("moe_added"), fi * 4 + k + CREDIT["moe_added"])
                sub(accT[:, th], accT[:, th], weighted[:, k % 2, :], ALU.add).then_inc(sig("moe_added"), 1)

            def main(it, p, kind, g, b):
                pool.wait_ge(sig("pv_done"), it * 16 + 2)
                pool.wait_ge(sig("maxed"), it * STEPS + AHEAD)
                stage((it + 1) % NI, 1 - p)
                if kind == "post":
                    residual2(b)
                    residual(b + 1)
                for s in range(STEPS):
                    u = ffn_unit(g, s) if kind == "ffn" else None
                    if u is not None:
                        fi = b * NG + u // UNITS
                        pool.wait_ge(sig("relus"), fi * UNITS + u % UNITS + 2)
                        sub(mid_lo[:, u % 2, :], mid[:, u % 2, :], mid_hi[:, u % 2, :].bitcast(F32), ALU.subtract).then_inc(sig("mid_split"), 1)
                        e, piece = u // 8 + 1, u % 8 - 1
                        if 0 <= piece < PIECES:
                            split_weights(e % 2, piece, b * (NG * 32) + (e // 2 + 1) * 32, b * ALL_UNITS + 8 * (e - 1) + 2)
                        if u % 4 == 1 and u > 1:
                            k = u // 4 - 1
                            add_weighted(k % 4, b * NG + k // 4, b + 1)
                if kind == "ffn" and g == NG - 1:
                    add_weighted(3, b * NG + NG - 1, b + 1)

            def residual(b):
                pool.wait_ge(sig("xg_loaded"), b * 16 + 16)
                for t in range(NT):
                    m = nc.gpsimd.tensor_tensor(xg[:, t, :], xg[:, t, :], bproj_g[:, b, :], ALU.add)
                m.then_inc(sig("xg_ready"), 1)

            def residual2(b):
                pool.wait_ge(sig("h2_normed"), b * NT + NT)
                for t in range(NT):
                    m = nc.gpsimd.tensor_tensor(x1[:, t, :], x1[:, t, :], bout_g[:, b, :], ALU.add)
                m.then_inc(sig("x1b_ready"), 1)

            nc.gpsimd.memset(ident[:, :], 0.0).then_inc(sig("ident"), 1)
            for w in (ka_phi2, ka_psi1, ka_psi2):
                nc.gpsimd.memset(w[:, :], 0.0).then_inc(sig("blocks_zero"), 1)
            pool.wait_ge(sig("ident"), 1)
            nc.gpsimd.affine_select(out=ident[:, :], in_=ident[:, :], compare_op=ALU.not_equal, fill=1.0,
                                    base=0, pattern=[[-1, P]], channel_multiplier=1).then_inc(sig("ident"), 1)
            for i in range(2):
                nc.gpsimd.memset(K[i][:, :, :].bitcast(F32), 0.0).then_inc(sig("qk_zero"), 1)
                nc.gpsimd.memset(Q[i][:, :].bitcast(F32), 0.0).then_inc(sig("qk_zero"), 1)
                nc.gpsimd.memset(V[i][:, :, :, :], 1.0).then_inc(sig("v_ones"), 1)
            pool.wait_ge(sig("v_ones"), 2)
            pool.wait_ge(sig("loaded"), 16 * len(loads[4:]))
            pool.wait_ge(sig("b1_ready"), 1)
            pool.wait_ge(sig("v_kept"), 2 + 1)
            stage(0, 0)
            pool.wait_ge(sig("v_kept"), 2 * B + 1)

            pool.wait_ge(sig("qk_stored"), B * 6 * 16 + 1)
            for piece in range(PIECES):
                split_weights(0, piece, 32, None)
            pool.wait_ge(sig("folded"), 1)
            residual(0)
            with pool.Fori(0, NG // 2) as gp:
                for p in range(2):
                    main(gp * 2 + p, p, "attention", None, None)
            with pool.Fori(0, B - 1) as b:
                ch.enter(b, E * PIECES)
                main(b * NG + NG, 0, "post", 0, b)
                for g in range(1, NG):
                    main(b * NG + (NG + g), g % 2, "ffn", g, b)
                ch.leave(B - 1)
            residual2(B - 1)
            stage_biases(0, 0)
            with pool.Fori(0, NG // 2) as gp:
                for p in range(2):
                    fi = gp * 2 + p + (NI - NG)
                    for q in range(UNITS):
                        if q == UNITS - 2:
                            pool.wait_ge(sig("relus"), fi * UNITS + 1)
                            stage_biases(1 - p, (gp * 2 + p + 1) % NG)
                        if q % 4 == 1 and q > 1:
                            add_weighted(q // 4 - 1, fi, B)
                    add_weighted(3, fi, B)


def kernel(**inputs):
    import numpy as _np
    import concourse.bacc as _bacc
    from concourse import mybir as _mybir
    from concourse.bass_utils import run_bass_kernel_spmd as _run

    nc = _bacc.Bacc("TRN2", target_bir_lowering=False, num_devices=1)
    arrays, args = {}, {}
    for name, value in inputs.items():
        v = _np.ascontiguousarray(value).reshape(_np.shape(value) or (1,))
        arrays[f"in_{name}"] = v
        args[name] = nc.dram_tensor(f"in_{name}", v.shape, _mybir.dt.from_np(v.dtype), kind="ExternalInput").ap()
    out = nc.dram_tensor("out_0", (B, N, C), F32, kind="ExternalOutput").ap()
    build(nc, args, out)
    r = _run(nc, [arrays], core_ids=[0])
    return r.results[0]["out_0"]
```
